# Optimizing a Trainium2 kernel written in Bass

```python
import numpy as np
import jax
import jax.numpy as jnp

def _softmax(x, axis=-1):
    return jax.nn.softmax(x, axis=axis)

def _gelu(x):
    return jax.nn.gelu(x, approximate=True)

def _silu(x):
    return jax.nn.silu(x)

def _sigmoid(x):
    return jax.nn.sigmoid(x)

def _layernorm(x, axis=-1, eps=1e-05):
    m = jnp.mean(x, axis=axis, keepdims=True)
    v = jnp.var(x, axis=axis, keepdims=True)
    return (x - m) / jnp.sqrt(v + eps)

def _scatter_add(tgt, idx, src, axis=0):
    return tgt.at[idx].add(src)

def _segment_sum(src, seg, n):
    return jax.ops.segment_sum(src, seg, n)
kernel_name = 'mk_adaln_ffn_d2_seqx_r4_790d44'

def setup_inputs(seed: int=0):
    np.random.seed(seed)
    _w = jnp.asarray

    def _rec_inputs():
        import jax
        import jax.numpy as jnp
        _rk = jax.random.key(seed)
        x = -0.000125 + 0.9999 * jax.random.normal(jax.random.fold_in(_rk, 1), (4, 512, 512), jnp.float32)
        _lenS = 512 - jax.random.randint(jax.random.fold_in(_rk, 7), (4,), 0, max(1, 512 // 4) + 1, jnp.int32)
        _lenS2 = 512 - jax.random.randint(jax.random.fold_in(_rk, 8), (4,), 0, max(1, 512 // 4) + 1, jnp.int32)
        fside_BxSxS_0 = -1.52775e-05 + 0.999936 * jax.random.normal(jax.random.fold_in(_rk, 11), (4, 512, 512), jnp.float32)
        cond_512 = -5.03954e-05 + 1.00559 * jax.random.normal(jax.random.fold_in(_rk, 12), (4, 128), jnp.float32)
        return (x, fside_BxSxS_0, cond_512)
    x, fside_BxSxS_0, cond_512 = _rec_inputs()

    def _L0_cond_setup():
        import jax, jax.numpy as jnp
        from jax import lax
        import numpy as np
        B, T, C, TD = (8, 512, 512, 128)

        def _bi_wkv(r, k, v, w, u, time_emb):
            tf = jax.nn.sigmoid(jnp.sum(time_emb, axis=-1))[:, None, None]
            decay = jnp.exp(-jnp.exp(w.astype(jnp.float32)))[None, :] * (0.5 + 0.5 * tf[:, :, 0])
            kf = k.astype(jnp.float32)
            vf = v.astype(jnp.float32)
            ek = jnp.exp(jnp.minimum(kf, 30.0))
            ekv = ek * vf

            def step(carry, x):
                a, b = carry
                ekv_t, ek_t = x
                a = a * decay + ekv_t
                b = b * decay + ek_t
                return ((a, b), (a, b))
            ekv_t = jnp.swapaxes(ekv, 0, 1)
            ek_t = jnp.swapaxes(ek, 0, 1)
            init = (jnp.zeros_like(decay), jnp.zeros_like(decay))
            _, (nf, df) = lax.scan(step, init, (ekv_t, ek_t))
            _, (nb, db) = lax.scan(step, init, (ekv_t, ek_t), reverse=True)
            nf = jnp.swapaxes(nf, 0, 1)
            df = jnp.swapaxes(df, 0, 1)
            nb = jnp.swapaxes(nb, 0, 1)
            db = jnp.swapaxes(db, 0, 1)
            euk = jnp.exp(jnp.minimum(u.astype(jnp.float32)[None, None, :] + kf, 30.0))
            num = nf + nb - ekv + euk * vf
            den = df + db - ek + euk
            base = jax.nn.sigmoid(r.astype(jnp.float32)) * (num / jnp.maximum(den, 1e-08))
            out = base * (0.8 + 0.2 * tf)
            return out.astype(r.dtype)
        key = jax.random.key(seed)
        ks = jax.random.split(key, 6)
        return {'r': jax.random.normal(ks[0], (B, T, C), dtype=jnp.float32), 'k': jax.random.normal(ks[1], (B, T, C), dtype=jnp.float32), 'v': jax.random.normal(ks[2], (B, T, C), dtype=jnp.float32), 'w': jax.random.normal(ks[3], (C,), dtype=jnp.float32), 'u': jax.random.normal(ks[4], (C,), dtype=jnp.float32), 'time_emb': jax.random.normal(ks[5], (B, TD), dtype=jnp.float32)}
    _L0_cond_all = _L0_cond_setup()
    _L0_cond_in = {k: v for k, v in _L0_cond_all.items() if k in ('w', 'u')}
    del _L0_cond_all

    def _L0_ffn_setup():
        import jax, jax.numpy as jnp
        import numpy as np
        TOP_K = 2
        EPS = 1e-06
        key = jax.random.key(seed)
        ks = jax.random.split(key, 4)
        B, L, D, E, ED = (2, 512, 512, 8, 512)
        scale_gu = (6.0 / D) ** 0.5
        scale_dn = (6.0 / ED) ** 0.5
        return {'x': jax.random.normal(ks[0], (B, L, D), jnp.float32), 'router_scale': jnp.ones((D,), jnp.float32), 'gate_w': jax.random.normal(ks[1], (D, E), jnp.float32) * D ** (-0.5), 'gate_up': jax.random.uniform(ks[2], (E, D, 2 * ED), jnp.float32, -scale_gu, scale_gu), 'down': jax.random.uniform(ks[3], (E, ED, D), jnp.float32, -scale_dn, scale_dn), 'per_expert_scale': jnp.ones((E,), jnp.float32)}
    _L0_ffn_all = _L0_ffn_setup()
    _L0_ffn_in = {k: v for k, v in _L0_ffn_all.items() if k in ('router_scale', 'gate_w', 'gate_up', 'down', 'per_expert_scale')}
    del _L0_ffn_all

    def _L1_cond_setup():
        import jax, jax.numpy as jnp
        from jax import lax
        import numpy as np
        B, T, C, TD = (8, 512, 512, 128)

        def _bi_wkv(r, k, v, w, u, time_emb):
            tf = jax.nn.sigmoid(jnp.sum(time_emb, axis=-1))[:, None, None]
            decay = jnp.exp(-jnp.exp(w.astype(jnp.float32)))[None, :] * (0.5 + 0.5 * tf[:, :, 0])
            kf = k.astype(jnp.float32)
            vf = v.astype(jnp.float32)
            ek = jnp.exp(jnp.minimum(kf, 30.0))
            ekv = ek * vf

            def step(carry, x):
                a, b = carry
                ekv_t, ek_t = x
                a = a * decay + ekv_t
                b = b * decay + ek_t
                return ((a, b), (a, b))
            ekv_t = jnp.swapaxes(ekv, 0, 1)
            ek_t = jnp.swapaxes(ek, 0, 1)
            init = (jnp.zeros_like(decay), jnp.zeros_like(decay))
            _, (nf, df) = lax.scan(step, init, (ekv_t, ek_t))
            _, (nb, db) = lax.scan(step, init, (ekv_t, ek_t), reverse=True)
            nf = jnp.swapaxes(nf, 0, 1)
            df = jnp.swapaxes(df, 0, 1)
            nb = jnp.swapaxes(nb, 0, 1)
            db = jnp.swapaxes(db, 0, 1)
            euk = jnp.exp(jnp.minimum(u.astype(jnp.float32)[None, None, :] + kf, 30.0))
            num = nf + nb - ekv + euk * vf
            den = df + db - ek + euk
            base = jax.nn.sigmoid(r.astype(jnp.float32)) * (num / jnp.maximum(den, 1e-08))
            out = base * (0.8 + 0.2 * tf)
            return out.astype(r.dtype)
        key = jax.random.key(seed)
        ks = jax.random.split(key, 6)
        return {'r': jax.random.normal(ks[0], (B, T, C), dtype=jnp.float32), 'k': jax.random.normal(ks[1], (B, T, C), dtype=jnp.float32), 'v': jax.random.normal(ks[2], (B, T, C), dtype=jnp.float32), 'w': jax.random.normal(ks[3], (C,), dtype=jnp.float32), 'u': jax.random.normal(ks[4], (C,), dtype=jnp.float32), 'time_emb': jax.random.normal(ks[5], (B, TD), dtype=jnp.float32)}
    _L1_cond_all = _L1_cond_setup()
    _L1_cond_in = {k: v for k, v in _L1_cond_all.items() if k in ('w', 'u')}
    del _L1_cond_all

    def _L1_ffn_setup():
        import jax, jax.numpy as jnp
        import numpy as np
        import math
        D_MODEL = 512
        D_FF = 2048
        NUM_EXPERTS = 8
        TOP_K = 2
        CAPACITY_FACTOR = 1.25
        BATCH, SEQ = (4, 512)

        def _moe_forward(x, Wg, w1, w2):
            B, T, d = x.shape
            S = B * T
            E, K = (NUM_EXPERTS, TOP_K)
            C = math.ceil(CAPACITY_FACTOR * S * K / E)
            xr = x.reshape(S, d)
            probs = jax.nn.softmax(xr @ Wg, axis=-1)
            gate_vals, expert_idx = jax.lax.top_k(probs, K)
            flat_e = expert_idx.reshape(-1)
            oh = jax.nn.one_hot(flat_e, E, dtype=jnp.int32)
            pos = jnp.sum((jnp.cumsum(oh, axis=0) - 1) * oh, axis=1)
            kept = pos < C
            i = jnp.arange(S * K)
            slot = i % K * S + i // K
            sentinel = S * K
            pos_w = jnp.where(kept, pos, C)
            dispatch_mask = jnp.full((E, C), sentinel, dtype=jnp.int32)
            dispatch_mask = dispatch_mask.at[flat_e, pos_w].set(slot.astype(jnp.int32), mode='drop')
            combine_weights = (gate_vals * kept.reshape(S, K)).T
            dispatched = xr[dispatch_mask.reshape(-1) % S].reshape(E, C, d)
            h = jax.nn.relu(jnp.einsum('ecd,edf->ecf', dispatched, w1))
            expert_out = jnp.einsum('ecf,efd->ecd', h, w2)
            rerouted = jnp.zeros((S * K + 1, d), dtype=expert_out.dtype)
            rerouted = rerouted.at[dispatch_mask.reshape(-1)].set(expert_out.reshape(-1, d))
            rerouted = rerouted[:-1].reshape(K, S, d)
            out = jnp.einsum('ks,ksm->sm', combine_weights, rerouted)
            return out.reshape(B, T, d)
        key = jax.random.key(seed)
        k1, k2, k3, k4 = jax.random.split(key, 4)
        x = jax.random.normal(k1, (BATCH, SEQ, D_MODEL), dtype=jnp.float32)
        Wg = jax.random.normal(k2, (D_MODEL, NUM_EXPERTS), dtype=jnp.float32) * 0.02
        w1 = jax.random.normal(k3, (NUM_EXPERTS, D_MODEL, D_FF), dtype=jnp.float32) * 0.02
        w2 = jax.random.normal(k4, (NUM_EXPERTS, D_FF, D_MODEL), dtype=jnp.float32) * 0.02
        return {'x': x, 'Wg': Wg, 'w1': w1, 'w2': w2}
    _L1_ffn_all = _L1_ffn_setup()
    _L1_ffn_in = {k: v for k, v in _L1_ffn_all.items() if k in ('Wg', 'w1', 'w2')}
    del _L1_ffn_all
    return {'x': x, 'fside_BxSxS_0': fside_BxSxS_0, 'cond_512': cond_512, 'L0_cond_w': _L0_cond_in['w'], 'L0_cond_u': _L0_cond_in['u'], 'L0_ffn_router_scale': _L0_ffn_in['router_scale'], 'L0_ffn_gate_w': _L0_ffn_in['gate_w'], 'L0_ffn_gate_up': _L0_ffn_in['gate_up'], 'L0_ffn_down': _L0_ffn_in['down'], 'L0_ffn_per_expert_scale': _L0_ffn_in['per_expert_scale'], 'L1_cond_w': _L1_cond_in['w'], 'L1_cond_u': _L1_cond_in['u'], 'L1_ffn_Wg': _L1_ffn_in['Wg'], 'L1_ffn_w1': _L1_ffn_in['w1'], 'L1_ffn_w2': _L1_ffn_in['w2']}

def reference(x, fside_BxSxS_0, cond_512, L0_cond_w, L0_cond_u, L0_ffn_router_scale, L0_ffn_gate_w, L0_ffn_gate_up, L0_ffn_down, L0_ffn_per_expert_scale, L1_cond_w, L1_cond_u, L1_ffn_Wg, L1_ffn_w1, L1_ffn_w2):
    import jax
    import jax.numpy as jnp

    def _L0_cond_ref(r, k, v, w, u, time_emb):
        import jax, jax.numpy as jnp
        from jax import lax
        import numpy as np
        B, T, C, TD = (8, 512, 512, 128)

        def _bi_wkv(r, k, v, w, u, time_emb):
            tf = jax.nn.sigmoid(jnp.sum(time_emb, axis=-1))[:, None, None]
            decay = jnp.exp(-jnp.exp(w.astype(jnp.float32)))[None, :] * (0.5 + 0.5 * tf[:, :, 0])
            kf = k.astype(jnp.float32)
            vf = v.astype(jnp.float32)
            ek = jnp.exp(jnp.minimum(kf, 30.0))
            ekv = ek * vf

            def step(carry, x):
                a, b = carry
                ekv_t, ek_t = x
                a = a * decay + ekv_t
                b = b * decay + ek_t
                return ((a, b), (a, b))
            ekv_t = jnp.swapaxes(ekv, 0, 1)
            ek_t = jnp.swapaxes(ek, 0, 1)
            init = (jnp.zeros_like(decay), jnp.zeros_like(decay))
            _, (nf, df) = lax.scan(step, init, (ekv_t, ek_t))
            _, (nb, db) = lax.scan(step, init, (ekv_t, ek_t), reverse=True)
            nf = jnp.swapaxes(nf, 0, 1)
            df = jnp.swapaxes(df, 0, 1)
            nb = jnp.swapaxes(nb, 0, 1)
            db = jnp.swapaxes(db, 0, 1)
            euk = jnp.exp(jnp.minimum(u.astype(jnp.float32)[None, None, :] + kf, 30.0))
            num = nf + nb - ekv + euk * vf
            den = df + db - ek + euk
            base = jax.nn.sigmoid(r.astype(jnp.float32)) * (num / jnp.maximum(den, 1e-08))
            out = base * (0.8 + 0.2 * tf)
            return out.astype(r.dtype)
        return _bi_wkv(r, k, v, w, u, time_emb)

    def _L0_ffn_ref(x, router_scale, gate_w, gate_up, down, per_expert_scale):
        import jax, jax.numpy as jnp
        import numpy as np
        TOP_K = 2
        EPS = 1e-06
        B, L, D = x.shape
        E = gate_up.shape[0]
        h = x * jax.lax.rsqrt(jnp.mean(x * x, axis=-1, keepdims=True) + EPS)
        h = h * D ** (-0.5) * router_scale
        logits = (h @ gate_w).astype(jnp.float32)
        probs = jax.nn.softmax(logits, axis=-1)
        w, idx = jax.lax.top_k(probs, TOP_K)
        w = w / jnp.clip(jnp.sum(w, axis=-1, keepdims=True), 1e-12)
        w = w.astype(x.dtype)
        N = B * L
        xf = x.reshape(N, D)
        idxf = idx.reshape(N, TOP_K)
        wf = w.reshape(N, TOP_K)
        combine = jnp.zeros((N, E), x.dtype).at[jnp.arange(N)[:, None], idxf].add(wf)
        hh = jnp.einsum('nd,edf->nef', xf, gate_up)
        gate, up = jnp.split(hh, 2, axis=-1)
        act = jax.nn.gelu(gate, approximate=False) * up
        y = jnp.einsum('nef,efd->ned', act, down)
        out = jnp.einsum('ne,ned->nd', combine * per_expert_scale, y)
        return out.reshape(B, L, D)

    def _L1_cond_ref(r, k, v, w, u, time_emb):
        import jax, jax.numpy as jnp
        from jax import lax
        import numpy as np
        B, T, C, TD = (8, 512, 512, 128)

        def _bi_wkv(r, k, v, w, u, time_emb):
            tf = jax.nn.sigmoid(jnp.sum(time_emb, axis=-1))[:, None, None]
            decay = jnp.exp(-jnp.exp(w.astype(jnp.float32)))[None, :] * (0.5 + 0.5 * tf[:, :, 0])
            kf = k.astype(jnp.float32)
            vf = v.astype(jnp.float32)
            ek = jnp.exp(jnp.minimum(kf, 30.0))
            ekv = ek * vf

            def step(carry, x):
                a, b = carry
                ekv_t, ek_t = x
                a = a * decay + ekv_t
                b = b * decay + ek_t
                return ((a, b), (a, b))
            ekv_t = jnp.swapaxes(ekv, 0, 1)
            ek_t = jnp.swapaxes(ek, 0, 1)
            init = (jnp.zeros_like(decay), jnp.zeros_like(decay))
            _, (nf, df) = lax.scan(step, init, (ekv_t, ek_t))
            _, (nb, db) = lax.scan(step, init, (ekv_t, ek_t), reverse=True)
            nf = jnp.swapaxes(nf, 0, 1)
            df = jnp.swapaxes(df, 0, 1)
            nb = jnp.swapaxes(nb, 0, 1)
            db = jnp.swapaxes(db, 0, 1)
            euk = jnp.exp(jnp.minimum(u.astype(jnp.float32)[None, None, :] + kf, 30.0))
            num = nf + nb - ekv + euk * vf
            den = df + db - ek + euk
            base = jax.nn.sigmoid(r.astype(jnp.float32)) * (num / jnp.maximum(den, 1e-08))
            out = base * (0.8 + 0.2 * tf)
            return out.astype(r.dtype)
        return _bi_wkv(r, k, v, w, u, time_emb)

    def _L1_ffn_ref(x, Wg, w1, w2):
        import jax, jax.numpy as jnp
        import numpy as np
        import math
        D_MODEL = 512
        D_FF = 2048
        NUM_EXPERTS = 8
        TOP_K = 2
        CAPACITY_FACTOR = 1.25
        BATCH, SEQ = (4, 512)

        def _moe_forward(x, Wg, w1, w2):
            B, T, d = x.shape
            S = B * T
            E, K = (NUM_EXPERTS, TOP_K)
            C = math.ceil(CAPACITY_FACTOR * S * K / E)
            xr = x.reshape(S, d)
            probs = jax.nn.softmax(xr @ Wg, axis=-1)
            gate_vals, expert_idx = jax.lax.top_k(probs, K)
            flat_e = expert_idx.reshape(-1)
            oh = jax.nn.one_hot(flat_e, E, dtype=jnp.int32)
            pos = jnp.sum((jnp.cumsum(oh, axis=0) - 1) * oh, axis=1)
            kept = pos < C
            i = jnp.arange(S * K)
            slot = i % K * S + i // K
            sentinel = S * K
            pos_w = jnp.where(kept, pos, C)
            dispatch_mask = jnp.full((E, C), sentinel, dtype=jnp.int32)
            dispatch_mask = dispatch_mask.at[flat_e, pos_w].set(slot.astype(jnp.int32), mode='drop')
            combine_weights = (gate_vals * kept.reshape(S, K)).T
            dispatched = xr[dispatch_mask.reshape(-1) % S].reshape(E, C, d)
            h = jax.nn.relu(jnp.einsum('ecd,edf->ecf', dispatched, w1))
            expert_out = jnp.einsum('ecf,efd->ecd', h, w2)
            rerouted = jnp.zeros((S * K + 1, d), dtype=expert_out.dtype)
            rerouted = rerouted.at[dispatch_mask.reshape(-1)].set(expert_out.reshape(-1, d))
            rerouted = rerouted[:-1].reshape(K, S, d)
            out = jnp.einsum('ks,ksm->sm', combine_weights, rerouted)
            return out.reshape(B, T, d)
        return _moe_forward(x, Wg, w1, w2)
    x = x + _L0_ffn_ref(_L0_cond_ref(x, fside_BxSxS_0, fside_BxSxS_0, L0_cond_w, L0_cond_u, cond_512), L0_ffn_router_scale, L0_ffn_gate_w, L0_ffn_gate_up, L0_ffn_down, L0_ffn_per_expert_scale)
    x = x + _L1_ffn_ref(_L1_cond_ref(x, fside_BxSxS_0, fside_BxSxS_0, L1_cond_w, L1_cond_u, cond_512), L1_ffn_Wg, L1_ffn_w1, L1_ffn_w2)
    return x

_drawn_inputs = setup_inputs


def setup_inputs(seed=0):
    import zlib

    import numpy as np

    out = dict(_drawn_inputs(seed))
    spreads = {'L0_ffn_router_scale': (1.0, 0.2), 'L0_ffn_per_expert_scale': (1.0, 0.2)}
    factors = {'L1_cond_w': 3.228, 'L1_cond_u': 5.991}
    for name, (base, spread) in spreads.items():
        noise = np.random.default_rng([zlib.crc32(name.encode()), seed]).standard_normal(out[name].shape)
        drawn = base * np.exp(spread * noise) if base else spread * noise
        out[name] = jnp.asarray(drawn.astype(out[name].dtype))
    for name, factor in factors.items():
        out[name] = (out[name] * factor).astype(out[name].dtype)
    return out
```

```python
from contextlib import ExitStack

import numpy as np

import concourse.bass as bass
from concourse import mybir

F32 = mybir.dt.float32
F32R = mybir.dt.float32r
BF16 = mybir.dt.bfloat16
I32 = mybir.dt.int32
U32 = mybir.dt.uint32
ALU = mybir.AluOpType
ACT = mybir.ActivationFunctionType
AX = mybir.AxisListType

P = 128
B, T, D = 4, 512, 512
S = B * T
NT = S // P
KD = D // P
TB = T // P
E = 8
NQ = B * KD
F0 = 512
F1 = 2048
CAP = 640
NG = 40
NTAB = NG + 4
ROWS = E * CAP
PADROWS = ROWS + CAP
HC = 256
NC1 = F1 // HC
HALF = CAP // 2
TXR = 80
NST = CAP // TXR
NGRP = E * F1 // P // 4
E30 = float(np.exp(np.float64(30.0)))
CLIP = 30.0
assert NG * P == ROWS and 2 * S // P + E - 1 <= NG


def static_wait(eng, sem, value):
    if isinstance(value, int) and value <= 0:
        return
    eng.wait_ge(sem, value)


def adaln_moe_kernel(nc, x, fs_t, params, rowpar, gu, dn, wc, out):
    ctx = ExitStack()
    with ctx:
        def sb(name, shape, dt):
            return ctx.enter_context(nc.sbuf_tensor(name, shape, dt))

        def sem(name):
            return ctx.enter_context(nc.semaphore(name))

        disp = nc.dram_tensor("disp", (PADROWS, D), F32, kind="Internal").ap()
        ybuf = [nc.dram_tensor(f"ybuf{l}", (ROWS + P, D), F32, kind="Internal").ap() for l in range(2)]
        ek_d = nc.dram_tensor("ek_d", (NQ, P, T), F32, kind="Internal").ap()
        eu_d = nc.dram_tensor("eu_d", (NQ, P, T), F32, kind="Internal").ap()
        ratio_d = nc.dram_tensor("ratio_d", (NQ, P, TB, P), F32, kind="Internal").ap()

        ident = sb("ident", [P, P], F32)
        tri = sb("tri", [P, P], BF16)
        ones = sb("ones", [P, P], BF16)
        iota_e = sb("iota_e", [P, E], F32)
        iota_m = sb("iota_m", [P, NT], F32)
        iota_t = sb("iota_t", [P, NTAB], F32)
        iota_i = sb("iota_i", [P, NTAB], I32)
        one8 = sb("one8", [P, E], F32)
        par = sb("par", [P, 5 * KD + 2 * KD * E], F32)
        rowp = sb("rowp", [P, B * P + E], F32)
        w_col = [par[:, 0:KD], par[:, 2 * KD:3 * KD]]
        u_col = [par[:, KD:2 * KD], par[:, 3 * KD:4 * KD]]
        rs_col = par[:, 4 * KD:5 * KD]
        gate = [par[:, 5 * KD + l * KD * E:5 * KD + (l + 1) * KD * E].rearrange("p (k e) -> p k e", k=KD)
                for l in range(2)]
        gate0s = sb("gate0s", [P, KD, E], F32)
        tsum = sb("tsum", [P, B], F32)
        tf = sb("tf", [P, B], F32)
        half = sb("half", [P, B], F32)
        gsc = sb("gsc", [P, B], F32)
        ew = sb("ew", [P, 2, KD], F32)
        dcy = sb("dcy", [P, 2, KD], F32)
        dec = sb("dec", [P, 2, B, KD], F32)
        ssq = sb("ssq", [P, NT], F32)
        rms = sb("rms", [P, NT], F32)
        rstd = sb("rstd", [P, NT], F32)
        lgs = sb("lgs", [P, NT, E], F32)
        mx = sb("mx", [P, NT], F32)
        ex = sb("ex", [P, NT, E], F32)
        sm = sb("sm", [P, NT], F32)
        rsm = sb("rsm", [P, NT], F32)
        prob = sb("prob", [P, NT, E], F32)
        top = sb("top", [P, NT, E], F32)
        tix = sb("tix", [P, NT, E], U32)
        tixf = sb("tixf", [P, NT, 2], F32)
        oh = sb("oh", [P, 2, NT, E], F32)
        msk = sb("msk", [P, NT, E], BF16)
        tmp8 = sb("tmp8", [P, 2, NT, E], F32)
        pos = sb("pos", [P, NT, E], F32)
        tot = sb("tot", [P, E], F32)
        cmp_m = sb("cmp_m", [P, E, NT], F32)
        ntile = sb("ntile", [P, E], F32)
        ends = sb("ends", [P, E], F32)
        base = sb("base", [P, E], F32)
        cmp_t = sb("cmp_t", [P, NTAB, E], F32)
        eidf = sb("eidf", [P, NTAB], F32)
        eidi = sb("eidi", [P, NTAB], I32)
        chgi = sb("chgi", [P, NTAB], I32)
        slotf = sb("slotf", [P, 2, NT], F32)
        kept = sb("kept", [P, 2, NT], F32)
        slot = [sb(f"slot{l}", [P, 2, NT], I32) for l in range(2)]
        wtok = sb("wtok", [P, 2, NT], F32)
        wsum = sb("wsum", [P, NT], F32)
        pesk = sb("pesk", [P, 2, NT], F32)
        tick = sb("tick", [P, 16], F32)

        arena0 = (nc.sbuf_base + 63) // 64 * 64
        used = [0]

        def at(kb, name, shape, dt):
            nbytes = int(np.prod(shape[1:])) * (2 if dt == BF16 else 4)
            off = int(kb * 1024)
            assert arena0 + off + nbytes <= nc.sbuf_usable_end, (name, off + nbytes, nc.sbuf_usable_end - arena0)
            return nc.alloc_sbuf_tensor_at(name, shape, dt, offset=arena0 + off)

        h_rows = at(0, "h_rows", [P, NT, D], F32)
        x_rows = at(32, "x_rows", [P, NT, D], F32)
        zero = at(64, "zero", [P, 2048], F32)
        names = ("kT", "e1", "e20", "e21", "ek", "ekv", "nf", "nb", "df", "db", "dd", "dv", "s1", "s2", "num", "rat")
        cA = {n: at(72 + 4 * i, "A_" + n, [P, 2, T], F32) for i, n in enumerate(names)}
        hT = at(136, "hT", [P, 2, KD, P], F32)
        sqj = at(140, "sqj", [P, D], F32)
        wgh = [at(16 * i, f"wgh{i}", [P, KD, 2 * F0], F32R) for i in range(2)]
        wgl = [at(32 + 16 * i, f"wgl{i}", [P, KD, 2 * F0], F32R) for i in range(2)]
        wdh = [at(64 + 8 * i, f"wdh{i}", [P, KD, D], F32R) for i in range(2)]
        wdl = [at(80 + 8 * i, f"wdl{i}", [P, KD, D], F32R) for i in range(2)]
        xr = [at(96 + 2 * i, f"xr{i}", [P, D], F32) for i in range(2)]
        xth = [at(100 + 2 * i, f"xth{i}", [P, KD, P], F32R) for i in range(2)]
        xtl = [at(104 + 2 * i, f"xtl{i}", [P, KD, P], F32R) for i in range(2)]
        ga = at(108, "ga", [P, F0], F32)
        actf = at(110, "actf", [P, F0], F32)
        ath = [at(112 + 2 * i, f"ath{i}", [P, KD, P], F32R) for i in range(2)]
        atl = [at(116 + 2 * i, f"atl{i}", [P, KD, P], F32R) for i in range(2)]
        yb = [at(120 + 2 * i, f"yb{i}", [P, D], F32) for i in range(2)]
        dnames = ("kT", "ek", "e21", "ekv", "nf", "nb", "df", "db", "dd", "dv", "s1", "s2", "num", "rat", "rt")
        rgu = [at(124 + 16 * i, f"rgu{i}", [P, KD, 2 * F0], F32) for i in range(2)]
        cD = {n: at(156 + 2 * i, "D_" + n, [P, T], F32) for i, n in enumerate(dnames[:14])}
        cD["rt"] = cD["kT"]
        rdn = at(184, "rdn", [P, KD, D], F32)
        rtb = at(192, "rtb", [P, TB, P], F32)
        y1g = [at(64 + 2 * i, f"y1g{i}", [P, D], F32) for i in range(4)]
        y2g = [at(72 + 2 * i, f"y2g{i}", [P, D], F32) for i in range(4)]
        xin = [at(80 + 2 * i, f"xin{i}", [P, D], F32) for i in range(4)]
        rin = [at(88 + 2 * i, f"rin{i}", [P, D], F32) for i in range(4)]
        xpt = [at(96 + 2 * i, f"xpt{i}", [P, D], F32) for i in range(2)]
        sgx = [at(100 + 2 * i, f"sgx{i}", [P, D], F32) for i in range(2)]
        osb = [at(104 + 2 * i, f"osb{i}", [P, D], F32) for i in range(4)]
        XTh = at(64, "XTh", [P, 2, KD, CAP], F32R)
        XTl = at(84, "XTl", [P, 2, KD, CAP], F32R)
        hth = [at(112 + 2.5 * i, f"hth{i}", [P, CAP], F32R) for i in range(2)]
        htl = [at(117 + 2.5 * i, f"htl{i}", [P, CAP], F32R) for i in range(2)]
        xg = [at(124 + 2 * i, f"xg{i}", [TXR, D], F32) for i in range(2)]
        yo = [at(128 + 2 * i, f"yo{i}", [P, D], F32) for i in range(5)]
        wrw = [at(144 + 8 * i, f"wrw{i}", [P, 2048], F32) for i in range(2)]
        wch = [at(160 + 8 * i, f"wch{i}", [P, 2048], F32R) for i in range(2)]
        wcl = [at(176 + 8 * i, f"wcl{i}", [P, 2048], F32R) for i in range(2)]

        def w1c(w, p):
            return w[p][:, 0:KD * HC].rearrange("p (k f) -> p k f", k=KD)

        def w2c(w, p):
            return w[p][:, KD * HC:].rearrange("p (s d) -> p s d", s=2)

        bank = [ctx.enter_context(nc.psum_tensor(f"bank{i}", [P, 512], F32)) for i in range(8)]
        TR = [bank[0], bank[1]]
        HTB = [bank[2], bank[3]]
        LG, RK, TOT = bank[4], bank[5], bank[6]
        GP, UP, TX, TA, YD, TRD = bank[0], bank[1], bank[2], bank[3], bank[4], bank[5]
        HB, TXF = [bank[5], bank[6]], bank[7]

        def quad(bk):
            return bk[:, :].rearrange("p (k f) -> p k f", k=4)

        s_par = sem("params_in")
        s_x = sem("x_in")
        s_zero = sem("zero_made")
        s_zout = sem("zero_filled")
        s_const = sem("pool_constants")
        s_vset = sem("vector_setup_steps")
        s_aset = sem("scalar_setup_steps")
        s_sig = sem("sigmoid_x")
        s_kin = [sem(f"k_in{i}") for i in range(2)]
        s_e1, s_e20, s_e21 = sem("exp_k"), sem("exp_k_u0"), sem("exp_k_u1")
        s_eko = [sem(f"ek_stored{i}") for i in range(2)]
        s_euo = [sem(f"eu_stored{i}") for i in range(2)]
        s_ek, s_ekv = sem("ek_clipped"), sem("ekv_made")
        s_nf, s_nb, s_df, s_db = sem("num_forward"), sem("num_backward"), sem("den_forward"), sem("den_backward")
        s_dd, s_dv = sem("bonus_den"), sem("bonus_num")
        s_s1, s_s2, s_den = sem("num_sum"), sem("den_sum"), sem("den_made")
        s_rec, c_rec = sem("den_inverse"), sem("D_den_inverse")
        s_dsum, c_dsum = sem("den_total"), sem("D_den_total")
        s_num, s_rat, s_tr = sem("num_made"), sem("ratio_made"), sem("ratio_turned")
        s_h = sem("h_part")
        s_ht, s_hte, s_lg = sem("h_turned"), sem("h_turned_copied"), sem("logits")
        s_sq = sem("h_squared")
        s_ms, s_rms = sem("mean_square"), sem("rms")
        s_vr = sem("vector_routing_steps")
        s_ex = sem("router_exp")
        s_lx = sem("router_shifted")
        s_mk = sem("expert_masks")
        s_rk = sem("ranks")
        s_slot = sem("slots_ready")
        s_sc = [sem(f"scattered{i}") for i in range(2)]
        d_xr = [sem(f"D_rows_in{i}") for i in range(2)]
        d_rgu = [sem(f"D_gate_up_in{i}") for i in range(2)]
        d_rdn = sem("D_down_in")
        d_hgu, d_lgu = sem("D_gate_up_hi"), sem("D_gate_up_lo")
        d_hdn, d_ldn = sem("D_down_hi"), sem("D_down_lo")
        d_tx, d_xh, d_xl = sem("D_rows_turned"), sem("D_xT_hi"), sem("D_xT_lo")
        d_gu, d_gelu, d_act = sem("D_gate_up_done"), sem("D_gelu"), sem("D_act")
        d_ta, d_ah, d_al = sem("D_act_turned"), sem("D_actT_hi"), sem("D_actT_lo")
        d_dn, d_ye = sem("D_down_done"), sem("D_y_copied")
        d_yo = [sem(f"D_y_stored{i}") for i in range(2)]
        c_in = sem("D_chunk_in")
        c_ekv, c_nf, c_nb, c_df, c_db = (sem("D_" + n) for n in ("ekv", "nf", "nb", "df", "db"))
        c_dd, c_dv, c_s1, c_s2, c_den = (sem("D_" + n) for n in ("dd", "dv", "s1", "s2", "den"))
        c_num, c_rat, c_tr, c_rt, c_out = (sem("D_" + n) for n in ("num", "rat", "tr", "rt", "ratio_stored"))
        s_yall = sem("layer0_rows_stored")
        e_g = [[sem(f"gathered{k}_{i}") for i in range(4)] for k in range(2)]
        e_x = [sem(f"E_x_in{i}") for i in range(4)]
        e_r = [sem(f"E_ratio_in{i}") for i in range(4)]
        e_p, e_x1, e_sg, e_h = sem("E_part"), sem("E_x1"), sem("E_sigmoid"), sem("E_h")
        g_o, g_out = sem("G_sum"), [sem(f"G_stored{i}") for i in range(4)]
        f_xg = [sem(f"F_rows_in{i}") for i in range(2)]
        f_w = [sem(f"F_weights_in{i}") for i in range(2)]
        f_wh1, f_wl1 = sem("F_w1_hi"), sem("F_w1_lo")
        f_wh2, f_wl2 = sem("F_w2_hi"), sem("F_w2_lo")
        f_tx, f_xh, f_xl = sem("F_rows_turned"), sem("F_XT_hi"), sem("F_XT_lo")
        f_h, f_hh, f_hl = sem("F_hidden"), sem("F_hidden_hi"), sem("F_hidden_lo")
        f_y, f_ye, f_yz = sem("F_y_part"), sem("F_y_copied"), sem("F_y_zeroed")
        f_yo = sem("F_y_stored")
        end_c = [sem(f"routing_ended{l}") for l in range(2)]
        end_d = sem("layer0_ended")
        end_f = sem("layer1_ended")

        def stage_ended(eng, s, of=5):
            eng.drain().then_inc(s, 1)
            eng.wait_ge(s, of)

        block = ctx.enter_context(nc.Block())

        @block.sync
        def _(sp):
            sp.dma_start(par[:, :], params).then_inc(s_par, 16)
            sp.dma_start(rowp[:, :], rowpar.partition_broadcast(P)).then_inc(s_par, 16)
            sp.dma_start(x_rows[:, :, :], x.rearrange("j p d -> p j d")).then_inc(s_x, 16)

            def load_k(b, ct):
                p = ct % 2
                static_wait(sp, s_rat, b * KD + ct - 1)
                sp.dma_start(cA["kT"][:, p, :], fs_t[b * KD + ct]).then_inc(s_kin[p], 16)

            def store_e(b, ct):
                p = ct % 2
                sp.wait_ge(s_ek, b * KD + ct + 1)
                sp.dma_start(ek_d[b * KD + ct], cA["ek"][:, p, :]).then_inc(s_eko[p], 16)
                sp.wait_ge(s_e21, b * KD + ct + 1)
                sp.dma_start(eu_d[b * KD + ct], cA["e21"][:, p, :]).then_inc(s_euo[p], 16)

            def stage_a(b):
                for ct in range(KD):
                    load_k(b, ct)
                    store_e(b, ct)

            stage_a(0)
            sp.wait_ge(s_zero, 1)
            flat = disp.rearrange("(p r) d -> p (r d)", p=P)
            for c in range(0, PADROWS // P * D, 2048):
                n = min(2048, PADROWS // P * D - c)
                sp.dma_start(flat[:, c:c + n], zero[:, 0:n]).then_inc(s_zout, 16)
            for l in range(2):
                sp.dma_start(ybuf[l][ROWS:ROWS + P, :], zero[:, 0:D]).then_inc(s_zout, 16)
            with sp.Fori(1, B) as b:
                stage_a(b)
            for p in range(2):
                sp.wait_ge(s_eko[p], 16 * NQ // 2)
                sp.wait_ge(s_euo[p], 16 * NQ // 2)
            stage_ended(sp, end_c[0])

            def load_gu(t, p, i):
                e = sp.value_load(eidi[0:1, bass.ds(t, 1)], min_val=0, max_val=E - 1)
                c = sp.value_load(chgi[0:1, bass.ds(t, 1)], min_val=0, max_val=1)
                static_wait(sp, d_lgu, t - 1)
                sp.dma_start(rgu[p][:, :, :].rearrange("p k f -> p (k f)"),
                             gu[bass.ds(e, 1)].rearrange("o p f -> (o p) f"), cond=c,
                             bounds_check="skip_entire_dma").then_inc(d_rgu[p], 16)

            def load_dn(t):
                e = sp.value_load(eidi[0:1, bass.ds(t, 1)], min_val=0, max_val=E - 1)
                c = sp.value_load(chgi[0:1, bass.ds(t, 1)], min_val=0, max_val=1)
                static_wait(sp, d_ldn, t)
                sp.dma_start(rdn[:, :, :].rearrange("p k f -> p (k f)"),
                             dn[bass.ds(e, 1)].rearrange("o p f -> (o p) f"), cond=c,
                             bounds_check="skip_entire_dma").then_inc(d_rdn, 16)

            def load_rows(t, p):
                static_wait(sp, d_tx, t - 1)
                sp.dma_start(xr[p][:, :], disp[bass.ds(t * P, P), :]).then_inc(d_xr[p], 16)

            def load_chunk(q):
                sp.dma_start(cD["kT"][:, :], fs_t[q]).then_inc(c_in, 16)
                sp.dma_start(cD["ek"][:, :], ek_d[q]).then_inc(c_in, 16)
                sp.dma_start(cD["e21"][:, :], eu_d[q]).then_inc(c_in, 16)

            def store_y(t, p):
                sp.wait_ge(d_ye, t + 1)
                sp.dma_start(ybuf[0][bass.ds(t * P, P), :], yb[p][:, :]).then_inc(d_yo[p], 16)

            load_chunk(0)
            load_gu(0, 0, 0)
            load_dn(0)
            load_rows(0, 0)
            load_gu(1, 1, 0)
            load_rows(1, 1)

            def stage_d(i, first, nxt, turn):
                for p in range(2):
                    t = 2 * i + p
                    load_dn(t + 1)
                    load_gu(t + 2, p, i)
                    load_rows(t + 2, p)
                    if p == 1 and turn:
                        sp.wait_ge(c_rt, i)
                        sp.dma_start(ratio_d[i - 1], rtb[:, :, :]).then_inc(c_out, 16)
                    if not (first and p == 0):
                        store_y(t - 1, 1 - p)
                    if p == 1 and nxt:
                        sp.wait_ge(c_dv, i + 1)
                        sp.wait_ge(c_db, i + 1)
                        load_chunk(i + 1)

            stage_d(0, True, True, False)
            with sp.Fori(1, NQ - 1) as i:
                stage_d(i, False, True, True)
            stage_d(NQ - 1, False, False, True)
            stage_d(NQ, False, False, True)
            with sp.Fori(NQ + 1, NG // 2) as i:
                stage_d(i, False, False, False)
            store_y(NG - 1, 1)
            sp.wait_ge(c_out, 16 * NQ)
            for p in range(2):
                sp.wait_ge(d_yo[p], 16 * NG // 2)
                sp.wait_ge(d_rgu[p], 16 * (NG + 2) // 2)
                sp.wait_ge(d_xr[p], 16 * (NG + 2) // 2)
            sp.wait_ge(d_rdn, 16 * (NG + 1))
            stage_ended(sp, end_d)

            for j in range(NT):
                n = j % 4
                if j >= 4:
                    sp.wait_ge(e_p, j - 3)
                sp.dma_start(xin[n][:, :], x[j]).then_inc(e_x[n], 16)
                if j >= 4:
                    sp.wait_ge(e_h, j - 3)
                b0 = j // TB * KD
                sp.dma_start(rin[n][:, :].rearrange("p (c f) -> p c f", c=KD),
                             ratio_d[b0:b0 + KD, :, j % TB, :].rearrange("c p f -> p c f")).then_inc(e_r[n], 16)
            stage_ended(sp, end_c[1])

            def load_w(c, src, p):
                static_wait(sp, f_wl2, c - 1)
                sp.dma_start(wrw[p][:, :], wc[src]).then_inc(f_w[p], 16)

            def load_xg(st, p):
                static_wait(sp, f_tx, st - 1)
                sp.dma_start(xg[p][:, :], disp[bass.ds(st * TXR, TXR), :]).then_inc(f_xg[p], 16)

            load_w(0, 0, 0)
            load_xg(0, 0)
            load_xg(1, 1)
            load_w(1, 1, 1)
            for st in range(2, NST):
                load_xg(st, st % 2)

            def stage_f(G, last):
                for p in range(2):
                    load_xg(NST + 2 * G + p, p)
                for p in range(2):
                    load_w(2 * G + 2 + p, 2 * G + p if last else 2 * G + 2 + p, p)

            with sp.Fori(0, NGRP - 1) as G:
                stage_f(G, False)
            stage_f(NGRP - 1, True)
            for p in range(2):
                sp.wait_ge(f_xg[p], 16 * (NST // 2 + NGRP))
                sp.wait_ge(f_w[p], 16 * (1 + NGRP))
            stage_ended(sp, end_f)

            for j in range(NT):
                sp.wait_ge(g_o, 2 * (j + 1))
                sp.dma_start(out[j], osb[j % 4][:, :]).then_inc(g_out[j % 4], 16)
            for n in range(4):
                sp.wait_ge(g_out[n], 16 * NT // 4)

        @block.gpsimd
        def _(pl):
            g = nc.gpsimd
            g.memset(zero[:, :], 0.0).then_inc(s_zero, 1)
            g.memset(ident[:, :], 0.0).then_inc(s_const, 1)
            g.memset(tri[:, :], 1.0).then_inc(s_const, 1)
            g.memset(ones[:, :], 1.0).then_inc(s_const, 1)
            g.memset(one8[:, :], 1.0).then_inc(s_const, 1)
            g.memset(tick[:, :], 0.0).then_inc(s_const, 1)
            g.iota(iota_i[:, :], [[1, NTAB]], base=0, channel_multiplier=0).then_inc(s_const, 1)
            pl.wait_ge(s_const, 6)
            g.affine_select(out=ident[:, :], in_=ident[:, :], compare_op=ALU.not_equal, fill=1.0, base=0,
                            pattern=[[-1, P]], channel_multiplier=1).then_inc(s_const, 1)
            g.affine_select(out=tri[:, :], in_=tri[:, :], compare_op=ALU.is_gt, fill=0.0, base=0,
                            pattern=[[1, P]], channel_multiplier=-1).then_inc(s_const, 1)
            g.tensor_copy(iota_t[:, :], iota_i[:, :]).then_inc(s_const, 1)
            pl.wait_ge(s_const, 9)
            g.tensor_copy(iota_e[:, :], iota_t[:, 0:E]).then_inc(s_const, 1)
            g.tensor_scalar(iota_m[:, :], iota_t[:, 0:NT], float(P), None, ALU.mult).then_inc(s_const, 1)

            def carry_wait(c):
                g.tensor_tensor(tick[0:1, c:c + 1], tick[0:1, 0:1], tick[0:1, 0:1], ALU.add)

            def stage_a(b):
                for ct in range(KD):
                    p, q = ct % 2, b * KD + ct
                    pl.wait_ge(s_ek, q + 1)
                    pl.wait_ge(s_e20, q + 1)
                    static_wait(pl, s_rat, q - 1)
                    static_wait(pl, s_dd, 2 * q)
                    carry_wait(9)
                    g.tensor_scalar(cA["dd"][:, p, :], cA["e20"][:, p, :], E30, None, ALU.min).then_inc(s_dd, 1)
                    pl.wait_ge(s_dd, 2 * q + 1)
                    g.tensor_tensor(cA["dd"][:, p, :], cA["dd"][:, p, :], cA["ek"][:, p, :], ALU.subtract)\
                     .then_inc(s_dd, 1)
                    pl.wait_ge(s_dd, 2 * q + 2)
                    pl.wait_ge(s_kin[p], 16 * (2 * b + ct // 2 + 1))
                    g.tensor_tensor(cA["dv"][:, p, :], cA["dd"][:, p, :], cA["kT"][:, p, :], ALU.mult)\
                     .then_inc(s_dv, 1)
                    pl.wait_ge(s_nb, q + 1)
                    g.tensor_tensor(cA["s1"][:, p, :], cA["nf"][:, p, :], cA["nb"][:, p, :], ALU.add).then_inc(s_s1, 1)
                    pl.wait_ge(s_db, q + 1)
                    g.tensor_tensor(cA["s2"][:, p, :], cA["df"][:, p, :], cA["db"][:, p, :], ALU.add).then_inc(s_s2, 1)
                    pl.wait_ge(s_s2, q + 1)
                    g.tensor_tensor(cA["dd"][:, p, :], cA["s2"][:, p, :], cA["dd"][:, p, :], ALU.add)\
                     .then_inc(s_dsum, 1)
                    pl.wait_ge(s_dsum, q + 1)
                    static_wait(pl, s_den, q)
                    carry_wait(10)
                    g.tensor_scalar(cA["dd"][:, p, :], cA["dd"][:, p, :], 1e-8, None, ALU.max).then_inc(s_den, 1)

            stage_a(0)
            with pl.Fori(1, B) as b:
                stage_a(b)

            def scatter(l):
                pl.wait_ge(s_slot, l + 1)
                pl.wait_ge(s_zout, 16 * ((PADROWS // P * D + 2047) // 2048 + 2))
                for k in range(2):
                    for j in range(NT):
                        g.indirect_dma_start(disp[0:ROWS, :], bass.IndirectOffsetOnAxis(slot[l][:, k, j:j + 1], 0),
                                             h_rows[:, j, :], None, bounds_check=ROWS - 1, oob_is_err=False)\
                         .then_inc(s_sc[l], 16)
                pl.wait_ge(s_sc[l], 16 * 2 * NT)
                stage_ended(pl, end_c[l])

            scatter(0)

            def lo_dn(t, p):
                c = pl.value_load(chgi[0:1, bass.ds(t, 1)], min_val=0, max_val=1)
                pl.wait_ge(d_hdn, t + 1)
                static_wait(pl, d_ldn, t)
                carry_wait(7)
                with pl.If(c):
                    g.tensor_tensor(wdl[p][:, :, :], rdn[:, :, :], wdh[p][:, :, :].bitcast(F32), ALU.subtract)
                g.tensor_copy(tick[0:1, 8:9], tick[0:1, 0:1]).then_inc(d_ldn, 1)

            def chunk_a(q):
                pl.wait_ge(c_in, 48 * (q + 1))
                static_wait(pl, c_rat, q)
                static_wait(pl, c_dd, 2 * q)
                carry_wait(11)
                g.tensor_scalar(cD["dd"][:, :], cD["e21"][:, :], E30, None, ALU.min).then_inc(c_dd, 1)
                pl.wait_ge(c_dd, 2 * q + 1)
                g.tensor_tensor(cD["dd"][:, :], cD["dd"][:, :], cD["ek"][:, :], ALU.subtract).then_inc(c_dd, 1)
                pl.wait_ge(c_dd, 2 * q + 2)
                g.tensor_tensor(cD["dv"][:, :], cD["dd"][:, :], cD["kT"][:, :], ALU.mult).then_inc(c_dv, 1)

            def chunk_b(q):
                pl.wait_ge(c_nb, q + 1)
                g.tensor_tensor(cD["s1"][:, :], cD["nf"][:, :], cD["nb"][:, :], ALU.add).then_inc(c_s1, 1)
                pl.wait_ge(c_db, q + 1)
                g.tensor_tensor(cD["s2"][:, :], cD["df"][:, :], cD["db"][:, :], ALU.add).then_inc(c_s2, 1)
                pl.wait_ge(c_s2, q + 1)
                g.tensor_tensor(cD["dd"][:, :], cD["s2"][:, :], cD["dd"][:, :], ALU.add).then_inc(c_dsum, 1)
                pl.wait_ge(c_dsum, q + 1)
                static_wait(pl, c_den, q)
                carry_wait(12)
                g.tensor_scalar(cD["dd"][:, :], cD["dd"][:, :], 1e-8, None, ALU.max).then_inc(c_den, 1)

            lo_dn(0, 0)

            def stage_d(i, cond):
                if cond:
                    chunk_a(i)
                lo_dn(2 * i + 1, 1)
                if cond:
                    chunk_b(i)
                lo_dn(2 * i + 2, 0)

            stage_d(0, True)
            with pl.Fori(1, NQ) as i:
                stage_d(i, True)
            with pl.Fori(NQ, NG // 2) as i:
                stage_d(i, False)
            stage_ended(pl, end_d)

            def gather(l):
                for j in range(NT):
                    n = j % 4
                    for k, dst in ((0, y1g), (1, y2g)):
                        if l == 0 and j >= 4:
                            pl.wait_ge(e_p if k == 0 else e_x1, j - 3)
                        if l == 1 and j >= 4:
                            pl.wait_ge(g_o, 2 * (j - 4) + 1 + k)
                        g.indirect_dma_start(dst[n][:, :], None, ybuf[l][:, :],
                                             bass.IndirectOffsetOnAxis(slot[l][:, k, j:j + 1], 0),
                                             bounds_check=ROWS + P - 1, oob_is_err=False)\
                         .then_inc(e_g[k][n], 16)

            gather(0)
            scatter(1)

            def lo_w(part, wh_sem, wl_sem, c, p):
                pl.wait_ge(wh_sem, c + 1)
                g.tensor_tensor(part(wcl, p), part(wrw, p), part(wch, p).bitcast(F32), ALU.subtract)\
                 .then_inc(wl_sem, 1)

            lo_w(w1c, f_wh1, f_wl1, 0, 0)
            lo_w(w2c, f_wh2, f_wl2, 0, 0)
            lo_w(w1c, f_wh1, f_wl1, 1, 1)
            with pl.Fori(0, NGRP) as G:
                lo_w(w1c, f_wh1, f_wl1, 2 * G + 2, 0)
                lo_w(w2c, f_wh2, f_wl2, 2 * G + 1, 1)
                lo_w(w2c, f_wh2, f_wl2, 2 * G + 2, 0)
                lo_w(w1c, f_wh1, f_wl1, 2 * G + 3, 1)
            stage_ended(pl, end_f)
            gather(1)

        @block.scalar
        def _(act):
            s = nc.scalar
            act.wait_ge(s_vset, 1)
            s.activation(tf[:, :], tsum[:, :], ACT.Sigmoid).then_inc(s_aset, 1)
            act.wait_ge(s_x, 16)
            for c in range(4):
                s.activation(x_rows[:, 4 * c:4 * c + 4, :], x_rows[:, 4 * c:4 * c + 4, :], ACT.Sigmoid)\
                 .then_inc(s_sig, 1)
            act.wait_ge(s_par, 32)
            for l in range(2):
                s.activation(ew[:, l, :], w_col[l], ACT.Exp).then_inc(s_aset, 1)
            act.wait_ge(s_aset, 3)
            s.activation(dcy[:, :, :], ew[:, :, :], ACT.Exp, scale=-1.0).then_inc(s_aset, 1)

            def route_tile(l, j, n):
                p = n % 2
                act.wait_ge(s_ht, NT * l + j + 1)
                static_wait(act, s_lg, NT * l + j - 1)
                s.activation(hT[:, p, :, :], quad(HTB[p]), ACT.Copy).then_inc(s_hte, 1)
                if l == 0:
                    static_wait(act, s_sq, j)
                    s.activation(sqj[:, :], h_rows[:, j, :], ACT.Square, accum_out=ssq[:, bass.ds(j, 1)])\
                     .then_inc(s_sq, 1)

            def stage_a(b, route):
                for ct in range(KD):
                    p, q = ct % 2, b * KD + ct
                    act.wait_ge(s_kin[p], 16 * (2 * b + ct // 2 + 1))
                    static_wait(act, s_ekv, q - 1)
                    s.activation(cA["e1"][:, p, :], cA["kT"][:, p, :], ACT.Exp).then_inc(s_e1, 1)
                    static_wait(act, s_dv, q - 1)
                    s.activation(cA["e20"][:, p, :], cA["kT"][:, p, :], ACT.Exp,
                                 bias=u_col[0][:, ct:ct + 1]).then_inc(s_e20, 1)
                    if not isinstance(b, int) or q >= 2:
                        act.wait_ge(s_euo[p], 16 * (2 * b + ct // 2))
                    s.activation(cA["e21"][:, p, :], cA["kT"][:, p, :], ACT.Exp,
                                 bias=u_col[1][:, ct:ct + 1]).then_inc(s_e21, 1)
                if route:
                    for c in range(TB):
                        route_tile(0, (b - 1) * TB + c, c)

            stage_a(0, False)
            stage_a(1, True)
            with act.Fori(2, B) as b:
                stage_a(b, True)
            for c in range(TB):
                route_tile(0, (B - 1) * TB + c, c)

            def softmax(l):
                act.wait_ge(s_lx, l + 1)
                s.activation(ex[:, :, :], lgs[:, :, :], ACT.Exp).then_inc(s_ex, 1)
                stage_ended(act, end_c[l])

            act.wait_ge(s_ms, 1)
            s.activation(rms[:, :], rstd[:, :], ACT.Sqrt).then_inc(s_rms, 1)
            softmax(0)

            def hi_gu(t, p, n_in):
                c = act.value_load(chgi[0:1, bass.ds(t, 1)], min_val=0, max_val=1)
                act.wait_ge(d_rgu[p], 16 * n_in)
                static_wait(act, d_gu, t - 1)
                static_wait(act, d_hgu, t)
                s.activation(tick[0:1, 1:2], tick[0:1, 0:1], ACT.Copy)
                with act.If(c):
                    s.activation(wgh[p][:, :, :], rgu[p][:, :, :], ACT.Copy)
                s.activation(tick[0:1, 2:3], tick[0:1, 0:1], ACT.Copy).then_inc(d_hgu, 1)

            def hi_dn(t, p):
                c = act.value_load(chgi[0:1, bass.ds(t, 1)], min_val=0, max_val=1)
                act.wait_ge(d_rdn, 16 * (t + 1))
                static_wait(act, d_dn, t - 1)
                static_wait(act, d_hdn, t)
                s.activation(tick[0:1, 3:4], tick[0:1, 0:1], ACT.Copy)
                with act.If(c):
                    s.activation(wdh[p][:, :, :], rdn[:, :, :], ACT.Copy)
                s.activation(tick[0:1, 4:5], tick[0:1, 0:1], ACT.Copy).then_inc(d_hdn, 1)

            def hi_x(t, p):
                act.wait_ge(d_tx, t + 1)
                s.activation(xth[p][:, :, :], quad(TX), ACT.Copy).then_inc(d_xh, 1)

            hi_gu(0, 0, 1)
            hi_dn(0, 0)
            hi_x(0, 0)

            def stage_d(i, first, turn):
                for p in range(2):
                    t = 2 * i + p
                    hi_gu(t + 1, 1 - p, i + 1 + p)
                    act.wait_ge(d_gu, t + 1)
                    s.activation(ga[:, :], GP[:, :], ACT.Gelu).then_inc(d_gelu, 1)
                    if not (first and p == 0):
                        act.wait_ge(d_dn, t)
                        static_wait(act, d_yo[1 - p], 16 * (i - 1 + p))
                        s.activation(yb[1 - p][:, :], YD[:, :], ACT.Copy).then_inc(d_ye, 1)
                    hi_x(t + 1, 1 - p)
                    act.wait_ge(d_ta, t + 1)
                    s.activation(ath[p][:, :, :], quad(TA), ACT.Copy).then_inc(d_ah, 1)
                    if p == 1 and turn:
                        act.wait_ge(c_tr, i)
                        static_wait(act, c_out, 16 * (i - 1))
                        s.activation(rtb[:, :, :], quad(TRD), ACT.Copy).then_inc(c_rt, 1)
                    hi_dn(t + 1, 1 - p)

            stage_d(0, True, False)
            stage_d(1, False, True)
            with act.Fori(2, NQ + 1) as i:
                stage_d(i, False, True)
            with act.Fori(NQ + 1, NG // 2) as i:
                stage_d(i, False, False)
            act.wait_ge(d_dn, NG)
            act.wait_ge(d_yo[1], 16 * (NG // 2 - 1))
            s.activation(yb[1][:, :], YD[:, :], ACT.Copy).then_inc(d_ye, 1)
            stage_ended(act, end_d)

            for j in range(NT):
                act.wait_ge(e_x1, j + 1)
                if j >= 2:
                    act.wait_ge(e_h, j - 1)
                s.activation(sgx[j % 2][:, :], x_rows[:, j, :], ACT.Sigmoid).then_inc(e_sg, 1)
                if j >= 1:
                    route_tile(1, j - 1, j - 1)
            route_tile(1, NT - 1, NT - 1)
            softmax(1)

            def hi_xg(st, par_next, cols):
                act.wait_ge(f_tx, st + 1)
                s.activation(XTh[:, par_next, :, cols], TXF[:, 0:4 * TXR].rearrange("p (k f) -> p k f", k=KD),
                             ACT.Copy).then_inc(f_xh, 1)

            def hi_w(part, wh_sem, c, p, n_in):
                act.wait_ge(f_w[p], 16 * n_in)
                s.activation(part(wch, p), part(wrw, p), ACT.Copy).then_inc(wh_sem, 1)

            def hi_h(f, p):
                for h in range(2):
                    act.wait_ge(f_h, 2 * f + h + 1)
                    s.activation(hth[p][:, h * HALF:(h + 1) * HALF], HB[h][:, 0:HALF], ACT.Relu).then_inc(f_hh, 1)

            hi_w(w1c, f_wh1, 0, 0, 1)
            for st in range(NST):
                hi_xg(st, 0, slice(st * TXR, (st + 1) * TXR))
            hi_w(w2c, f_wh2, 0, 0, 1)
            hi_w(w1c, f_wh1, 1, 1, 1)
            hi_h(0, 0)

            def stage_f(e, g, ep, last):
                G = 4 * e + g
                for q in range(4):
                    if q % 2 == 0:
                        hi_xg(NST + 2 * G + q // 2, 1 - ep, bass.ds((2 * g + q // 2) * TXR, TXR))
                    hi_h(4 * G + q + 1, (q + 1) % 2)
                    if q == 0:
                        hi_w(w1c, f_wh1, 2 * G + 2, 0, G + 2)
                        hi_w(w2c, f_wh2, 2 * G + 1, 1, G + 1)
                    if q == 2:
                        hi_w(w2c, f_wh2, 2 * G + 2, 0, G + 2)
                        hi_w(w1c, f_wh1, 2 * G + 3, 1, G + 2)
                if last:
                    for j in range(5):
                        act.wait_ge(f_y, 20 * G + 15 + j + 1)
                        if j == 0 and ep == 1:
                            act.wait_ge(f_yo, 80 * e)
                        s.activation(yo[j][:, :], bank[j][:, :], ACT.Copy).then_inc(f_ye, 1)
                    for j in range(5):
                        act.wait_ge(f_ye, 5 * e + j + 1)
                        act.dma_start(ybuf[1][bass.ds(e * CAP + j * P, P), :], yo[j][:, :]).then_inc(f_yo, 16)

            with act.Fori(0, E // 2) as e2:
                for ep in range(2):
                    e = 2 * e2 + ep
                    with act.Fori(0, 3) as g:
                        stage_f(e, g, ep, False)
                    stage_f(e, 3, ep, True)
                act.wait_ge(f_yo, 160 * (e2 + 1))
            stage_ended(act, end_f)

        @block.tensor
        def _(pe):
            m = nc.tensor

            def turn_rows(bank_, rows, np_=P, width=P):
                for k in range(KD):
                    last = m.transpose(bank_[:, k * width:(k + 1) * width], rows(k), ident[0:np_, 0:np_])
                return last

            def route_tile(l, j, n):
                p = n % 2
                static_wait(pe, s_hte, NT * l + j - 1)
                turn_rows(HTB[p], lambda k: h_rows[:, j, k * P:(k + 1) * P]).then_inc(s_ht, 1)
                pe.wait_ge(s_hte, NT * l + j + 1)
                w = gate0s if l == 0 else gate[1]
                for k in range(KD):
                    last = m.matmul(LG[:, bass.ds(j * E, E)], hT[:, p, k, :], w[:, k, :],
                                    start=(k == 0), stop=(k == KD - 1))
                last.then_inc(s_lg, 1)

            pe.wait_ge(s_const, 9)
            pe.wait_ge(s_vset, 15)

            def turn_ratio(q, ct):
                pe.wait_ge(s_rat, q + 1)
                static_wait(pe, s_h, q - 1)
                turn_rows(TR[ct % 2], lambda j: cA["rat"][:, ct % 2, j * P:(j + 1) * P]).then_inc(s_tr, 1)

            def stage_a(b, route):
                for ct in range(3):
                    turn_ratio(b * KD + ct, ct)
                if route:
                    pe.wait_ge(s_h, b * KD)
                    for c in range(TB):
                        route_tile(0, (b - 1) * TB + c, c)
                turn_ratio(b * KD + 3, 3)

            for b in range(B):
                stage_a(b, b > 0)
            pe.wait_ge(s_h, NQ)
            for c in range(TB):
                route_tile(0, (B - 1) * TB + c, c)

            def ranks(l):
                pe.wait_ge(s_mk, l + 1)
                m.matmul(RK[:, 0:NT * E], tri[:, :], msk[:, :, :].rearrange("p j e -> p (j e)"),
                         start=True, stop=False, skip_group_check=True)
                for j in range(NT - 1):
                    m.matmul(RK[:, (j + 1) * E:NT * E].rearrange("p (j e) -> p j e", e=E), ones[:, :],
                             msk[:, j:j + 1, :].to_broadcast([P, NT - 1 - j, E]),
                             start=False, stop=(j == NT - 2), skip_group_check=True)
                for j in range(NT):
                    last = m.matmul(TOT[:, 0:E], ones[:, :], msk[:, j, :], start=(j == 0), stop=(j == NT - 1))
                last.then_inc(s_rk, 1)

            ranks(0)
            stage_ended(pe, end_c[0])

            def turn_x(t, p, n_in):
                pe.wait_ge(d_xr[p], 16 * n_in)
                turn_rows(TX, lambda k: xr[p][:, k * P:(k + 1) * P]).then_inc(d_tx, 1)

            def hidden(t, p):
                pe.wait_ge(d_xl, t + 1)
                pe.wait_ge(d_lgu, t + 1)
                for k in range(KD):
                    for n, (a, w) in enumerate(((xth, wgh), (xth, wgl), (xtl, wgh))):
                        for h, acc in enumerate((GP, UP)):
                            last = m.matmul(acc[:, :], a[p][:, k, :], w[p][:, k, h * F0:(h + 1) * F0],
                                            start=(k == 0 and n == 0), stop=(k == KD - 1 and n == 2))
                last.then_inc(d_gu, 1)

            def turn_act(t):
                pe.wait_ge(d_act, t + 1)
                turn_rows(TA, lambda k: actf[:, k * P:(k + 1) * P]).then_inc(d_ta, 1)

            def down(t, p):
                pe.wait_ge(d_al, t + 1)
                pe.wait_ge(d_ldn, t + 1)
                static_wait(pe, d_ye, t)
                for k in range(KD):
                    for n, (a, w) in enumerate(((ath, wdh), (ath, wdl), (atl, wdh))):
                        last = m.matmul(YD[:, :], a[p][:, k, :], w[p][:, k, :],
                                        start=(k == 0 and n == 0), stop=(k == KD - 1 and n == 2))
                last.then_inc(d_dn, 1)

            turn_x(0, 0, 1)

            def stage_d(i, first, turn):
                for p in range(2):
                    t = 2 * i + p
                    hidden(t, p)
                    if not (first and p == 0):
                        down(t - 1, 1 - p)
                    turn_x(t + 1, 1 - p, i + 1 + p)
                    turn_act(t)
                    if p == 1 and turn:
                        pe.wait_ge(c_rat, i)
                        static_wait(pe, c_rt, i - 1)
                        turn_rows(TRD, lambda j: cD["rat"][:, j * P:(j + 1) * P]).then_inc(c_tr, 1)

            stage_d(0, True, False)
            stage_d(1, False, True)
            with pe.Fori(2, NQ + 1) as i:
                stage_d(i, False, True)
            with pe.Fori(NQ + 1, NG // 2) as i:
                stage_d(i, False, False)
            down(NG - 1, 1)
            stage_ended(pe, end_d)

            for j in range(NT):
                pe.wait_ge(e_h, j + 1)
                route_tile(1, j, j)
            ranks(1)
            stage_ended(pe, end_c[1])

            def turn_xg(st, p, n_in):
                pe.wait_ge(f_xg[p], 16 * n_in)
                static_wait(pe, f_xl, st)
                turn_rows(TXF, lambda k: xg[p][:, k * P:(k + 1) * P], TXR, TXR).then_inc(f_tx, 1)

            def hidden1(f, sub, wp, xp):
                for h in range(2):
                    static_wait(pe, f_hl, 2 * (f - 1) + h + 1)
                    for k in range(KD):
                        for n, (w, a) in enumerate(((wch, XTh), (wch, XTl), (wcl, XTh))):
                            last = m.matmul(HB[h][:, 0:HALF], w1c(w, wp)[:, k, sub * P:(sub + 1) * P],
                                            a[:, xp, k, h * HALF:(h + 1) * HALF],
                                            start=(k == 0 and n == 0), stop=(k == KD - 1 and n == 2))
                    last.then_inc(f_h, 1)

            def y_part(f, sub, wp, hp, zeroed):
                pe.wait_ge(f_hl, 2 * f + 2)
                for j in range(5):
                    if zeroed is not None:
                        pe.wait_ge(f_yz, zeroed + j)
                    for n, (a, w) in enumerate(((hth, wch), (hth, wcl), (htl, wch))):
                        last = m.matmul(bank[j][:, :], a[hp][:, j * P:(j + 1) * P], w2c(w, wp)[:, sub, :],
                                        start=False, stop=False, skip_group_check=True)
                    last.then_inc(f_y, 1)

            for st in range(NST):
                turn_xg(st, st % 2, st // 2 + 1)
            pe.wait_ge(f_xl, NST)
            pe.wait_ge(f_wl1, 1)
            hidden1(0, 0, 0, 0)

            def stage_f(e, g, ep, last):
                G = 4 * e + g
                for q in range(4):
                    f = 4 * G + q
                    if q % 2 == 0:
                        turn_xg(NST + 2 * G + q // 2, q // 2, NST // 2 + G + 1)
                    if q == 1:
                        pe.wait_ge(f_wl1, 2 * G + 2)
                    if q == 3:
                        pe.wait_ge(f_wl1, 2 * G + 3)
                        if last:
                            pe.wait_ge(f_xl, NST * (e + 2))
                    hidden1(f + 1, (q + 1) % 2, ((q + 1) // 2) % 2, 1 - ep if last and q == 3 else ep)
                    if q == 0:
                        pe.wait_ge(f_wl2, 2 * G + 1)
                    if q == 2:
                        pe.wait_ge(f_wl2, 2 * G + 2)
                    y_part(f, q % 2, q // 2, q % 2, 5 * e + 1 if q == 0 else None)

            with pe.Fori(0, E // 2) as e2:
                for ep in range(2):
                    e = 2 * e2 + ep
                    with pe.Fori(0, 3) as g:
                        stage_f(e, g, ep, False)
                    stage_f(e, 3, ep, True)
            stage_ended(pe, end_f)

        @block.vector
        def _(dve):
            v = nc.vector

            dve.wait_ge(s_par, 32)
            v.tensor_reduce(tsum[:, :], rowp[:, 0:B * P].rearrange("p (b t) -> p b t", b=B), AX.X, ALU.add)\
             .then_inc(s_vset, 1)
            dve.wait_ge(s_aset, 1)
            v.tensor_scalar(half[:, :], tf[:, :], 0.5, 0.5, ALU.mult, ALU.add).then_inc(s_vset, 1)
            v.tensor_scalar(gsc[:, :], tf[:, :], 0.2, 0.8, ALU.mult, ALU.add).then_inc(s_vset, 1)
            dve.wait_ge(s_aset, 4)
            dve.wait_ge(s_vset, 3)
            for l in range(2):
                for b in range(B):
                    v.tensor_scalar(dec[:, l, b, :], dcy[:, l, :], half[:, b:b + 1], None, ALU.mult)\
                     .then_inc(s_vset, 1)
            for k in range(KD):
                v.tensor_scalar(gate0s[:, k, :], gate[0][:, k, :], rs_col[:, k:k + 1], float(D) ** -0.5,
                                ALU.mult, ALU.mult).then_inc(s_vset, 1)
            dve.wait_ge(s_vset, 15)

            def scan(dst, src, d, reverse):
                st = slice(None, None, -1) if reverse else slice(None)
                return v.tensor_tensor_scan(dst[:, st], d.to_broadcast([P, T]), src[:, st], 0.0,
                                            ALU.mult, ALU.add)

            def scans(b, ct):
                p, q = ct % 2, b * KD + ct
                d = dec[:, 0, :, :].rearrange("p b c -> p (b c)")[:, bass.ds(q, 1)]
                dve.wait_ge(s_e1, q + 1)
                static_wait(dve, s_eko[p], 16 * (2 * b + ct // 2))
                v.tensor_scalar(cA["ek"][:, p, :], cA["e1"][:, p, :], E30, None, ALU.min).then_inc(s_ek, 1)
                v.scalar_tensor_tensor(cA["ekv"][:, p, :], cA["e1"][:, p, :], E30, cA["kT"][:, p, :],
                                       ALU.min, ALU.mult).then_inc(s_ekv, 1)
                dve.wait_ge(s_ekv, q + 1)
                scan(cA["nf"][:, p, :], cA["ekv"][:, p, :], d, False).then_inc(s_nf, 1)
                scan(cA["nb"][:, p, :], cA["ekv"][:, p, :], d, True).then_inc(s_nb, 1)
                dve.wait_ge(s_ek, q + 1)
                scan(cA["df"][:, p, :], cA["ek"][:, p, :], d, False).then_inc(s_df, 1)
                scan(cA["db"][:, p, :], cA["ek"][:, p, :], d, True).then_inc(s_db, 1)

            def ratio(q, p):
                dve.wait_ge(s_s1, q + 1)
                v.tensor_tensor(cA["num"][:, p, :], cA["s1"][:, p, :], cA["dv"][:, p, :], ALU.add).then_inc(s_num, 1)
                dve.wait_ge(s_den, q + 1)
                v.reciprocal(cA["dd"][:, p, :], cA["dd"][:, p, :]).then_inc(s_rec, 1)
                dve.wait_ge(s_rec, q + 1)
                v.tensor_tensor(cA["rat"][:, p, :], cA["num"][:, p, :], cA["dd"][:, p, :], ALU.mult)\
                 .then_inc(s_rat, 1)

            def h_part(b, ct):
                q = b * KD + ct
                dve.wait_ge(s_tr, q + 1)
                rows = bass.ds(b * TB, TB)
                v.scalar_tensor_tensor(h_rows[:, rows, ct * P:(ct + 1) * P], x_rows[:, rows, ct * P:(ct + 1) * P],
                                       gsc[:, bass.ds(b, 1)], quad(TR[ct % 2]), ALU.mult, ALU.mult)\
                 .then_inc(s_h, 1)

            def stage_a(b, first):
                for ct in range(KD):
                    scans(b, ct)
                    if not (first and ct == 0):
                        ratio(b * KD + ct - 1, (ct + 1) % 2)
                    if ct >= 2:
                        h_part(b, ct - 2)
                    elif not first:
                        h_part(b - 1, ct + 2)

            dve.wait_ge(s_sig, 4)
            stage_a(0, True)
            with dve.Fori(1, B) as b:
                stage_a(b, False)
            ratio(NQ - 1, 1)
            h_part(B - 1, 2)
            h_part(B - 1, 3)

            steps = [0]

            def link(ins):
                steps[0] += 1
                ins.then_inc(s_vr, 1)
                dve.wait_ge(s_vr, steps[0])

            def over_e(a):
                return a.unsqueeze(2).to_broadcast([P, NT, E])

            def routing(l):
                dve.wait_ge(s_lg, NT * (l + 1))
                lg = LG[:, 0:NT * E].rearrange("p (j e) -> p j e", e=E)
                if l == 0:
                    dve.wait_ge(s_sq, NT)
                    v.tensor_scalar(rstd[:, :], ssq[:, :], 1.0 / D, 1e-6, ALU.mult, ALU.add).then_inc(s_ms, 1)
                    dve.wait_ge(s_rms, 1)
                    link(v.reciprocal(rstd[:, :], rms[:, :]))
                    link(v.tensor_tensor(lgs[:, :, :], lg, over_e(rstd[:, :]), ALU.mult))
                else:
                    link(v.tensor_copy(lgs[:, :, :], lg))
                link(v.tensor_reduce(mx[:, :], lgs[:, :, :], AX.X, ALU.max))
                v.tensor_tensor(lgs[:, :, :], lgs[:, :, :], over_e(mx[:, :]), ALU.subtract).then_inc(s_lx, 1)
                dve.wait_ge(s_ex, l + 1)
                link(v.tensor_reduce(sm[:, :], ex[:, :, :], AX.X, ALU.add))
                link(v.reciprocal(rsm[:, :], sm[:, :]))
                link(v.tensor_tensor(prob[:, :, :], ex[:, :, :], over_e(rsm[:, :]), ALU.mult))
                for j in range(NT):
                    last = v.max(top[:, j, :], prob[:, j, :])
                link(last)
                for j in range(NT):
                    last = v.max_index(tix[:, j, :], top[:, j, :], prob[:, j, :])
                link(last)
                link(v.tensor_copy(tixf[:, :, :], tix[:, :, 0:2]))
                for k in range(2):
                    last = v.tensor_tensor(oh[:, k, :, :], iota_e[:, :].unsqueeze(1).to_broadcast([P, NT, E]),
                                           over_e(tixf[:, :, k]), ALU.is_equal)
                link(last)
                v.tensor_tensor(msk[:, :, :], oh[:, 0, :, :], oh[:, 1, :, :], ALU.add).then_inc(s_mk, 1)
                dve.wait_ge(s_rk, l + 1)
                rank = RK[:, 0:NT * E].rearrange("p (j e) -> p j e", e=E)
                if l == 0:
                    link(v.tensor_copy(tot[:, :], TOT[:, 0:E]))
                    link(v.tensor_tensor(cmp_m[:, :, :], tot[:, :].unsqueeze(2).to_broadcast([P, E, NT]),
                                         iota_m[:, :].unsqueeze(1).to_broadcast([P, E, NT]), ALU.is_gt))
                    link(v.tensor_reduce(ntile[:, :], cmp_m[:, :, :], AX.X, ALU.add))
                    link(v.tensor_tensor_scan(ends[:, :], one8[:, :], ntile[:, :], 0.0, ALU.mult, ALU.add))
                    link(v.tensor_tensor(base[:, :], ends[:, :], ntile[:, :], ALU.subtract))
                    link(v.tensor_scalar(base[:, :], base[:, :], float(P), None, ALU.mult))
                    link(v.tensor_tensor(pos[:, :, :], rank, base[:, :].unsqueeze(1).to_broadcast([P, NT, E]), ALU.add))
                    link(v.tensor_tensor(cmp_t[:, :, :], ends[:, :].unsqueeze(1).to_broadcast([P, NTAB, E]),
                                         iota_t[:, :].unsqueeze(2).to_broadcast([P, NTAB, E]), ALU.is_le))
                    link(v.tensor_reduce(eidf[:, :], cmp_t[:, :, :], AX.X, ALU.add))
                    link(v.tensor_scalar(eidf[:, :], eidf[:, :], float(E - 1), None, ALU.min))
                    v.tensor_copy(eidi[:, :], eidf[:, :])
                    link(v.memset(chgi[:, :], 1))
                    v.tensor_tensor(chgi[:, 2:NG], eidf[:, 2:NG], eidf[:, 0:NG - 2], ALU.not_equal)
                    link(v.memset(chgi[:, NG:NTAB], 0))
                else:
                    link(v.tensor_copy(pos[:, :, :], rank))
                for k in range(2):
                    last = v.tensor_tensor(tmp8[:, k, :, :], oh[:, k, :, :], pos[:, :, :], ALU.mult)
                link(last)
                link(v.tensor_reduce(slotf[:, :, :], tmp8[:, :, :, :], AX.X, ALU.add))
                topk = top[:, :, 0:2].rearrange("p j k -> p k j")
                if l == 0:
                    link(v.tensor_tensor(wsum[:, :], top[:, :, 0], top[:, :, 1], ALU.add))
                    link(v.tensor_scalar(wsum[:, :], wsum[:, :], 1e-12, None, ALU.max))
                    link(v.reciprocal(wsum[:, :], wsum[:, :]))
                    pes = rowp[:, B * P:B * P + E].unsqueeze(1).to_broadcast([P, NT, E])
                    for k in range(2):
                        last = v.tensor_tensor(tmp8[:, k, :, :], oh[:, k, :, :], pes, ALU.mult)
                    link(last)
                    link(v.tensor_reduce(pesk[:, :, :], tmp8[:, :, :, :], AX.X, ALU.add))
                    for k in range(2):
                        last = v.tensor_tensor(wtok[:, k, :], top[:, :, k], wsum[:, :], ALU.mult)
                    link(last)
                    link(v.tensor_tensor(wtok[:, :, :], wtok[:, :, :], pesk[:, :, :], ALU.mult))
                else:
                    link(v.tensor_scalar(kept[:, :, :], slotf[:, :, :], float(CAP), None, ALU.is_lt))
                    for k in range(2):
                        last = v.scalar_tensor_tensor(slotf[:, k, :], tixf[:, :, k], float(CAP), slotf[:, k, :],
                                                      ALU.mult, ALU.add)
                    link(last)
                    link(v.scalar_tensor_tensor(slotf[:, :, :], slotf[:, :, :], float(ROWS), kept[:, :, :],
                                                ALU.subtract, ALU.mult))
                    link(v.tensor_scalar(slotf[:, :, :], slotf[:, :, :], float(ROWS), None, ALU.add))
                    for k in range(2):
                        last = v.tensor_tensor(wtok[:, k, :], top[:, :, k], kept[:, k, :], ALU.mult)
                    link(last)
                v.tensor_copy(slot[l][:, :, :], slotf[:, :, :]).then_inc(s_slot, 1)
                stage_ended(dve, end_c[l])

            routing(0)

            def lo_gu(t, p):
                c = dve.value_load(chgi[0:1, bass.ds(t, 1)], min_val=0, max_val=1)
                dve.wait_ge(d_hgu, t + 1)
                static_wait(dve, d_lgu, t)
                v.tensor_copy(tick[0:1, 5:6], tick[0:1, 0:1])
                with dve.If(c):
                    v.tensor_tensor(wgl[p][:, :, :], rgu[p][:, :, :], wgh[p][:, :, :].bitcast(F32), ALU.subtract)
                v.tensor_copy(tick[0:1, 6:7], tick[0:1, 0:1]).then_inc(d_lgu, 1)

            def lo_x(t, p):
                dve.wait_ge(d_xh, t + 1)
                v.tensor_tensor(xtl[p][:, :, :], quad(TX), xth[p][:, :, :].bitcast(F32), ALU.subtract)\
                 .then_inc(d_xl, 1)

            def chunk_num(q):
                d = dec[:, 1, :, :].rearrange("p b c -> p (b c)")[:, bass.ds(q, 1)]
                dve.wait_ge(c_in, 48 * (q + 1))
                v.tensor_tensor(cD["ekv"][:, :], cD["ek"][:, :], cD["kT"][:, :], ALU.mult).then_inc(c_ekv, 1)
                dve.wait_ge(c_ekv, q + 1)
                scan(cD["nf"], cD["ekv"], d, False).then_inc(c_nf, 1)
                scan(cD["nb"], cD["ekv"], d, True).then_inc(c_nb, 1)

            def chunk_den(q):
                d = dec[:, 1, :, :].rearrange("p b c -> p (b c)")[:, bass.ds(q, 1)]
                scan(cD["df"], cD["ek"], d, False).then_inc(c_df, 1)
                scan(cD["db"], cD["ek"], d, True).then_inc(c_db, 1)

            def chunk_ratio(q):
                dve.wait_ge(c_s1, q + 1)
                v.tensor_tensor(cD["num"][:, :], cD["s1"][:, :], cD["dv"][:, :], ALU.add).then_inc(c_num, 1)
                dve.wait_ge(c_den, q + 1)
                v.reciprocal(cD["dd"][:, :], cD["dd"][:, :]).then_inc(c_rec, 1)
                dve.wait_ge(c_rec, q + 1)
                static_wait(dve, c_tr, q)
                v.tensor_tensor(cD["rat"][:, :], cD["num"][:, :], cD["dd"][:, :], ALU.mult).then_inc(c_rat, 1)

            lo_gu(0, 0)
            lo_x(0, 0)

            def stage_d(i, cond, turn):
                for p in range(2):
                    t = 2 * i + p
                    lo_gu(t + 1, 1 - p)
                    dve.wait_ge(d_gelu, t + 1)
                    v.tensor_tensor(actf[:, :], ga[:, :], UP[:, :], ALU.mult).then_inc(d_act, 1)
                    lo_x(t + 1, 1 - p)
                    dve.wait_ge(d_ah, t + 1)
                    v.tensor_tensor(atl[p][:, :, :], quad(TA), ath[p][:, :, :].bitcast(F32), ALU.subtract)\
                     .then_inc(d_al, 1)
                    if p == 0 and turn:
                        chunk_ratio(i - 1)
                    if cond:
                        (chunk_num if p == 0 else chunk_den)(i)

            stage_d(0, True, False)
            stage_d(1, True, True)
            with dve.Fori(2, NQ) as i:
                stage_d(i, True, True)
            stage_d(NQ, False, True)
            with dve.Fori(NQ + 1, NG // 2) as i:
                stage_d(i, False, False)
            stage_ended(dve, end_d)

            def h1(j):
                dve.wait_ge(e_sg, j + 1)
                dve.wait_ge(e_r[j % 4], 16 * (j // 4 + 1))
                v.scalar_tensor_tensor(h_rows[:, j, :], sgx[j % 2][:, :], gsc[:, j // TB:j // TB + 1],
                                       rin[j % 4][:, :], ALU.mult, ALU.mult).then_inc(e_h, 1)

            for j in range(NT):
                n = j % 4
                dve.wait_ge(e_g[0][n], 16 * (j // 4 + 1))
                dve.wait_ge(e_x[n], 16 * (j // 4 + 1))
                v.scalar_tensor_tensor(xpt[j % 2][:, :], y1g[n][:, :], wtok[:, 0, j:j + 1], xin[n][:, :],
                                       ALU.mult, ALU.add).then_inc(e_p, 1)
                dve.wait_ge(e_p, j + 1)
                dve.wait_ge(e_g[1][n], 16 * (j // 4 + 1))
                v.scalar_tensor_tensor(x_rows[:, j, :], y2g[n][:, :], wtok[:, 1, j:j + 1], xpt[j % 2][:, :],
                                       ALU.mult, ALU.add).then_inc(e_x1, 1)
                if j >= 1:
                    h1(j - 1)
            h1(NT - 1)
            routing(1)

            def lo_xg(st, par_next, cols):
                dve.wait_ge(f_xh, st + 1)
                v.tensor_tensor(XTl[:, par_next, :, cols], TXF[:, 0:4 * TXR].rearrange("p (k f) -> p k f", k=KD),
                                XTh[:, par_next, :, cols].bitcast(F32), ALU.subtract).then_inc(f_xl, 1)

            def lo_h(f, p):
                for h in range(2):
                    dve.wait_ge(f_hh, 2 * f + h + 1)
                    c = slice(h * HALF, (h + 1) * HALF)
                    v.scalar_tensor_tensor(htl[p][:, c], HB[h][:, 0:HALF], 0.0, hth[p][:, c].bitcast(F32),
                                           ALU.max, ALU.subtract).then_inc(f_hl, 1)

            for j in range(5):
                v.memset(bank[j][:, :], 0.0).then_inc(f_yz, 1)
            for st in range(NST):
                lo_xg(st, 0, slice(st * TXR, (st + 1) * TXR))
            lo_h(0, 0)

            def stage_f(e, g, ep, last):
                G = 4 * e + g
                for q in range(4):
                    if q % 2 == 0:
                        lo_xg(NST + 2 * G + q // 2, 1 - ep, bass.ds((2 * g + q // 2) * TXR, TXR))
                    lo_h(4 * G + q + 1, (q + 1) % 2)
                if last:
                    for j in range(5):
                        dve.wait_ge(f_ye, 5 * e + j + 1)
                        v.memset(bank[j][:, :], 0.0).then_inc(f_yz, 1)

            with dve.Fori(0, E // 2) as e2:
                for ep in range(2):
                    e = 2 * e2 + ep
                    with dve.Fori(0, 3) as g:
                        stage_f(e, g, ep, False)
                    stage_f(e, 3, ep, True)
            stage_ended(dve, end_f)

            for j in range(NT):
                n = j % 4
                dve.wait_ge(e_g[0][n], 16 * (NT // 4 + j // 4 + 1))
                if j >= 4:
                    dve.wait_ge(g_out[n], 16 * (j // 4))
                v.scalar_tensor_tensor(osb[n][:, :], y1g[n][:, :], wtok[:, 0, j:j + 1], x_rows[:, j, :],
                                       ALU.mult, ALU.add).then_inc(g_o, 1)
                dve.wait_ge(g_o, 2 * j + 1)
                dve.wait_ge(e_g[1][n], 16 * (NT // 4 + j // 4 + 1))
                v.scalar_tensor_tensor(osb[n][:, :], y2g[n][:, :], wtok[:, 1, j:j + 1], osb[n][:, :],
                                       ALU.mult, ALU.add).then_inc(g_o, 1)


def kernel(x, fside_BxSxS_0, cond_512, L0_cond_w, L0_cond_u, L0_ffn_router_scale, L0_ffn_gate_w,
           L0_ffn_gate_up, L0_ffn_down, L0_ffn_per_expert_scale, L1_cond_w, L1_cond_u, L1_ffn_Wg,
           L1_ffn_w1, L1_ffn_w2):
    import concourse.bacc as bacc
    from concourse.bass_utils import run_bass_kernel_spmd

    def cols(a):
        return np.asarray(a).reshape(KD, P).T

    def gates(a):
        return np.asarray(a).reshape(KD, P, E).transpose(1, 0, 2).reshape(P, KD * E)

    def blocks(a, k):
        a = np.asarray(a)
        return a.reshape(a.shape[0], k, P, a.shape[2]).transpose(0, 2, 1, 3).reshape(a.shape[0], P, -1)

    w1 = np.asarray(L1_ffn_w1).reshape(E, KD, P, NC1, HC).transpose(0, 3, 2, 1, 4).reshape(E * NC1, P, KD * HC)
    w2 = blocks(np.asarray(L1_ffn_w2).reshape(E * NC1, HC, D), HC // P)
    arrays = {
        "x": np.asarray(x).reshape(NT, P, D),
        "fs_t": np.asarray(fside_BxSxS_0).transpose(0, 2, 1).reshape(NQ, P, T),
        "params": np.concatenate([cols(L0_cond_w), cols(L0_cond_u), cols(L1_cond_w), cols(L1_cond_u),
                                  cols(L0_ffn_router_scale), gates(L0_ffn_gate_w), gates(L1_ffn_Wg)], axis=1),
        "rowpar": np.concatenate([np.asarray(cond_512).reshape(-1), np.asarray(L0_ffn_per_expert_scale)]),
        "gu": blocks(L0_ffn_gate_up, KD),
        "dn": blocks(L0_ffn_down, KD),
        "wc": np.concatenate([w1, w2], axis=2),
    }
    arrays = {n: np.ascontiguousarray(a) for n, a in arrays.items()}
    nc = bacc.Bacc("TRN2", target_bir_lowering=False, num_devices=1)
    args = [nc.dram_tensor(n, a.shape, mybir.dt.from_np(a.dtype), kind="ExternalInput").ap()
            for n, a in arrays.items()]
    out = nc.dram_tensor("out", (NT, P, D), F32, kind="ExternalOutput").ap()
    adaln_moe_kernel(nc, *args, out)
    r = run_bass_kernel_spmd(nc, [arrays], core_ids=[0])
    return r.results[0]["out"].reshape(B, T, D)
```

```python
from contextlib import ExitStack

import numpy as np

import concourse.bass as bass
from concourse import mybir

F32 = mybir.dt.float32
F32R = mybir.dt.float32r
BF16 = mybir.dt.bfloat16
I32 = mybir.dt.int32
U32 = mybir.dt.uint32
ALU = mybir.AluOpType
ACT = mybir.ActivationFunctionType
AX = mybir.AxisListType

P = 128
B, T, D = 4, 512, 512
S = B * T
NT = S // P
KD = D // P
TB = T // P
E = 8
NQ = B * KD
F0 = 512
F1 = 2048
CAP = 640
NG = 40
NTAB = NG + 4
ROWS = E * CAP
PADROWS = ROWS + CAP
HC = 256
NC1 = F1 // HC
PART = (512, CAP - 512)
LIM = (3 * P, 512)
TXR = 80
NST = CAP // TXR
NGRP = E * F1 // P // 4
ZW = PADROWS // P * D // (NQ - KD)
NZ = NQ - KD + 2
E30 = float(np.exp(np.float64(30.0)))
CLIP = 30.0
assert NG * P == ROWS and 2 * S // P + E - 1 <= NG


def static_wait(eng, sem, value):
    if isinstance(value, int) and value <= 0:
        return
    eng.wait_ge(sem, value)


def adaln_moe_kernel(nc, x, fs_t, params, rowpar, gu, dn, wc, out):
    ctx = ExitStack()
    with ctx:
        def sb(name, shape, dt):
            return ctx.enter_context(nc.sbuf_tensor(name, shape, dt))

        def sem(name):
            return ctx.enter_context(nc.semaphore(name))

        disp = nc.dram_tensor("disp", (PADROWS, D), F32, kind="Internal").ap()
        ybuf = [nc.dram_tensor(f"ybuf{l}", (ROWS + P, D), F32, kind="Internal").ap() for l in range(2)]
        ek_d = nc.dram_tensor("ek_d", (NQ, P, T), F32, kind="Internal").ap()
        eu_d = nc.dram_tensor("eu_d", (NQ, P, T), F32, kind="Internal").ap()
        ratio_d = nc.dram_tensor("ratio_d", (NQ, P, TB, P), F32, kind="Internal").ap()

        ident = sb("ident", [P, P], F32)
        tri = sb("tri", [P, P], BF16)
        ones = sb("ones", [P, P], BF16)
        iota_e = sb("iota_e", [P, E], F32)
        iota_m = sb("iota_m", [P, NT], F32)
        iota_t = sb("iota_t", [P, NTAB], F32)
        one8 = sb("one8", [P, E], F32)
        par = sb("par", [P, 5 * KD + 2 * KD * E], F32)
        rowp = sb("rowp", [P, B * P + E], F32)
        w_col = [par[:, 0:KD], par[:, 2 * KD:3 * KD]]
        u_col = [par[:, KD:2 * KD], par[:, 3 * KD:4 * KD]]
        rs_col = par[:, 4 * KD:5 * KD]
        gate = [par[:, 5 * KD + l * KD * E:5 * KD + (l + 1) * KD * E].rearrange("p (k e) -> p k e", k=KD)
                for l in range(2)]
        gate0s = sb("gate0s", [P, KD, E], F32)
        tsum = sb("tsum", [P, B], F32)
        tf = sb("tf", [P, B], F32)
        half = sb("half", [P, B], F32)
        gsc = sb("gsc", [P, B], F32)
        ew = sb("ew", [P, 2, KD], F32)
        dcy = sb("dcy", [P, 2, KD], F32)
        dec = sb("dec", [P, 2, B, KD], F32)
        ssq = sb("ssq", [P, NT], F32)
        rms = sb("rms", [P, NT], F32)
        rstd = sb("rstd", [P, NT], F32)
        lgs = sb("lgs", [P, NT, E], F32)
        mx = sb("mx", [P, NT], F32)
        ex = sb("ex", [P, NT, E], F32)
        sm = sb("sm", [P, NT], F32)
        rsm = sb("rsm", [P, NT], F32)
        prob = sb("prob", [P, NT, E], F32)
        top = sb("top", [P, NT, E], F32)
        tix = sb("tix", [P, NT, E], U32)
        tixf = sb("tixf", [P, NT, 2], F32)
        oh = sb("oh", [P, 2, NT, E], F32)
        msk = sb("msk", [P, NT, E], BF16)
        tmp8 = sb("tmp8", [P, 2, NT, E], F32)
        pos = sb("pos", [P, NT, E], F32)
        tot = sb("tot", [P, E], F32)
        cmp_m = sb("cmp_m", [P, E, NT], F32)
        ntile = sb("ntile", [P, E], F32)
        ends = sb("ends", [P, E], F32)
        base = sb("base", [P, E], F32)
        cmp_t = sb("cmp_t", [P, NTAB, E], F32)
        eidf = sb("eidf", [P, NTAB], F32)
        eidi = sb("eidi", [P, NTAB], I32)
        chgi = sb("chgi", [P, NTAB], I32)
        vali = sb("vali", [P, NTAB], I32)
        moref = sb("moref", [P, 2, E + 1], F32)
        more = sb("more", [P, 2, E + 1], I32)
        slotf = sb("slotf", [P, 2, NT], F32)
        kept = sb("kept", [P, 2, NT], F32)
        slot = [sb(f"slot{l}", [P, 2, NT], I32) for l in range(2)]
        wtok = sb("wtok", [P, 2, NT], F32)
        wsum = sb("wsum", [P, NT], F32)
        pesk = sb("pesk", [P, 2, NT], F32)
        tick = sb("tick", [P, 16], F32)

        arena0 = (nc.sbuf_base + 63) // 64 * 64
        used = [0]

        def at(kb, name, shape, dt):
            nbytes = int(np.prod(shape[1:])) * (2 if dt == BF16 else 4)
            off = int(kb * 1024)
            assert arena0 + off + nbytes <= nc.sbuf_usable_end, (name, off + nbytes, nc.sbuf_usable_end - arena0)
            return nc.alloc_sbuf_tensor_at(name, shape, dt, offset=arena0 + off)

        h_rows = at(0, "h_rows", [P, NT, D], F32)
        x_rows = at(32, "x_rows", [P, NT, D], F32)
        zero = at(64, "zero", [P, ZW], F32)
        a_at = 72
        cA = {}
        for n, deep in (("kT", 2), ("e1", 2), ("e20", 2), ("e21", 2), ("ek", 2), ("ekv", 2), ("nb", 2), ("db", 2),
                        ("dv", 2), ("rat", 2), ("nf", 4), ("df", 4), ("dd", 4), ("r0", 4)):
            cA[n] = at(a_at, "A_" + n, [P, deep, T], F32)
            a_at += 2 * deep
        hT = at(a_at, "hT", [P, 2, KD, P], F32)
        sqj = at(a_at + 4, "sqj", [P, D], F32)
        wgh = [at(16 * i, f"wgh{i}", [P, KD, 2 * F0], F32R) for i in range(2)]
        wgl = [at(32 + 16 * i, f"wgl{i}", [P, KD, 2 * F0], F32R) for i in range(2)]
        wdh = [at(64 + 8 * i, f"wdh{i}", [P, KD, D], F32R) for i in range(2)]
        wdl = [at(80 + 8 * i, f"wdl{i}", [P, KD, D], F32R) for i in range(2)]
        xr = [at(96 + 2 * i, f"xr{i}", [P, D], F32) for i in range(2)]
        xth = [at(100 + 2 * i, f"xth{i}", [P, KD, P], F32R) for i in range(2)]
        xtl = [at(104 + 2 * i, f"xtl{i}", [P, KD, P], F32R) for i in range(2)]
        ga = at(108, "ga", [P, F0], F32)
        ath = [at(112 + 2 * i, f"ath{i}", [P, KD, P], F32R) for i in range(2)]
        atl = [at(116 + 2 * i, f"atl{i}", [P, KD, P], F32R) for i in range(2)]
        yb = [at(120 + 2 * i, f"yb{i}", [P, D], F32) for i in range(2)]
        rgu = [at(124 + 16 * i, f"rgu{i}", [P, KD, 2 * F0], F32) for i in range(2)]
        rdn = [at(156 + 8 * i, f"rdn{i}", [P, KD, D], F32) for i in range(2)]
        cD = {n: at(172 + 2 * i, "D_" + n, [P, T], F32)
              for i, n in enumerate(("kT", "ek", "e21", "nf", "nb", "df", "db", "dd", "num", "inv", "rat"))}
        rtb = at(110, "rtb", [P, TB, P], F32)
        y1g = [at(64 + 2 * i, f"y1g{i}", [P, D], F32) for i in range(4)]
        y2g = [at(72 + 2 * i, f"y2g{i}", [P, D], F32) for i in range(4)]
        xin = [at(80 + 2 * i, f"xin{i}", [P, D], F32) for i in range(4)]
        rin = [at(88 + 2 * i, f"rin{i}", [P, D], F32) for i in range(4)]
        xpt = [at(96 + 2 * i, f"xpt{i}", [P, D], F32) for i in range(2)]
        sgx = [at(100 + 2 * i, f"sgx{i}", [P, D], F32) for i in range(2)]
        osb = [at(104 + 2 * i, f"osb{i}", [P, D], F32) for i in range(4)]
        XTh = at(64, "XTh", [P, 2, KD, CAP], F32R)
        XTl = at(84, "XTl", [P, 2, KD, CAP], F32R)
        hth = [at(112 + 2.5 * i, f"hth{i}", [P, CAP], F32R) for i in range(2)]
        htl = [at(117 + 2.5 * i, f"htl{i}", [P, CAP], F32R) for i in range(2)]
        xg = [at(124 + 2 * i, f"xg{i}", [TXR, D], F32) for i in range(2)]
        yo = [at(128 + 2 * i, f"yo{i}", [P, D], F32) for i in range(5)]
        wrw = [at(144 + 8 * i, f"wrw{i}", [P, 2048], F32) for i in range(2)]
        wch = [at(160 + 8 * i, f"wch{i}", [P, 2048], F32R) for i in range(2)]
        wcl = [at(176 + 8 * i, f"wcl{i}", [P, 2048], F32R) for i in range(2)]

        def w1c(w, p):
            return w[p][:, 0:KD * HC].rearrange("p (k f) -> p k f", k=KD)

        def w2c(w, p):
            return w[p][:, KD * HC:].rearrange("p (s d) -> p s d", s=2)

        bank = [ctx.enter_context(nc.psum_tensor(f"bank{i}", [P, 512], F32)) for i in range(8)]
        TR = [bank[0], bank[1]]
        HTB = [bank[2], bank[3]]
        LG, RK, TOT = bank[4], bank[5], bank[6]
        GP, UP, TX, TA, YD, TRD = bank[0], bank[1], bank[2], bank[3], bank[4], bank[5]
        HB, TXF = [bank[5], bank[6]], bank[7]

        def quad(bk):
            return bk[:, :].rearrange("p (k f) -> p k f", k=4)

        s_par = sem("params_in")
        s_x = sem("x_in")
        s_zero = sem("zero_made")
        s_zout = sem("zero_filled")
        s_const = sem("pool_constants")
        s_vset = sem("vector_setup_steps")
        s_aset = sem("scalar_setup_steps")
        s_sig = sem("sigmoid_x")
        s_kin = [sem(f"k_in{i}") for i in range(2)]
        s_e1, s_e20, s_e21 = sem("exp_k"), sem("exp_k_u0"), sem("exp_k_u1")
        s_eko = [sem(f"ek_stored{i}") for i in range(2)]
        s_euo = [sem(f"eu_stored{i}") for i in range(2)]
        s_ek, s_ekv = sem("ek_clipped"), sem("ekv_made")
        s_nf, s_nb, s_df, s_db = sem("num_forward"), sem("num_backward"), sem("den_forward"), sem("den_backward")
        s_dd, s_dv = sem("bonus_den"), sem("bonus_num")
        s_s1, s_s2, s_den = sem("num_sum"), sem("den_sum"), sem("den_made")
        s_dm, s_ln, s_r0, s_t, s_a = (sem(n) for n in ("den_bounded", "den_ln", "inverse", "den_inverse", "num_inverse"))
        c_dm, c_inv = sem("D_den_bounded"), sem("D_inverse")
        s_num, s_rat, s_tr = sem("num_made"), sem("ratio_made"), sem("ratio_turned")
        s_h = sem("h_part")
        s_ht, s_hte, s_lg = sem("h_turned"), sem("h_turned_copied"), sem("logits")
        s_sq = sem("h_squared")
        s_ms, s_rms = sem("mean_square"), sem("rms")
        s_vr = sem("vector_routing_steps")
        s_ex = sem("router_exp")
        s_lx = sem("router_shifted")
        s_mk = sem("expert_masks")
        s_rk = sem("ranks")
        s_slot = sem("slots_ready")
        s_sc = [sem(f"scattered{i}") for i in range(2)]
        d_xr = [sem(f"D_rows_in{i}") for i in range(2)]
        d_rgu = [sem(f"D_gate_up_in{i}") for i in range(2)]
        d_rdn = [sem(f"D_down_in{i}") for i in range(2)]
        d_hgu, d_lgu = sem("D_gate_up_hi"), sem("D_gate_up_lo")
        d_hdn, d_ldn = sem("D_down_hi"), sem("D_down_lo")
        d_tx, d_xh, d_xl = sem("D_rows_turned"), sem("D_xT_hi"), sem("D_xT_lo")
        d_gu, d_gelu, d_act = sem("D_gate_up_done"), sem("D_gelu"), sem("D_act")
        d_ta, d_ah, d_al = sem("D_act_turned"), sem("D_actT_hi"), sem("D_actT_lo")
        d_dn, d_ye = sem("D_down_done"), sem("D_y_copied")
        d_yo = [sem(f"D_y_stored{i}") for i in range(2)]
        c_in = sem("D_chunk_in")
        c_ekv, c_nf, c_nb, c_df, c_db = (sem("D_" + n) for n in ("ekv", "nf", "nb", "df", "db"))
        c_dd, c_dv, c_s1, c_s2, c_den = (sem("D_" + n) for n in ("dd", "dv", "s1", "s2", "den"))
        c_num, c_rat, c_tr, c_rt, c_out = (sem("D_" + n) for n in ("num", "rat", "tr", "rt", "ratio_stored"))
        s_yall = sem("layer0_rows_stored")
        e_g = [[sem(f"gathered{k}_{i}") for i in range(4)] for k in range(2)]
        e_x = [sem(f"E_x_in{i}") for i in range(4)]
        e_r = [sem(f"E_ratio_in{i}") for i in range(4)]
        e_p, e_x1, e_sg, e_h = sem("E_part"), sem("E_x1"), sem("E_sigmoid"), sem("E_h")
        g_o, g_out = sem("G_sum"), [sem(f"G_stored{i}") for i in range(4)]
        f_xg = [sem(f"F_rows_in{i}") for i in range(2)]
        f_w = [sem(f"F_weights_in{i}") for i in range(2)]
        f_wh1, f_wl1 = sem("F_w1_hi"), sem("F_w1_lo")
        f_wh2, f_wl2 = sem("F_w2_hi"), sem("F_w2_lo")
        f_tx, f_xh, f_xl = sem("F_rows_turned"), sem("F_XT_hi"), sem("F_XT_lo")
        f_h, f_hh, f_hl = sem("F_hidden"), sem("F_hidden_hi"), sem("F_hidden_lo")
        f_y, f_ye, f_yz = sem("F_y_part"), sem("F_y_copied"), sem("F_y_zeroed")
        f_yo = sem("F_y_stored")
        end_c = [sem(f"routing_ended{l}") for l in range(2)]
        end_d = sem("layer0_ended")
        end_f = sem("layer1_ended")

        def stage_ended(eng, s, of=5):
            eng.drain().then_inc(s, 1)
            eng.wait_ge(s, of)

        block = ctx.enter_context(nc.Block())

        @block.sync
        def _(sp):
            sp.dma_start(par[:, :], params).then_inc(s_par, 16)
            sp.dma_start(rowp[:, :], rowpar.partition_broadcast(P)).then_inc(s_par, 16)

            def load_k(b, ct):
                p, q = ct % 2, b * KD + ct
                static_wait(sp, s_dv, q - 1)
                static_wait(sp, s_e21, q - 1)
                sp.dma_start(cA["kT"][:, p, :], fs_t[q]).then_inc(s_kin[p], 16)

            def store_e(b, ct):
                p, q = ct % 2, b * KD + ct
                sp.wait_ge(s_ek, q + 1)
                sp.dma_start(ek_d[q], cA["ek"][:, p, :]).then_inc(s_eko[p], 16)
                sp.wait_ge(s_e21, q + 1)
                sp.dma_start(eu_d[q], cA["e21"][:, p, :]).then_inc(s_euo[p], 16)

            load_k(0, 0)
            load_k(0, 1)
            for b in range(B):
                sp.dma_start(x_rows[:, b * TB:(b + 1) * TB, :], x[b * TB:(b + 1) * TB].rearrange("j p d -> p j d"))\
                  .then_inc(s_x, 16)
            store_e(0, 0)
            load_k(0, 2)
            store_e(0, 1)
            load_k(0, 3)
            sp.wait_ge(s_zero, 1)
            for l in range(2):
                sp.dma_start(ybuf[l][ROWS:ROWS + P, :], zero[:, 0:D]).then_inc(s_zout, 16)
            flat = disp.rearrange("(p r) d -> p (r d)", p=P)

            def stage_a(b):
                for ct in range(KD):
                    load_k(b, ct)
                    store_e(b if ct >= 2 else b - 1, (ct + 2) % KD)
                    sp.dma_start(flat[:, bass.ds(((b - 1) * KD + ct) * ZW, ZW)], zero[:, 0:ZW]).then_inc(s_zout, 16)

            with sp.Fori(1, B) as b:
                stage_a(b)
            store_e(B - 1, 2)
            store_e(B - 1, 3)
            for p in range(2):
                sp.wait_ge(s_eko[p], 16 * NQ // 2)
                sp.wait_ge(s_euo[p], 16 * NQ // 2)
            sp.wait_ge(s_zout, 16 * NZ)
            stage_ended(sp, end_c[0])

            def load_gu(t, p):
                e = sp.value_load(eidi[0:1, bass.ds(t, 1)], min_val=0, max_val=E - 1)
                c = sp.value_load(chgi[0:1, bass.ds(t, 1)], min_val=0, max_val=1)
                static_wait(sp, d_lgu, t - 1)
                sp.dma_start(rgu[p][:, :, :].rearrange("p k f -> p (k f)"),
                             gu[bass.ds(e, 1)].rearrange("o p f -> (o p) f"), cond=c,
                             bounds_check="skip_entire_dma").then_inc(d_rgu[p], 16)

            def load_dn(t, p):
                e = sp.value_load(eidi[0:1, bass.ds(t, 1)], min_val=0, max_val=E - 1)
                c = sp.value_load(chgi[0:1, bass.ds(t, 1)], min_val=0, max_val=1)
                static_wait(sp, d_ldn, t - 1)
                sp.dma_start(rdn[p][:, :, :].rearrange("p k f -> p (k f)"),
                             dn[bass.ds(e, 1)].rearrange("o p f -> (o p) f"), cond=c,
                             bounds_check="skip_entire_dma").then_inc(d_rdn[p], 16)

            def load_rows(t, p):
                static_wait(sp, d_tx, t - 1)
                sp.dma_start(xr[p][:, :], disp[bass.ds(t * P, P), :]).then_inc(d_xr[p], 16)

            for p in range(2):
                load_rows(p, p)
                load_gu(p, p)
            load_dn(0, 0)
            for n, src in (("kT", fs_t), ("ek", ek_d), ("e21", eu_d)):
                sp.dma_start(cD[n][:, :], src[0]).then_inc(c_in, 16)
            load_dn(1, 1)
            load_rows(2, 0)
            load_gu(2, 0)
            load_gu(3, 1)
            load_dn(2, 0)

            def stage_d(i, more_chunks):
                for p in range(2):
                    load_rows(2 * i + p + 3, 1 - p)
                    if p == 1 and more_chunks:
                        sp.wait_ge(c_num, i + 1)
                        sp.wait_ge(c_db, i + 1)
                        for n, src in (("kT", fs_t), ("ek", ek_d), ("e21", eu_d)):
                            sp.dma_start(cD[n][:, :], src[i + 1]).then_inc(c_in, 16)
                    load_gu(2 * i + p + 4, p)
                    load_dn(2 * i + p + 3, 1 - p)

            with sp.Fori(0, NQ - 1) as i:
                stage_d(i, True)
            with sp.Fori(NQ - 1, NG // 2 - 1) as i:
                stage_d(i, False)
            for p in range(2):
                sp.wait_ge(d_rgu[p], 16 * (NG // 2 + 1))
                sp.wait_ge(d_rdn[p], 16 * (NG // 2 + 1 - p))
                sp.wait_ge(d_xr[p], 16 * (NG // 2 + 1 - p))
            stage_ended(sp, end_d)

            for j in range(NT):
                n = j % 4
                if j >= 4:
                    sp.wait_ge(e_p, j - 3)
                sp.dma_start(xin[n][:, :], x[j]).then_inc(e_x[n], 16)
                if j >= 4:
                    sp.wait_ge(e_h, j - 3)
                b0 = j // TB * KD
                sp.dma_start(rin[n][:, :].rearrange("p (c f) -> p c f", c=KD),
                             ratio_d[b0:b0 + KD, :, j % TB, :].rearrange("c p f -> p c f")).then_inc(e_r[n], 16)
            stage_ended(sp, end_c[1])

            def load_w(c, src, p):
                static_wait(sp, f_wl2, c - 1)
                sp.dma_start(wrw[p][:, :], wc[src]).then_inc(f_w[p], 16)

            def load_xg(st, p):
                static_wait(sp, f_tx, st - 1)
                sp.dma_start(xg[p][:, :], disp[bass.ds(st * TXR, TXR), :]).then_inc(f_xg[p], 16)

            load_w(0, 0, 0)
            load_xg(0, 0)
            load_xg(1, 1)
            load_w(1, 1, 1)
            for st in range(2, NST):
                load_xg(st, st % 2)

            def stage_f(G, last):
                for p in range(2):
                    load_xg(NST + 2 * G + p, p)
                for p in range(2):
                    load_w(2 * G + 2 + p, 2 * G + p if last else 2 * G + 2 + p, p)

            with sp.Fori(0, NGRP - 1) as G:
                stage_f(G, False)
            stage_f(NGRP - 1, True)
            for p in range(2):
                sp.wait_ge(f_xg[p], 16 * (NST // 2 + NGRP))
                sp.wait_ge(f_w[p], 16 * (1 + NGRP))
            stage_ended(sp, end_f)

            for j in range(NT):
                sp.wait_ge(g_o, 2 * (j + 1))
                sp.dma_start(out[j], osb[j % 4][:, :]).then_inc(g_out[j % 4], 16)
            for n in range(4):
                sp.wait_ge(g_out[n], 16 * NT // 4)

        @block.gpsimd
        def _(pl):
            g = nc.gpsimd
            g.memset(zero[:, :], 0.0).then_inc(s_zero, 1)
            g.memset(ident[:, :], 0.0).then_inc(s_const, 1)
            g.memset(tri[:, :], 1.0).then_inc(s_const, 1)
            g.memset(ones[:, :], 1.0).then_inc(s_const, 1)
            g.memset(one8[:, :], 1.0).then_inc(s_const, 1)
            g.memset(tick[:, :], 0.0).then_inc(s_const, 1)
            g.iota(vali[:, :], [[1, NTAB]], base=0, channel_multiplier=0).then_inc(s_const, 1)
            pl.wait_ge(s_const, 6)
            g.affine_select(out=ident[:, :], in_=ident[:, :], compare_op=ALU.not_equal, fill=1.0, base=0,
                            pattern=[[-1, P]], channel_multiplier=1).then_inc(s_const, 1)
            g.affine_select(out=tri[:, :], in_=tri[:, :], compare_op=ALU.is_gt, fill=0.0, base=0,
                            pattern=[[1, P]], channel_multiplier=-1).then_inc(s_const, 1)
            g.tensor_copy(iota_t[:, :], vali[:, :]).then_inc(s_const, 1)
            pl.wait_ge(s_const, 9)
            g.tensor_copy(iota_e[:, :], iota_t[:, 0:E]).then_inc(s_const, 1)
            g.tensor_scalar(iota_m[:, :], iota_t[:, 0:NT], float(P), None, ALU.mult).then_inc(s_const, 1)

            def carry_wait(c):
                g.tensor_tensor(tick[0:1, c:c + 1], tick[0:1, 0:1], tick[0:1, 0:1], ALU.add)

            def inverse_check(q, n):
                pl.wait_ge(s_r0, q + 1)
                g.tensor_tensor(cA["df"][:, n, :], cA["dd"][:, n, :], cA["r0"][:, n, :], ALU.mult).then_inc(s_t, 1)

            def stage_a(b, first):
                for ct in range(KD):
                    p, q = ct % 2, b * KD + ct
                    pl.wait_ge(s_dd, q + 1)
                    static_wait(pl, s_num, q - 1)
                    g.tensor_tensor(cA["dv"][:, p, :], cA["dd"][:, ct, :], cA["kT"][:, p, :], ALU.mult)\
                     .then_inc(s_dv, 1)
                    if not (first and ct < 2):
                        inverse_check(q - 2, (ct + 2) % 4)
                    pl.wait_ge(s_nb, q + 1)
                    g.tensor_tensor(cA["nf"][:, ct, :], cA["nf"][:, ct, :], cA["nb"][:, p, :], ALU.add)\
                     .then_inc(s_s1, 1)
                    pl.wait_ge(s_db, q + 1)
                    g.tensor_tensor(cA["df"][:, ct, :], cA["df"][:, ct, :], cA["db"][:, p, :], ALU.add)\
                     .then_inc(s_s2, 1)
                    pl.wait_ge(s_s2, q + 1)
                    g.tensor_tensor(cA["dd"][:, ct, :], cA["df"][:, ct, :], cA["dd"][:, ct, :], ALU.add)\
                     .then_inc(s_den, 1)

            stage_a(0, True)
            with pl.Fori(1, B) as b:
                stage_a(b, False)
            inverse_check(NQ - 2, 2)
            inverse_check(NQ - 1, 3)

            def scatter(l):
                pl.wait_ge(s_slot, l + 1)
                pl.wait_ge(s_zout, 16 * NZ)
                for k in range(2):
                    for j in range(NT):
                        g.indirect_dma_start(disp[0:ROWS, :], bass.IndirectOffsetOnAxis(slot[l][:, k, j:j + 1], 0),
                                             h_rows[:, j, :], None, bounds_check=ROWS - 1, oob_is_err=False)\
                         .then_inc(s_sc[l], 16)
                pl.wait_ge(s_sc[l], 16 * 2 * NT)
                stage_ended(pl, end_c[l])

            scatter(0)

            def lo_dn(t, p):
                c = pl.value_load(chgi[0:1, bass.ds(t, 1)], min_val=0, max_val=1)
                pl.wait_ge(d_hdn, t + 1)
                static_wait(pl, d_ldn, t)
                carry_wait(7)
                with pl.If(c):
                    g.tensor_tensor(wdl[p][:, :, :], rdn[p][:, :, :], wdh[p][:, :, :].bitcast(F32), ALU.subtract)
                g.tensor_copy(tick[0:1, 8:9], tick[0:1, 0:1]).then_inc(d_ldn, 1)

            lo_dn(0, 0)

            def stage_d(i, cond):
                if cond:
                    pl.wait_ge(c_dd, i + 1)
                    g.tensor_tensor(cD["e21"][:, :], cD["dd"][:, :], cD["kT"][:, :], ALU.mult).then_inc(c_dv, 1)
                    pl.wait_ge(c_nb, i + 1)
                    g.tensor_tensor(cD["nf"][:, :], cD["nf"][:, :], cD["nb"][:, :], ALU.add).then_inc(c_s1, 1)
                lo_dn(2 * i + 1, 1)
                if cond:
                    pl.wait_ge(c_db, i + 1)
                    g.tensor_tensor(cD["df"][:, :], cD["df"][:, :], cD["db"][:, :], ALU.add).then_inc(c_s2, 1)
                    pl.wait_ge(c_s2, i + 1)
                    g.tensor_tensor(cD["dd"][:, :], cD["df"][:, :], cD["dd"][:, :], ALU.add).then_inc(c_den, 1)
                lo_dn(2 * i + 2, 0)

            with pl.Fori(0, NQ) as i:
                stage_d(i, True)
            with pl.Fori(NQ, NG // 2) as i:
                stage_d(i, False)
            stage_ended(pl, end_d)

            def gather(l):
                for j in range(NT):
                    n = j % 4
                    for k, dst in ((0, y1g), (1, y2g)):
                        if l == 0 and j >= 4:
                            pl.wait_ge(e_p if k == 0 else e_x1, j - 3)
                        if l == 1 and j >= 4:
                            pl.wait_ge(g_o, 2 * (j - 4) + 1 + k)
                        g.indirect_dma_start(dst[n][:, :], None, ybuf[l][:, :],
                                             bass.IndirectOffsetOnAxis(slot[l][:, k, j:j + 1], 0),
                                             bounds_check=ROWS + P - 1, oob_is_err=False)\
                         .then_inc(e_g[k][n], 16)

            gather(0)
            scatter(1)

            def lo_w(part, wh_sem, wl_sem, c, p):
                pl.wait_ge(wh_sem, c + 1)
                g.tensor_tensor(part(wcl, p), part(wrw, p), part(wch, p).bitcast(F32), ALU.subtract)\
                 .then_inc(wl_sem, 1)

            lo_w(w1c, f_wh1, f_wl1, 0, 0)
            lo_w(w2c, f_wh2, f_wl2, 0, 0)
            lo_w(w1c, f_wh1, f_wl1, 1, 1)
            with pl.Fori(0, NGRP) as G:
                lo_w(w1c, f_wh1, f_wl1, 2 * G + 2, 0)
                lo_w(w2c, f_wh2, f_wl2, 2 * G + 1, 1)
                lo_w(w2c, f_wh2, f_wl2, 2 * G + 2, 0)
                lo_w(w1c, f_wh1, f_wl1, 2 * G + 3, 1)
            stage_ended(pl, end_f)
            gather(1)

        @block.scalar
        def _(act):
            s = nc.scalar
            act.wait_ge(s_vset, 1)
            s.activation(tf[:, :], tsum[:, :], ACT.Sigmoid).then_inc(s_aset, 1)
            act.wait_ge(s_par, 32)
            for l in range(2):
                s.activation(ew[:, l, :], w_col[l], ACT.Exp).then_inc(s_aset, 1)
            act.wait_ge(s_aset, 3)
            s.activation(dcy[:, :, :], ew[:, :, :], ACT.Exp, scale=-1.0).then_inc(s_aset, 1)

            def route_tile(l, j, n):
                p = n % 2
                act.wait_ge(s_ht, NT * l + j + 1)
                s.activation(hT[:, p, :, :], quad(HTB[p]), ACT.Copy).then_inc(s_hte, 1)
                if l == 0:
                    static_wait(act, s_sq, j)
                    s.activation(sqj[:, :], h_rows[:, j, :], ACT.Square, accum_out=ssq[:, bass.ds(j, 1)])\
                     .then_inc(s_sq, 1)

            def exps(b, ct):
                p, q = ct % 2, b * KD + ct
                act.wait_ge(s_kin[p], 16 * (2 * b + ct // 2 + 1))
                static_wait(act, s_ekv, q - 1)
                s.activation(cA["e1"][:, p, :], cA["kT"][:, p, :], ACT.Exp).then_inc(s_e1, 1)
                static_wait(act, s_dd, q - 1)
                s.activation(cA["e20"][:, p, :], cA["kT"][:, p, :], ACT.Exp,
                             bias=u_col[0][:, ct:ct + 1]).then_inc(s_e20, 1)
                static_wait(act, s_euo[p], 16 * (2 * b + ct // 2))
                s.activation(cA["e21"][:, p, :], cA["kT"][:, p, :], ACT.Exp,
                             bias=u_col[1][:, ct:ct + 1]).then_inc(s_e21, 1)

            def first_inverse(q, n):
                act.wait_ge(s_dm, q + 1)
                s.activation(cA["r0"][:, n, :], cA["dd"][:, n, :], ACT.Ln).then_inc(s_ln, 1)
                act.wait_ge(s_ln, q + 1)
                s.activation(cA["r0"][:, n, :], cA["r0"][:, n, :], ACT.Exp, scale=-1.0).then_inc(s_r0, 1)

            def stage_a(b):
                for ct in range(KD):
                    q = b * KD + ct
                    exps(b, ct)
                    if not isinstance(b, int) or q >= 2:
                        first_inverse(q - 2, (ct + 2) % 4)
                    if not isinstance(b, int) or q >= 7:
                        route_tile(0, q - 7, (ct + 1) % 2)
                    if isinstance(b, int) and q == 3:
                        act.wait_ge(s_x, 16 * B)
                        for c in range(4):
                            s.activation(x_rows[:, 4 * c:4 * c + 4, :], x_rows[:, 4 * c:4 * c + 4, :], ACT.Sigmoid)\
                             .then_inc(s_sig, 1)

            stage_a(0)
            stage_a(1)
            with act.Fori(2, B) as b:
                stage_a(b)
            first_inverse(NQ - 2, 2)
            first_inverse(NQ - 1, 3)
            for j in range(NQ - 7, NT):
                route_tile(0, j, j)

            def softmax(l):
                act.wait_ge(s_lx, l + 1)
                s.activation(ex[:, :, :], lgs[:, :, :], ACT.Exp).then_inc(s_ex, 1)
                stage_ended(act, end_c[l])

            act.wait_ge(s_ms, 1)
            s.activation(rms[:, :], rstd[:, :], ACT.Sqrt).then_inc(s_rms, 1)
            softmax(0)

            def hi_gu(t, p, n_in):
                c = act.value_load(chgi[0:1, bass.ds(t, 1)], min_val=0, max_val=1)
                act.wait_ge(d_rgu[p], 16 * n_in)
                static_wait(act, d_gu, t - 1)
                static_wait(act, d_hgu, t)
                s.activation(tick[0:1, 1:2], tick[0:1, 0:1], ACT.Copy)
                with act.If(c):
                    s.activation(wgh[p][:, :, :], rgu[p][:, :, :], ACT.Copy)
                s.activation(tick[0:1, 2:3], tick[0:1, 0:1], ACT.Copy).then_inc(d_hgu, 1)

            def hi_dn(t, p, n_in):
                c = act.value_load(chgi[0:1, bass.ds(t, 1)], min_val=0, max_val=1)
                act.wait_ge(d_rdn[p], 16 * n_in)
                static_wait(act, d_dn, t - 1)
                static_wait(act, d_hdn, t)
                s.activation(tick[0:1, 3:4], tick[0:1, 0:1], ACT.Copy)
                with act.If(c):
                    s.activation(wdh[p][:, :, :], rdn[p][:, :, :], ACT.Copy)
                s.activation(tick[0:1, 4:5], tick[0:1, 0:1], ACT.Copy).then_inc(d_hdn, 1)

            def hi_x(t, p):
                act.wait_ge(d_tx, t + 1)
                s.activation(xth[p][:, :, :], quad(TX), ACT.Copy).then_inc(d_xh, 1)

            hi_gu(0, 0, 1)
            hi_x(0, 0)
            hi_gu(1, 1, 1)
            hi_dn(0, 0, 1)

            def store_y(t, p):
                act.wait_ge(d_dn, t + 1)
                s.activation(yb[p][:, :], YD[:, :], ACT.Copy).then_inc(d_ye, 1)
                act.wait_ge(d_ye, t + 1)
                act.dma_start(ybuf[0][bass.ds(t * P, P), :], yb[p][:, :]).then_inc(d_yo[p], 16)

            def stage_d(i, first, turn):
                for p in range(2):
                    t = 2 * i + p
                    hi_x(t + 1, 1 - p)
                    act.wait_ge(d_gu, t + 1)
                    s.activation(ga[:, :], GP[:, :], ACT.Gelu).then_inc(d_gelu, 1)
                    hi_gu(t + 2, p, i + 2)
                    if not (first and p == 0):
                        store_y(t - 1, 1 - p)
                    static_wait(act, d_yo[p], 16 * i)
                    act.wait_ge(d_ta, t + 1)
                    s.activation(ath[p][:, :, :], quad(TA), ACT.Copy).then_inc(d_ah, 1)
                    if p == 0 and turn:
                        act.wait_ge(c_tr, i - 1)
                        s.activation(rtb[:, :, :], quad(TRD), ACT.Copy).then_inc(c_rt, 1)
                        act.wait_ge(c_rt, i - 1)
                        act.dma_start(ratio_d[i - 2], rtb[:, :, :]).then_inc(c_out, 16)
                    hi_dn(t + 1, 1 - p, i + 1 + p)
                    if p == 1 and turn:
                        act.wait_ge(c_out, 16 * (i - 1))

            stage_d(0, True, False)
            stage_d(1, False, False)
            with act.Fori(2, NQ + 2) as i:
                stage_d(i, False, True)
            with act.Fori(NQ + 2, NG // 2) as i:
                stage_d(i, False, False)
            store_y(NG - 1, 1)
            for p in range(2):
                act.wait_ge(d_yo[p], 16 * NG // 2)
            stage_ended(act, end_d)

            for j in range(NT):
                act.wait_ge(e_x1, j + 1)
                if j >= 2:
                    act.wait_ge(e_h, j - 1)
                s.activation(sgx[j % 2][:, :], x_rows[:, j, :], ACT.Sigmoid).then_inc(e_sg, 1)
                if j >= 1:
                    route_tile(1, j - 1, j - 1)
            route_tile(1, NT - 1, NT - 1)
            softmax(1)

            def hi_xg(st, par_next, cols):
                act.wait_ge(f_tx, st + 1)
                s.activation(XTh[:, par_next, :, cols], TXF[:, 0:4 * TXR].rearrange("p (k f) -> p k f", k=KD),
                             ACT.Copy).then_inc(f_xh, 1)

            def hi_w(part, wh_sem, c, p, n_in):
                act.wait_ge(f_w[p], 16 * n_in)
                s.activation(part(wch, p), part(wrw, p), ACT.Copy).then_inc(wh_sem, 1)

            def hi_h(f, p):
                act.wait_ge(f_h, f + 1)
                for h, at_ in enumerate((0, 512)):
                    s.activation(hth[p][:, at_:at_ + PART[h]], HB[h][:, 0:PART[h]], ACT.Relu).then_inc(f_hh, 1)

            hi_w(w1c, f_wh1, 0, 0, 1)
            for st in range(NST):
                hi_xg(st, 0, slice(st * TXR, (st + 1) * TXR))
            hi_w(w2c, f_wh2, 0, 0, 1)
            hi_w(w1c, f_wh1, 1, 1, 1)
            hi_h(0, 0)

            def stage_f(e, g, ep, last):
                G = 4 * e + g
                for q in range(4):
                    if q % 2 == 0:
                        hi_xg(NST + 2 * G + q // 2, 1 - ep, bass.ds((2 * g + q // 2) * TXR, TXR))
                    hi_h(4 * G + q + 1, (q + 1) % 2)
                    if q == 0:
                        hi_w(w1c, f_wh1, 2 * G + 2, 0, G + 2)
                        hi_w(w2c, f_wh2, 2 * G + 1, 1, G + 1)
                    if q == 2:
                        hi_w(w2c, f_wh2, 2 * G + 2, 0, G + 2)
                        hi_w(w1c, f_wh1, 2 * G + 3, 1, G + 2)
                if last:
                    act.wait_ge(f_y, 4 * G + 4)
                    for j in range(5):
                        if j == 0 and ep == 1:
                            act.wait_ge(f_yo, 80 * e)
                        s.activation(yo[j][:, :], bank[j][:, :], ACT.Copy).then_inc(f_ye, 1)
                    for j in range(5):
                        act.wait_ge(f_ye, 5 * e + j + 1)
                        act.dma_start(ybuf[1][bass.ds(e * CAP + j * P, P), :], yo[j][:, :]).then_inc(f_yo, 16)

            with act.Fori(0, E // 2) as e2:
                for ep in range(2):
                    e = 2 * e2 + ep
                    with act.Fori(0, 3) as g:
                        stage_f(e, g, ep, False)
                    stage_f(e, 3, ep, True)
                act.wait_ge(f_yo, 160 * (e2 + 1))
            stage_ended(act, end_f)

        @block.tensor
        def _(pe):
            m = nc.tensor

            def turn_rows(bank_, rows, np_=P, width=P):
                for k in range(KD):
                    last = m.transpose(bank_[:, k * width:(k + 1) * width], rows(k), ident[0:np_, 0:np_])
                return last

            def route_tile(l, j, n):
                p = n % 2
                static_wait(pe, s_hte, NT * l + j - 1)
                turn_rows(HTB[p], lambda k: h_rows[:, j, k * P:(k + 1) * P]).then_inc(s_ht, 1)
                pe.wait_ge(s_hte, NT * l + j + 1)
                w = gate0s if l == 0 else gate[1]
                for k in range(KD):
                    last = m.matmul(LG[:, bass.ds(j * E, E)], hT[:, p, k, :], w[:, k, :],
                                    start=(k == 0), stop=(k == KD - 1))
                last.then_inc(s_lg, 1)

            pe.wait_ge(s_const, 9)
            pe.wait_ge(s_vset, 15)

            for q in range(NQ + 7):
                if 2 <= q < NQ + 2:
                    pe.wait_ge(s_rat, q - 1)
                    static_wait(pe, s_h, q - 3)
                    turn_rows(TR[q % 2], lambda j: cA["rat"][:, q % 2, j * P:(j + 1) * P]).then_inc(s_tr, 1)
                if q >= 7:
                    pe.wait_ge(s_h, (q - 7) // TB * KD + KD)
                    route_tile(0, q - 7, q - 7)

            def ranks(l):
                pe.wait_ge(s_mk, l + 1)
                m.matmul(RK[:, 0:NT * E], tri[:, :], msk[:, :, :].rearrange("p j e -> p (j e)"),
                         start=True, stop=False, skip_group_check=True)
                for j in range(NT - 1):
                    m.matmul(RK[:, (j + 1) * E:NT * E].rearrange("p (j e) -> p j e", e=E), ones[:, :],
                             msk[:, j:j + 1, :].to_broadcast([P, NT - 1 - j, E]),
                             start=False, stop=(j == NT - 2), skip_group_check=True)
                for j in range(NT):
                    last = m.matmul(TOT[:, 0:E], ones[:, :], msk[:, j, :], start=(j == 0), stop=(j == NT - 1))
                last.then_inc(s_rk, 1)

            ranks(0)
            stage_ended(pe, end_c[0])

            def turn_x(t, p, n_in):
                pe.wait_ge(d_xr[p], 16 * n_in)
                static_wait(pe, d_xl, t)
                turn_rows(TX, lambda k: xr[p][:, k * P:(k + 1) * P]).then_inc(d_tx, 1)

            def products(p, a_hi, a_lo, w_hi, w_lo, accs, width):
                for k in range(KD):
                    for n, (a, w) in enumerate(((a_hi, w_hi), (a_hi, w_lo), (a_lo, w_hi))):
                        for h, acc in enumerate(accs):
                            yield (acc[:, :], a[p][:, k, :], w[p][:, k, h * width:(h + 1) * width],
                                   k == 0 and n == 0, k == KD - 1 and n == 2)

            def if_rows(t, terms, n_last, done):
                terms = list(terms)
                with pe.If(t):
                    for o, a, w, start, stop in terms[:-n_last]:
                        m.matmul(o, a, w, start=start, stop=stop, skip_group_check=True)
                for o, a, w, start, stop in terms[-n_last:]:
                    last = m.matmul(o, a, w, start=start, stop=stop, skip_group_check=True)
                last.then_inc(done, 1)

            def hidden(t, p):
                some = pe.value_load(vali[0:1, bass.ds(t, 1)], min_val=0, max_val=1)
                pe.wait_ge(d_xl, t + 1)
                pe.wait_ge(d_lgu, t + 1)
                if_rows(some, products(p, xth, xtl, wgh, wgl, (GP, UP), F0), 2, d_gu)

            def turn_act(t):
                pe.wait_ge(d_act, t + 1)
                turn_rows(TA, lambda k: ga[:, k * P:(k + 1) * P]).then_inc(d_ta, 1)

            def down(t, p):
                some = pe.value_load(vali[0:1, bass.ds(t, 1)], min_val=0, max_val=1)
                pe.wait_ge(d_al, t + 1)
                pe.wait_ge(d_ldn, t + 1)
                static_wait(pe, d_ye, t)
                if_rows(some, products(p, ath, atl, wdh, wdl, (YD,), D), 1, d_dn)

            turn_x(0, 0, 1)

            def stage_d(i, first, turn):
                for p in range(2):
                    t = 2 * i + p
                    turn_x(t + 1, 1 - p, i + 1 + p)
                    hidden(t, p)
                    if not (first and p == 0):
                        down(t - 1, 1 - p)
                    turn_act(t)
                    if p == 0 and turn:
                        pe.wait_ge(c_rat, i - 1)
                        turn_rows(TRD, lambda j: cD["rat"][:, j * P:(j + 1) * P]).then_inc(c_tr, 1)

            stage_d(0, True, False)
            stage_d(1, False, False)
            with pe.Fori(2, NQ + 2) as i:
                stage_d(i, False, True)
            with pe.Fori(NQ + 2, NG // 2) as i:
                stage_d(i, False, False)
            down(NG - 1, 1)
            stage_ended(pe, end_d)

            for j in range(NT):
                pe.wait_ge(e_h, j + 1)
                route_tile(1, j, j)
            ranks(1)
            stage_ended(pe, end_c[1])

            def turn_xg(st, p, n_in):
                pe.wait_ge(f_xg[p], 16 * n_in)
                static_wait(pe, f_xl, st)
                turn_rows(TXF, lambda k: xg[p][:, k * P:(k + 1) * P], TXR, TXR).then_inc(f_tx, 1)

            def hidden1(f, sub, wp, xp, fifth):
                static_wait(pe, f_hl, 2 * f)

                def part(h):
                    for k in range(KD):
                        for n, (w, a) in enumerate(((wch, XTh), (wch, XTl), (wcl, XTh))):
                            last = m.matmul(HB[h][:, 0:PART[h]], w1c(w, wp)[:, k, sub * P:(sub + 1) * P],
                                            a[:, xp, k, h * 512:h * 512 + PART[h]],
                                            start=(k == 0 and n == 0), stop=(k == KD - 1 and n == 2),
                                            skip_group_check=True)
                    return last

                with pe.If(fifth):
                    part(1)
                part(0).then_inc(f_h, 1)

            def y_part(f, sub, wp, hp, zeroed, fourth, fifth):
                pe.wait_ge(f_hl, 2 * f + 2)
                if zeroed is not None:
                    pe.wait_ge(f_yz, zeroed)

                def rows(j):
                    for n, (a, w) in enumerate(((hth, wch), (hth, wcl), (htl, wch))):
                        last = m.matmul(bank[j][:, :], a[hp][:, j * P:(j + 1) * P], w2c(w, wp)[:, sub, :],
                                        start=False, stop=False, skip_group_check=True)
                    return last

                with pe.If(fifth):
                    rows(4)
                with pe.If(fourth):
                    rows(3)
                for j in range(3):
                    last = rows(j)
                last.then_inc(f_y, 1)

            def row_counts(e):
                return [pe.value_load(more[0:1, n, bass.ds(e, 1)], min_val=0, max_val=1) for n in range(2)]

            for st in range(NST):
                turn_xg(st, st % 2, st // 2 + 1)
            pe.wait_ge(f_xl, NST)
            pe.wait_ge(f_wl1, 1)
            hidden1(0, 0, 0, 0, row_counts(0)[1])

            def stage_f(e, g, ep, last, now, after):
                G = 4 * e + g
                for q in range(4):
                    f = 4 * G + q
                    if q % 2 == 0:
                        turn_xg(NST + 2 * G + q // 2, q // 2, NST // 2 + G + 1)
                    if q == 1:
                        pe.wait_ge(f_wl1, 2 * G + 2)
                    if q == 3:
                        pe.wait_ge(f_wl1, 2 * G + 3)
                        if last:
                            pe.wait_ge(f_xl, NST * (e + 2))
                    ahead = last and q == 3
                    hidden1(f + 1, (q + 1) % 2, ((q + 1) // 2) % 2, 1 - ep if ahead else ep,
                            after[1] if ahead else now[1])
                    if q == 0:
                        pe.wait_ge(f_wl2, 2 * G + 1)
                    if q == 2:
                        pe.wait_ge(f_wl2, 2 * G + 2)
                    y_part(f, q % 2, q // 2, q % 2, 5 * e + 5 if q == 0 else None, *now)

            with pe.Fori(0, E // 2) as e2:
                for ep in range(2):
                    e = 2 * e2 + ep
                    now, after = row_counts(e), row_counts(e + 1)
                    with pe.Fori(0, 3) as g:
                        stage_f(e, g, ep, False, now, after)
                    stage_f(e, 3, ep, True, now, after)
            stage_ended(pe, end_f)

        @block.vector
        def _(dve):
            v = nc.vector

            dve.wait_ge(s_par, 32)
            v.tensor_reduce(tsum[:, :], rowp[:, 0:B * P].rearrange("p (b t) -> p b t", b=B), AX.X, ALU.add)\
             .then_inc(s_vset, 1)
            dve.wait_ge(s_aset, 1)
            v.tensor_scalar(half[:, :], tf[:, :], 0.5, 0.5, ALU.mult, ALU.add).then_inc(s_vset, 1)
            v.tensor_scalar(gsc[:, :], tf[:, :], -0.2, -0.8, ALU.mult, ALU.add).then_inc(s_vset, 1)
            dve.wait_ge(s_aset, 4)
            dve.wait_ge(s_vset, 3)
            for l in range(2):
                for b in range(B):
                    v.tensor_scalar(dec[:, l, b, :], dcy[:, l, :], half[:, b:b + 1], None, ALU.mult)\
                     .then_inc(s_vset, 1)
            for k in range(KD):
                v.tensor_scalar(gate0s[:, k, :], gate[0][:, k, :], rs_col[:, k:k + 1], float(D) ** -0.5,
                                ALU.mult, ALU.mult).then_inc(s_vset, 1)
            dve.wait_ge(s_vset, 15)

            def scan(dst, src, d, reverse):
                st = slice(None, None, -1) if reverse else slice(None)
                return v.tensor_tensor_scan(dst[:, st], d.to_broadcast([P, T]), src[:, st], 0.0,
                                            ALU.mult, ALU.add)

            def scans(b, ct):
                p, q = ct % 2, b * KD + ct
                d = dec[:, 0, :, :].rearrange("p b c -> p (b c)")[:, bass.ds(q, 1)]
                dve.wait_ge(s_e1, q + 1)
                static_wait(dve, s_eko[p], 16 * (2 * b + ct // 2))
                v.tensor_scalar(cA["ek"][:, p, :], cA["e1"][:, p, :], E30, None, ALU.min).then_inc(s_ek, 1)
                v.scalar_tensor_tensor(cA["ekv"][:, p, :], cA["e1"][:, p, :], E30, cA["kT"][:, p, :],
                                       ALU.min, ALU.mult).then_inc(s_ekv, 1)
                dve.wait_ge(s_ek, q + 1)
                dve.wait_ge(s_e20, q + 1)
                v.scalar_tensor_tensor(cA["dd"][:, ct, :], cA["e20"][:, p, :], E30, cA["ek"][:, p, :],
                                       ALU.min, ALU.subtract).then_inc(s_dd, 1)
                dve.wait_ge(s_ekv, q + 1)
                scan(cA["nf"][:, ct, :], cA["ekv"][:, p, :], d, False).then_inc(s_nf, 1)
                scan(cA["nb"][:, p, :], cA["ekv"][:, p, :], d, True).then_inc(s_nb, 1)
                scan(cA["df"][:, ct, :], cA["ek"][:, p, :], d, False).then_inc(s_df, 1)
                scan(cA["db"][:, p, :], cA["ek"][:, p, :], d, True).then_inc(s_db, 1)

            def num_den(q, ct):
                dve.wait_ge(s_s1, q + 1)
                v.tensor_tensor(cA["nf"][:, ct, :], cA["nf"][:, ct, :], cA["dv"][:, ct % 2, :], ALU.add)\
                 .then_inc(s_num, 1)
                dve.wait_ge(s_den, q + 1)
                v.tensor_scalar(cA["dd"][:, ct, :], cA["dd"][:, ct, :], 1e-8, None, ALU.max).then_inc(s_dm, 1)

            def ratio(q, ct):
                dve.wait_ge(s_r0, q + 1)
                dve.wait_ge(s_num, q + 1)
                v.tensor_tensor(cA["nf"][:, ct, :], cA["nf"][:, ct, :], cA["r0"][:, ct, :], ALU.mult).then_inc(s_a, 1)
                dve.wait_ge(s_a, q + 1)
                dve.wait_ge(s_t, q + 1)
                v.scalar_tensor_tensor(cA["rat"][:, ct % 2, :], cA["df"][:, ct, :], 2.0, cA["nf"][:, ct, :],
                                       ALU.subtract, ALU.mult).then_inc(s_rat, 1)

            def h_part(b, ct):
                q = b * KD + ct
                dve.wait_ge(s_tr, q + 1)
                rows = bass.ds(b * TB, TB)
                v.scalar_tensor_tensor(h_rows[:, rows, ct * P:(ct + 1) * P], x_rows[:, rows, ct * P:(ct + 1) * P],
                                       gsc[:, bass.ds(b, 1)], quad(TR[ct % 2]), ALU.mult, ALU.mult)\
                 .then_inc(s_h, 1)

            def stage_a(b, first):
                for ct in range(KD):
                    q = b * KD + ct
                    scans(b, ct)
                    if not (first and ct < 1):
                        num_den(q - 1, (ct + 3) % 4)
                    if not (first and ct < 2):
                        ratio(q - 2, (ct + 2) % 4)
                    if ct >= 3:
                        if first:
                            dve.wait_ge(s_sig, 4)
                        h_part(b, ct - 3)
                    elif not first:
                        h_part(b - 1, ct + 1)

            stage_a(0, True)
            with dve.Fori(1, B) as b:
                stage_a(b, False)
            num_den(NQ - 1, 3)
            ratio(NQ - 2, 2)
            h_part(B - 1, 1)
            ratio(NQ - 1, 3)
            h_part(B - 1, 2)
            h_part(B - 1, 3)

            steps = [0]

            def link(ins):
                steps[0] += 1
                ins.then_inc(s_vr, 1)
                dve.wait_ge(s_vr, steps[0])

            def over_e(a):
                return a.unsqueeze(2).to_broadcast([P, NT, E])

            def routing(l):
                dve.wait_ge(s_lg, NT * (l + 1))
                lg = LG[:, 0:NT * E].rearrange("p (j e) -> p j e", e=E)
                if l == 0:
                    dve.wait_ge(s_sq, NT)
                    v.tensor_scalar(rstd[:, :], ssq[:, :], 1.0 / D, 1e-6, ALU.mult, ALU.add).then_inc(s_ms, 1)
                    dve.wait_ge(s_rms, 1)
                    link(v.reciprocal(rstd[:, :], rms[:, :]))
                    link(v.tensor_tensor(lgs[:, :, :], lg, over_e(rstd[:, :]), ALU.mult))
                else:
                    link(v.tensor_copy(lgs[:, :, :], lg))
                link(v.tensor_reduce(mx[:, :], lgs[:, :, :], AX.X, ALU.max))
                v.tensor_tensor(lgs[:, :, :], lgs[:, :, :], over_e(mx[:, :]), ALU.subtract).then_inc(s_lx, 1)
                dve.wait_ge(s_ex, l + 1)
                link(v.tensor_reduce(sm[:, :], ex[:, :, :], AX.X, ALU.add))
                link(v.reciprocal(rsm[:, :], sm[:, :]))
                link(v.tensor_tensor(prob[:, :, :], ex[:, :, :], over_e(rsm[:, :]), ALU.mult))
                for j in range(NT):
                    last = v.max(top[:, j, :], prob[:, j, :])
                link(last)
                for j in range(NT):
                    last = v.max_index(tix[:, j, :], top[:, j, :], prob[:, j, :])
                link(last)
                link(v.tensor_copy(tixf[:, :, :], tix[:, :, 0:2]))
                for k in range(2):
                    last = v.tensor_tensor(oh[:, k, :, :], iota_e[:, :].unsqueeze(1).to_broadcast([P, NT, E]),
                                           over_e(tixf[:, :, k]), ALU.is_equal)
                link(last)
                v.tensor_tensor(msk[:, :, :], oh[:, 0, :, :], oh[:, 1, :, :], ALU.add).then_inc(s_mk, 1)
                dve.wait_ge(s_rk, l + 1)
                rank = RK[:, 0:NT * E].rearrange("p (j e) -> p j e", e=E)
                if l == 0:
                    link(v.tensor_copy(tot[:, :], TOT[:, 0:E]))
                    link(v.tensor_tensor(cmp_m[:, :, :], tot[:, :].unsqueeze(2).to_broadcast([P, E, NT]),
                                         iota_m[:, :].unsqueeze(1).to_broadcast([P, E, NT]), ALU.is_gt))
                    link(v.tensor_reduce(ntile[:, :], cmp_m[:, :, :], AX.X, ALU.add))
                    link(v.tensor_tensor_scan(ends[:, :], one8[:, :], ntile[:, :], 0.0, ALU.mult, ALU.add))
                    link(v.tensor_tensor(base[:, :], ends[:, :], ntile[:, :], ALU.subtract))
                    link(v.tensor_scalar(base[:, :], base[:, :], float(P), None, ALU.mult))
                    link(v.tensor_tensor(pos[:, :, :], rank, base[:, :].unsqueeze(1).to_broadcast([P, NT, E]), ALU.add))
                    link(v.tensor_tensor(cmp_t[:, :, :], ends[:, :].unsqueeze(1).to_broadcast([P, NTAB, E]),
                                         iota_t[:, :].unsqueeze(2).to_broadcast([P, NTAB, E]), ALU.is_le))
                    link(v.tensor_reduce(eidf[:, :], cmp_t[:, :, :], AX.X, ALU.add))
                    link(v.tensor_scalar(eidf[:, :], eidf[:, :], float(E - 1), None, ALU.min))
                    v.tensor_copy(eidi[:, :], eidf[:, :])
                    link(v.memset(chgi[:, :], 1))
                    v.tensor_tensor(chgi[:, 2:NG], eidf[:, 2:NG], eidf[:, 0:NG - 2], ALU.not_equal)
                    v.tensor_tensor(vali[:, :], iota_t[:, :], ends[:, E - 1:E].to_broadcast([P, NTAB]), ALU.is_lt)
                    link(v.memset(chgi[:, NG:NTAB], 0))
                else:
                    link(v.tensor_copy(pos[:, :, :], rank))
                    link(v.memset(moref[:, :, :], 0.0))
                    for n in range(2):
                        last = v.tensor_scalar(moref[:, n, 0:E], TOT[:, 0:E], float(LIM[n]), None, ALU.is_gt)
                    link(last)
                    link(v.tensor_copy(more[:, :, :], moref[:, :, :]))
                for k in range(2):
                    last = v.tensor_tensor(tmp8[:, k, :, :], oh[:, k, :, :], pos[:, :, :], ALU.mult)
                link(last)
                link(v.tensor_reduce(slotf[:, :, :], tmp8[:, :, :, :], AX.X, ALU.add))
                topk = top[:, :, 0:2].rearrange("p j k -> p k j")
                if l == 0:
                    link(v.tensor_tensor(wsum[:, :], top[:, :, 0], top[:, :, 1], ALU.add))
                    link(v.tensor_scalar(wsum[:, :], wsum[:, :], 1e-12, None, ALU.max))
                    link(v.reciprocal(wsum[:, :], wsum[:, :]))
                    pes = rowp[:, B * P:B * P + E].unsqueeze(1).to_broadcast([P, NT, E])
                    for k in range(2):
                        last = v.tensor_tensor(tmp8[:, k, :, :], oh[:, k, :, :], pes, ALU.mult)
                    link(last)
                    link(v.tensor_reduce(pesk[:, :, :], tmp8[:, :, :, :], AX.X, ALU.add))
                    for k in range(2):
                        last = v.tensor_tensor(wtok[:, k, :], top[:, :, k], wsum[:, :], ALU.mult)
                    link(last)
                    link(v.tensor_tensor(wtok[:, :, :], wtok[:, :, :], pesk[:, :, :], ALU.mult))
                else:
                    link(v.tensor_scalar(kept[:, :, :], slotf[:, :, :], float(CAP), None, ALU.is_lt))
                    for k in range(2):
                        last = v.scalar_tensor_tensor(slotf[:, k, :], tixf[:, :, k], float(CAP), slotf[:, k, :],
                                                      ALU.mult, ALU.add)
                    link(last)
                    link(v.scalar_tensor_tensor(slotf[:, :, :], slotf[:, :, :], float(ROWS), kept[:, :, :],
                                                ALU.subtract, ALU.mult))
                    link(v.tensor_scalar(slotf[:, :, :], slotf[:, :, :], float(ROWS), None, ALU.add))
                    for k in range(2):
                        last = v.tensor_tensor(wtok[:, k, :], top[:, :, k], kept[:, k, :], ALU.mult)
                    link(last)
                v.tensor_copy(slot[l][:, :, :], slotf[:, :, :]).then_inc(s_slot, 1)
                stage_ended(dve, end_c[l])

            routing(0)

            def lo_gu(t, p):
                c = dve.value_load(chgi[0:1, bass.ds(t, 1)], min_val=0, max_val=1)
                dve.wait_ge(d_hgu, t + 1)
                static_wait(dve, d_lgu, t)
                v.tensor_copy(tick[0:1, 5:6], tick[0:1, 0:1])
                with dve.If(c):
                    v.tensor_tensor(wgl[p][:, :, :], rgu[p][:, :, :], wgh[p][:, :, :].bitcast(F32), ALU.subtract)
                v.tensor_copy(tick[0:1, 6:7], tick[0:1, 0:1]).then_inc(d_lgu, 1)

            def lo_x(t, p):
                dve.wait_ge(d_xh, t + 1)
                v.tensor_tensor(xtl[p][:, :, :], quad(TX), xth[p][:, :, :].bitcast(F32), ALU.subtract)\
                 .then_inc(d_xl, 1)

            def scans_num(q):
                d = dec[:, 1, :, :].rearrange("p b c -> p (b c)")[:, bass.ds(q, 1)]
                dve.wait_ge(c_in, 48 * (q + 1))
                v.tensor_tensor(cD["df"][:, :], cD["ek"][:, :], cD["kT"][:, :], ALU.mult).then_inc(c_ekv, 1)
                static_wait(dve, c_dm, q)
                v.scalar_tensor_tensor(cD["dd"][:, :], cD["e21"][:, :], E30, cD["ek"][:, :],
                                       ALU.min, ALU.subtract).then_inc(c_dd, 1)
                static_wait(dve, c_num, q)
                dve.wait_ge(c_ekv, q + 1)
                scan(cD["nf"], cD["df"], d, False).then_inc(c_nf, 1)
                scan(cD["nb"], cD["df"], d, True).then_inc(c_nb, 1)

            def scans_den(q):
                d = dec[:, 1, :, :].rearrange("p b c -> p (b c)")[:, bass.ds(q, 1)]
                dve.wait_ge(c_nb, q + 1)
                scan(cD["df"], cD["ek"], d, False).then_inc(c_df, 1)
                scan(cD["db"], cD["ek"], d, True).then_inc(c_db, 1)

            def num(q):
                dve.wait_ge(c_s1, q + 1)
                static_wait(dve, c_rat, q)
                v.tensor_tensor(cD["num"][:, :], cD["nf"][:, :], cD["e21"][:, :], ALU.add).then_inc(c_num, 1)

            def bound(q):
                dve.wait_ge(c_den, q + 1)
                v.tensor_scalar(cD["inv"][:, :], cD["dd"][:, :], 1e-8, None, ALU.max).then_inc(c_dm, 1)

            def inverse(q):
                dve.wait_ge(c_dm, q + 1)
                v.reciprocal(cD["inv"][:, :], cD["inv"][:, :]).then_inc(c_inv, 1)

            def ratio1(q):
                dve.wait_ge(c_inv, q + 1)
                static_wait(dve, c_tr, q)
                v.scalar_tensor_tensor(cD["rat"][:, :], cD["num"][:, :], -1.0, cD["inv"][:, :],
                                       ALU.mult, ALU.mult).then_inc(c_rat, 1)

            lo_gu(0, 0)
            lo_x(0, 0)
            lo_gu(1, 1)

            def stage_d(i, cond, fin):
                for p in range(2):
                    t = 2 * i + p
                    lo_x(t + 1, 1 - p)
                    dve.wait_ge(d_gelu, t + 1)
                    v.tensor_tensor(ga[:, :], ga[:, :], UP[:, :], ALU.mult).then_inc(d_act, 1)
                    if p == 0 and fin:
                        bound(i - 1)
                        inverse(i - 1)
                    if p == 1 and cond:
                        scans_den(i)
                    if p == 1 and fin:
                        ratio1(i - 1)
                    if p == 1 and cond:
                        num(i)
                    dve.wait_ge(d_ah, t + 1)
                    v.tensor_tensor(atl[p][:, :, :], quad(TA), ath[p][:, :, :].bitcast(F32), ALU.subtract)\
                     .then_inc(d_al, 1)
                    lo_gu(t + 2, p)
                    if p == 0 and cond:
                        scans_num(i)

            stage_d(0, True, False)
            with dve.Fori(1, NQ) as i:
                stage_d(i, True, True)
            stage_d(NQ, False, True)
            with dve.Fori(NQ + 1, NG // 2) as i:
                stage_d(i, False, False)
            stage_ended(dve, end_d)

            def h1(j):
                dve.wait_ge(e_sg, j + 1)
                dve.wait_ge(e_r[j % 4], 16 * (j // 4 + 1))
                v.scalar_tensor_tensor(h_rows[:, j, :], sgx[j % 2][:, :], gsc[:, j // TB:j // TB + 1],
                                       rin[j % 4][:, :], ALU.mult, ALU.mult).then_inc(e_h, 1)

            for j in range(NT):
                n = j % 4
                dve.wait_ge(e_g[0][n], 16 * (j // 4 + 1))
                dve.wait_ge(e_x[n], 16 * (j // 4 + 1))
                v.scalar_tensor_tensor(xpt[j % 2][:, :], y1g[n][:, :], wtok[:, 0, j:j + 1], xin[n][:, :],
                                       ALU.mult, ALU.add).then_inc(e_p, 1)
                dve.wait_ge(e_p, j + 1)
                dve.wait_ge(e_g[1][n], 16 * (j // 4 + 1))
                v.scalar_tensor_tensor(x_rows[:, j, :], y2g[n][:, :], wtok[:, 1, j:j + 1], xpt[j % 2][:, :],
                                       ALU.mult, ALU.add).then_inc(e_x1, 1)
                if j >= 1:
                    h1(j - 1)
            h1(NT - 1)
            routing(1)

            def lo_xg(st, par_next, cols):
                dve.wait_ge(f_xh, st + 1)
                v.tensor_tensor(XTl[:, par_next, :, cols], TXF[:, 0:4 * TXR].rearrange("p (k f) -> p k f", k=KD),
                                XTh[:, par_next, :, cols].bitcast(F32), ALU.subtract).then_inc(f_xl, 1)

            def lo_h(f, p):
                for h, at_ in enumerate((0, 512)):
                    dve.wait_ge(f_hh, 2 * f + h + 1)
                    c = slice(at_, at_ + PART[h])
                    v.scalar_tensor_tensor(htl[p][:, c], HB[h][:, 0:PART[h]], 0.0, hth[p][:, c].bitcast(F32),
                                           ALU.max, ALU.subtract).then_inc(f_hl, 1)

            v.memset(HB[1][:, 0:PART[1]], 0.0)
            for j in range(5):
                v.memset(bank[j][:, :], 0.0).then_inc(f_yz, 1)
            for st in range(NST):
                lo_xg(st, 0, slice(st * TXR, (st + 1) * TXR))
            lo_h(0, 0)

            def stage_f(e, g, ep, last):
                G = 4 * e + g
                for q in range(4):
                    if q % 2 == 0:
                        lo_xg(NST + 2 * G + q // 2, 1 - ep, bass.ds((2 * g + q // 2) * TXR, TXR))
                    lo_h(4 * G + q + 1, (q + 1) % 2)
                if last:
                    for j in range(5):
                        dve.wait_ge(f_ye, 5 * e + j + 1)
                        v.memset(bank[j][:, :], 0.0).then_inc(f_yz, 1)

            with dve.Fori(0, E // 2) as e2:
                for ep in range(2):
                    e = 2 * e2 + ep
                    with dve.Fori(0, 3) as g:
                        stage_f(e, g, ep, False)
                    stage_f(e, 3, ep, True)
            stage_ended(dve, end_f)

            for j in range(NT):
                n = j % 4
                dve.wait_ge(e_g[0][n], 16 * (NT // 4 + j // 4 + 1))
                if j >= 4:
                    dve.wait_ge(g_out[n], 16 * (j // 4))
                v.scalar_tensor_tensor(osb[n][:, :], y1g[n][:, :], wtok[:, 0, j:j + 1], x_rows[:, j, :],
                                       ALU.mult, ALU.add).then_inc(g_o, 1)
                dve.wait_ge(g_o, 2 * j + 1)
                dve.wait_ge(e_g[1][n], 16 * (NT // 4 + j // 4 + 1))
                v.scalar_tensor_tensor(osb[n][:, :], y2g[n][:, :], wtok[:, 1, j:j + 1], osb[n][:, :],
                                       ALU.mult, ALU.add).then_inc(g_o, 1)


def kernel(x, fside_BxSxS_0, cond_512, L0_cond_w, L0_cond_u, L0_ffn_router_scale, L0_ffn_gate_w,
           L0_ffn_gate_up, L0_ffn_down, L0_ffn_per_expert_scale, L1_cond_w, L1_cond_u, L1_ffn_Wg,
           L1_ffn_w1, L1_ffn_w2):
    import concourse.bacc as bacc
    from concourse.bass_utils import run_bass_kernel_spmd

    def cols(a):
        return np.asarray(a).reshape(KD, P).T

    def gates(a):
        return np.asarray(a).reshape(KD, P, E).transpose(1, 0, 2).reshape(P, KD * E)

    def blocks(a, k):
        a = np.asarray(a)
        return a.reshape(a.shape[0], k, P, a.shape[2]).transpose(0, 2, 1, 3).reshape(a.shape[0], P, -1)

    w1 = np.asarray(L1_ffn_w1).reshape(E, KD, P, NC1, HC).transpose(0, 3, 2, 1, 4).reshape(E * NC1, P, KD * HC)
    w2 = blocks(np.asarray(L1_ffn_w2).reshape(E * NC1, HC, D), HC // P)
    arrays = {
        "x": np.asarray(x).reshape(NT, P, D),
        "fs_t": np.asarray(fside_BxSxS_0).transpose(0, 2, 1).reshape(NQ, P, T),
        "params": np.concatenate([cols(L0_cond_w), cols(L0_cond_u), cols(L1_cond_w), cols(L1_cond_u),
                                  cols(L0_ffn_router_scale), gates(L0_ffn_gate_w), gates(L1_ffn_Wg)], axis=1),
        "rowpar": np.concatenate([np.asarray(cond_512).reshape(-1), np.asarray(L0_ffn_per_expert_scale)]),
        "gu": blocks(L0_ffn_gate_up, KD),
        "dn": blocks(L0_ffn_down, KD),
        "wc": np.concatenate([w1, w2], axis=2),
    }
    arrays = {n: np.ascontiguousarray(a) for n, a in arrays.items()}
    nc = bacc.Bacc("TRN2", target_bir_lowering=False, num_devices=1)
    args = [nc.dram_tensor(n, a.shape, mybir.dt.from_np(a.dtype), kind="ExternalInput").ap()
            for n, a in arrays.items()]
    out = nc.dram_tensor("out", (NT, P, D), F32, kind="ExternalOutput").ap()
    adaln_moe_kernel(nc, *args, out)
    r = run_bass_kernel_spmd(nc, [arrays], core_ids=[0])
    return r.results[0]["out"].reshape(B, T, D)
```

```python
from contextlib import ExitStack

import numpy as np

import concourse.bass as bass
from concourse import mybir

F32 = mybir.dt.float32
F32R = mybir.dt.float32r
BF16 = mybir.dt.bfloat16
I32 = mybir.dt.int32
U32 = mybir.dt.uint32
ALU = mybir.AluOpType
ACT = mybir.ActivationFunctionType
AX = mybir.AxisListType

P = 128
B, T, D = 4, 512, 512
S = B * T
NT = S // P
KD = D // P
TB = T // P
E = 8
NQ = B * KD
F0 = 512
F1 = 2048
CAP = 640
NG = 40
NTAB = NG + 4
ROWS = E * CAP
PADROWS = ROWS + CAP
HC = 256
NC1 = F1 // HC
W3, W4, WB = 3 * P, 4 * P, CAP - 3 * P
PART = ((0, W4), (W4, WB))
LIM = (W3, W4)
TXR = 80
NST = CAP // TXR
NGRP = E * F1 // P // 4
ZW = PADROWS // P * D // (NQ - KD)
NZ = NQ - KD + 2
E30 = float(np.exp(np.float64(30.0)))
assert NG * P == ROWS and 2 * S // P + E - 1 <= NG


ROUTE_A, ROUTE_B = NT // 2 + 2, NT // 2 + 5
ROUTE = ((0, 0, NT), (1, 0, NT // 2), (1, NT // 2, NT))


def static_wait(eng, sem, value):
    if isinstance(value, int) and value <= 0:
        return
    eng.wait_ge(sem, value)


def adaln_moe_kernel(nc, x, fs_t, params, rowpar, gu, dn, wc, out):
    ctx = ExitStack()
    with ctx:
        def sb(name, shape, dt):
            return ctx.enter_context(nc.sbuf_tensor(name, shape, dt))

        def sem(name):
            return ctx.enter_context(nc.semaphore(name))

        disp = nc.dram_tensor("disp", (PADROWS, D), F32, kind="Internal").ap()
        ybuf = [nc.dram_tensor(f"ybuf{l}", (ROWS + P, D), F32, kind="Internal").ap() for l in range(2)]
        ek_d = nc.dram_tensor("ek_d", (NQ, P, T), F32, kind="Internal").ap()
        eu_d = nc.dram_tensor("eu_d", (NQ, P, T), F32, kind="Internal").ap()
        ratio_d = nc.dram_tensor("ratio_d", (NQ, P, TB, P), F32, kind="Internal").ap()

        ident = sb("ident", [P, P], F32)
        tri = sb("tri", [P, P], BF16)
        ones = sb("ones", [P, P], BF16)
        iota_e = sb("iota_e", [P, E], F32)
        iota_m = sb("iota_m", [P, NT], F32)
        iota_t = sb("iota_t", [P, NTAB], F32)
        one8 = sb("one8", [P, E], F32)
        par = sb("par", [P, 5 * KD + 2 * KD * E], F32)
        rowp = sb("rowp", [P, B * P + E], F32)
        w_col = [par[:, 0:KD], par[:, 2 * KD:3 * KD]]
        u_col = [par[:, KD:2 * KD], par[:, 3 * KD:4 * KD]]
        rs_col = par[:, 4 * KD:5 * KD]
        gate = [par[:, 5 * KD + l * KD * E:5 * KD + (l + 1) * KD * E].rearrange("p (k e) -> p k e", k=KD)
                for l in range(2)]
        gate0s = sb("gate0s", [P, KD, E], F32)
        tsum = sb("tsum", [P, B], F32)
        tf = sb("tf", [P, B], F32)
        half = sb("half", [P, B], F32)
        gsc = sb("gsc", [P, B], F32)
        ew = sb("ew", [P, 2, KD], F32)
        dcy = sb("dcy", [P, 2, KD], F32)
        dec = sb("dec", [P, 2, B, KD], F32)
        ssq = sb("ssq", [P, NT], F32)
        rms = sb("rms", [P, NT], F32)
        rstd = sb("rstd", [P, NT], F32)
        lgs = sb("lgs", [P, NT, E], F32)
        mx = sb("mx", [P, NT], F32)
        ex = sb("ex", [P, NT, E], F32)
        sm = sb("sm", [P, NT], F32)
        rsm = sb("rsm", [P, NT], F32)
        prob = sb("prob", [P, NT, E], F32)
        top = sb("top", [P, NT, E], F32)
        tix = sb("tix", [P, NT, E], U32)
        tixf = sb("tixf", [P, NT, 2], F32)
        oh = sb("oh", [P, 2, NT, E], F32)
        msk = sb("msk", [P, NT, E], BF16)
        tmp8 = sb("tmp8", [P, 2, NT, E], F32)
        pos = sb("pos", [P, NT, E], F32)
        tot = sb("tot", [P, E], F32)
        cmp_m = sb("cmp_m", [P, E, NT], F32)
        ntile = sb("ntile", [P, E], F32)
        ends = sb("ends", [P, E], F32)
        base = sb("base", [P, E], F32)
        cmp_t = sb("cmp_t", [P, NTAB, E], F32)
        eidf = sb("eidf", [P, NTAB], F32)
        eidi = sb("eidi", [P, NTAB], I32)
        chgi = sb("chgi", [P, NTAB], I32)
        vali = sb("vali", [P, NTAB], I32)
        moref = sb("moref", [P, 3, E + 1], F32)
        more = sb("more", [P, 3, E + 1], I32)
        slotf = sb("slotf", [P, 2, NT], F32)
        kept = sb("kept", [P, 2, NT], F32)
        slot = [sb(f"slot{l}", [P, 2, NT], I32) for l in range(2)]
        wtok = sb("wtok", [P, 2, NT], F32)
        wsum = sb("wsum", [P, NT], F32)
        pesk = sb("pesk", [P, 2, NT], F32)
        tick = sb("tick", [P, 16], F32)

        arena0 = (nc.sbuf_base + 63) // 64 * 64

        def at(kb, name, shape, dt):
            nbytes = int(np.prod(shape[1:])) * (2 if dt == BF16 else 4)
            off = int(kb * 1024)
            assert arena0 + off + nbytes <= nc.sbuf_usable_end, (name, off + nbytes, nc.sbuf_usable_end - arena0)
            return nc.alloc_sbuf_tensor_at(name, shape, dt, offset=arena0 + off)

        h_rows = at(0, "h_rows", [P, NT, D], F32)
        x_rows = at(32, "x_rows", [P, NT, D], F32)
        zero = at(64, "zero", [P, ZW], F32)
        a_at = 72
        cA = {}
        for n, deep in (("kT", 2), ("e1", 2), ("e20", 2), ("e21", 2), ("ek", 2), ("ekv", 2), ("nb", 2), ("db", 2),
                        ("dv", 2), ("rat", 2), ("nf", 4), ("df", 4), ("dd", 4), ("r0", 4)):
            cA[n] = at(a_at, "A_" + n, [P, deep, T], F32)
            a_at += 2 * deep
        hT = at(a_at, "hT", [P, 2, KD, P], F32)
        sqj = at(a_at + 4, "sqj", [P, D], F32)
        wgu = at(0, "wgu", [P, 4, KD, 2 * F0], F32R)
        wdn = at(64, "wdn", [P, 4, KD, D], F32R)

        def place_of(w, n):
            return w[:, bass.ds(n, 1), :, :].rearrange("p o k f -> p (o k) f")

        wplace = cmp_m[:, :, :].rearrange("p e j -> p (e j)")[:, 0:NTAB].bitcast(I32)
        xr = [at(96 + 2 * i, f"xr{i}", [P, D], F32) for i in range(2)]
        xth = [at(100 + 2 * i, f"xth{i}", [P, KD, P], F32R) for i in range(2)]
        xtl = [at(104 + 2 * i, f"xtl{i}", [P, KD, P], F32R) for i in range(2)]
        ga = at(108, "ga", [P, F0], F32)
        ath = [at(112 + 2 * i, f"ath{i}", [P, KD, P], F32R) for i in range(2)]
        atl = [at(116 + 2 * i, f"atl{i}", [P, KD, P], F32R) for i in range(2)]
        yb = [at(120 + 2 * i, f"yb{i}", [P, D], F32) for i in range(2)]
        rgu = [at(124 + 16 * i, f"rgu{i}", [P, KD, 2 * F0], F32) for i in range(2)]
        rdn = [at(156 + 8 * i, f"rdn{i}", [P, KD, D], F32) for i in range(2)]
        cD = {n: at(172 + 2 * i, "D_" + n, [P, T], F32)
              for i, n in enumerate(("kT", "ek", "e21", "nf", "nb", "df", "db", "dd", "num", "inv", "rat"))}
        rtb = at(110, "rtb", [P, TB, P], F32)
        y1g = [at(64 + 2 * i, f"y1g{i}", [P, D], F32) for i in range(4)]
        y2g = [at(72 + 2 * i, f"y2g{i}", [P, D], F32) for i in range(4)]
        xin = [at(80 + 2 * i, f"xin{i}", [P, D], F32) for i in range(4)]
        rin = [at(88 + 2 * i, f"rin{i}", [P, D], F32) for i in range(4)]
        xpt = [at(96 + 2 * i, f"xpt{i}", [P, D], F32) for i in range(2)]
        sgx = [at(100 + 2 * i, f"sgx{i}", [P, D], F32) for i in range(2)]
        osb = [at(104 + 2 * i, f"osb{i}", [P, D], F32) for i in range(4)]
        XTh = at(64, "XTh", [P, 2, KD, CAP], F32R)
        XTl = at(84, "XTl", [P, 2, KD, CAP], F32R)
        hth = [at(112 + 3 * i, f"hth{i}", [P, W4 + WB], F32R) for i in range(2)]
        htl = [at(118 + 3 * i, f"htl{i}", [P, W4 + WB], F32R) for i in range(2)]
        xg = [at(124 + 2 * i, f"xg{i}", [TXR, D], F32) for i in range(2)]
        yo = [at(128 + 2 * i, f"yo{i}", [P, D], F32) for i in range(5)]
        wrw = [at(144 + 8 * i, f"wrw{i}", [P, 2048], F32) for i in range(2)]
        wch = [at(160 + 8 * i, f"wch{i}", [P, 2048], F32R) for i in range(2)]
        wcl = [at(176 + 8 * i, f"wcl{i}", [P, 2048], F32R) for i in range(2)]

        def w1c(w, p):
            return w[p][:, 0:KD * HC].rearrange("p (k f) -> p k f", k=KD)

        def w2c(w, p):
            return w[p][:, KD * HC:].rearrange("p (s d) -> p s d", s=2)

        bank = [ctx.enter_context(nc.psum_tensor(f"bank{i}", [P, 512], F32)) for i in range(8)]
        TR = [bank[0], bank[1]]
        HTB = [bank[2], bank[3]]
        LGS, RK, TOT = [bank[4], bank[4], bank[7]], bank[5], bank[6]
        GP, UP, TX, TA, YD, TRD = bank[0], bank[1], bank[2], bank[3], bank[4], bank[5]
        HB, TXF = [bank[5], bank[6]], bank[7]
        TXS = [bank[7], bank[6]]

        def quad(bk):
            return bk[:, :].rearrange("p (k f) -> p k f", k=4)

        s_par = sem("params_in")
        s_x = sem("x_in")
        s_zero = sem("zero_made")
        s_zout = sem("zero_filled")
        s_const = sem("pool_constants")
        s_vset = sem("vector_setup_steps")
        s_aset = sem("scalar_setup_steps")
        s_sig = sem("sigmoid_x")
        s_kin = [sem(f"k_in{i}") for i in range(2)]
        s_e1, s_e20, s_e21 = sem("exp_k"), sem("exp_k_u0"), sem("exp_k_u1")
        s_eko = [sem(f"ek_stored{i}") for i in range(2)]
        s_euo = [sem(f"eu_stored{i}") for i in range(2)]
        s_ek, s_ekv = sem("ek_clipped"), sem("ekv_made")
        s_nf, s_nb, s_df, s_db = sem("num_forward"), sem("num_backward"), sem("den_forward"), sem("den_backward")
        s_dd, s_dv = sem("bonus_den"), sem("bonus_num")
        s_s1, s_s2, s_den = sem("num_sum"), sem("den_sum"), sem("den_made")
        s_dm, s_ln, s_r0, s_t, s_a = (sem(n) for n in ("den_bounded", "den_ln", "inverse", "den_inverse", "num_inverse"))
        c_dm, c_inv = sem("D_den_bounded"), sem("D_inverse")
        s_num, s_rat, s_tr = sem("num_made"), sem("ratio_made"), sem("ratio_turned")
        s_h = sem("h_part")
        s_ht, s_hte, s_lg = sem("h_turned"), sem("h_turned_copied"), sem("logits")
        s_sq = sem("h_squared")
        s_ms, s_rms = sem("mean_square"), sem("rms")
        s_vr = sem("vector_routing_steps")
        s_ex = sem("router_exp")
        s_lx = sem("router_shifted")
        s_mk = sem("expert_masks")
        s_rk = sem("ranks")
        s_slot = sem("slots_ready")
        s_sc = [sem(f"scattered{i}") for i in range(2)]
        d_xr = [sem(f"D_rows_in{i}") for i in range(2)]
        d_rgu = [sem(f"D_gate_up_in{i}") for i in range(2)]
        d_rdn = [sem(f"D_down_in{i}") for i in range(2)]
        d_hgu, d_lgu = sem("D_gate_up_hi"), sem("D_gate_up_lo")
        d_hdn, d_ldn = sem("D_down_hi"), sem("D_down_lo")
        d_tx, d_xh, d_xl = sem("D_rows_turned"), sem("D_xT_hi"), sem("D_xT_lo")
        d_gu, d_gelu, d_act = sem("D_gate_up_done"), sem("D_gelu"), sem("D_act")
        d_ta, d_ah, d_al = sem("D_act_turned"), sem("D_actT_hi"), sem("D_actT_lo")
        d_dn, d_ye = sem("D_down_done"), sem("D_y_copied")
        d_yo = [sem(f"D_y_stored{i}") for i in range(2)]
        c_in = sem("D_chunk_in")
        c_ekv, c_nf, c_nb, c_df, c_db = (sem("D_" + n) for n in ("ekv", "nf", "nb", "df", "db"))
        c_dd, c_dv, c_s1, c_s2, c_den = (sem("D_" + n) for n in ("dd", "dv", "s1", "s2", "den"))
        c_num, c_rat, c_tr, c_rt, c_out = (sem("D_" + n) for n in ("num", "rat", "tr", "rt", "ratio_stored"))
        e_g = [[sem(f"gathered{k}_{i}") for i in range(4)] for k in range(2)]
        e_x = [sem(f"E_x_in{i}") for i in range(4)]
        e_r = [sem(f"E_ratio_in{i}") for i in range(4)]
        e_p, e_x1, e_sg, e_h = sem("E_part"), sem("E_x1"), sem("E_sigmoid"), sem("E_h")
        g_o, g_out = sem("G_sum"), [sem(f"G_stored{i}") for i in range(4)]
        f_xg = [sem(f"F_rows_in{i}") for i in range(2)]
        f_w = [sem(f"F_weights_in{i}") for i in range(2)]
        f_wh1, f_wl1 = sem("F_w1_hi"), sem("F_w1_lo")
        f_wh2, f_wl2 = sem("F_w2_hi"), sem("F_w2_lo")
        f_tx, f_xh, f_xl = sem("F_rows_turned"), sem("F_XT_hi"), sem("F_XT_lo")
        f_h, f_hh, f_hl = sem("F_hidden"), sem("F_hidden_hi"), sem("F_hidden_lo")
        f_y, f_ye, f_yz = sem("F_y_part"), sem("F_y_copied"), sem("F_y_zeroed")
        f_yo = sem("F_y_stored")
        end_c = [sem(f"routing_ended{l}") for l in range(2)]
        end_d = sem("layer0_ended")
        end_f = sem("layer1_ended")

        def stage_ended(eng, s, of=5):
            eng.drain().then_inc(s, 1)
            eng.wait_ge(s, of)

        block = ctx.enter_context(nc.Block())

        @block.sync
        def _(sp):
            sp.dma_start(par[:, :], params).then_inc(s_par, 16)
            sp.dma_start(rowp[:, :], rowpar.partition_broadcast(P)).then_inc(s_par, 16)

            def load_k(b, ct):
                p, q = ct % 2, b * KD + ct
                static_wait(sp, s_dv, q - 1)
                static_wait(sp, s_e21, q - 1)
                sp.dma_start(cA["kT"][:, p, :], fs_t[q]).then_inc(s_kin[p], 16)

            def store_e(b, ct):
                p, q = ct % 2, b * KD + ct
                sp.wait_ge(s_ek, q + 1)
                sp.dma_start(ek_d[q], cA["ek"][:, p, :]).then_inc(s_eko[p], 16)
                sp.wait_ge(s_e21, q + 1)
                sp.dma_start(eu_d[q], cA["e21"][:, p, :]).then_inc(s_euo[p], 16)

            def load_x(b):
                sp.dma_start(x_rows[:, b * TB:(b + 1) * TB, :], x[b * TB:(b + 1) * TB].rearrange("j p d -> p j d"))\
                  .then_inc(s_x, 16)

            load_k(0, 0)
            load_k(0, 1)
            load_x(0)
            store_e(0, 0)
            load_k(0, 2)
            load_x(1)
            store_e(0, 1)
            load_k(0, 3)
            load_x(2)
            load_x(3)
            sp.wait_ge(s_zero, 1)
            for l in range(2):
                sp.dma_start(ybuf[l][ROWS:ROWS + P, :], zero[:, 0:D]).then_inc(s_zout, 16)
            flat = disp.rearrange("(p r) d -> p (r d)", p=P)

            def stage_a(b):
                for ct in range(KD):
                    load_k(b, ct)
                    store_e(b if ct >= 2 else b - 1, (ct + 2) % KD)
                    sp.dma_start(flat[:, bass.ds(((b - 1) * KD + ct) * ZW, ZW)], zero[:, 0:ZW]).then_inc(s_zout, 16)

            with sp.Fori(1, B) as b:
                stage_a(b)
            store_e(B - 1, 2)
            store_e(B - 1, 3)
            for p in range(2):
                sp.wait_ge(s_eko[p], 16 * NQ // 2)
                sp.wait_ge(s_euo[p], 16 * NQ // 2)
            sp.wait_ge(s_zout, 16 * NZ)
            stage_ended(sp, end_c[0])

            def load_gu(t, p):
                e = sp.value_load(eidi[0:1, bass.ds(t, 1)], min_val=0, max_val=E - 1)
                c = sp.value_load(chgi[0:1, bass.ds(t, 1)], min_val=0, max_val=1)
                static_wait(sp, d_lgu, t - 1)
                sp.dma_start(rgu[p][:, :, :].rearrange("p k f -> p (k f)"),
                             gu[bass.ds(e, 1)].rearrange("o p f -> (o p) f"), cond=c,
                             bounds_check="skip_entire_dma").then_inc(d_rgu[p], 16)

            def load_dn(t, p):
                e = sp.value_load(eidi[0:1, bass.ds(t, 1)], min_val=0, max_val=E - 1)
                c = sp.value_load(chgi[0:1, bass.ds(t, 1)], min_val=0, max_val=1)
                static_wait(sp, d_ldn, t - 1)
                sp.dma_start(rdn[p][:, :, :].rearrange("p k f -> p (k f)"),
                             dn[bass.ds(e, 1)].rearrange("o p f -> (o p) f"), cond=c,
                             bounds_check="skip_entire_dma").then_inc(d_rdn[p], 16)

            def load_rows(t, p):
                static_wait(sp, d_tx, t - 1)
                sp.dma_start(xr[p][:, :], disp[bass.ds(t * P, P), :]).then_inc(d_xr[p], 16)

            load_gu(0, 0)
            load_dn(0, 0)
            load_gu(1, 1)
            load_dn(1, 1)
            for n, src in (("kT", fs_t), ("ek", ek_d), ("e21", eu_d)):
                sp.dma_start(cD[n][:, :], src[0]).then_inc(c_in, 16)
            load_gu(2, 0)
            sp.wait_ge(s_sc[0], 16 * 2 * NT)
            load_rows(0, 0)
            load_rows(1, 1)
            load_rows(2, 0)
            load_gu(3, 1)
            load_dn(2, 0)

            def stage_d(i, more_chunks):
                for p in range(2):
                    load_rows(2 * i + p + 3, 1 - p)
                    if p == 1 and more_chunks:
                        sp.wait_ge(c_num, i + 1)
                        sp.wait_ge(c_db, i + 1)
                        for n, src in (("kT", fs_t), ("ek", ek_d), ("e21", eu_d)):
                            sp.dma_start(cD[n][:, :], src[i + 1]).then_inc(c_in, 16)
                    load_gu(2 * i + p + 4, p)
                    load_dn(2 * i + p + 3, 1 - p)

            with sp.Fori(0, NQ - 1) as i:
                stage_d(i, True)
            with sp.Fori(NQ - 1, NG // 2 - 1) as i:
                stage_d(i, False)
            for p in range(2):
                sp.wait_ge(d_rgu[p], 16 * (NG // 2 + 1))
                sp.wait_ge(d_rdn[p], 16 * (NG // 2 + 1 - p))
                sp.wait_ge(d_xr[p], 16 * (NG // 2 + 1 - p))
            stage_ended(sp, end_d)

            for j in range(NT):
                n = j % 4
                if j >= 4:
                    sp.wait_ge(e_p, j - 3)
                sp.dma_start(xin[n][:, :], x[j]).then_inc(e_x[n], 16)
                if j >= 4:
                    sp.wait_ge(e_h, j - 3)
                b0 = j // TB * KD
                sp.dma_start(rin[n][:, :].rearrange("p (c f) -> p c f", c=KD),
                             ratio_d[b0:b0 + KD, :, j % TB, :].rearrange("c p f -> p c f")).then_inc(e_r[n], 16)
            stage_ended(sp, end_c[1])

            def load_w(c, src, p):
                static_wait(sp, f_wl2, c - 1)
                sp.dma_start(wrw[p][:, :], wc[src]).then_inc(f_w[p], 16)

            def load_xg(st, p):
                static_wait(sp, f_tx, st - 1)
                sp.dma_start(xg[p][:, :], disp[bass.ds(st * TXR, TXR), :]).then_inc(f_xg[p], 16)

            load_w(0, 0, 0)
            load_xg(0, 0)
            load_xg(1, 1)
            load_w(1, 1, 1)
            for st in range(2, NST):
                load_xg(st, st % 2)

            def stage_f(G, last):
                for p in range(2):
                    load_xg(NST + 2 * G + p, p)
                for p in range(2):
                    load_w(2 * G + 2 + p, 2 * G + p if last else 2 * G + 2 + p, p)

            with sp.Fori(0, NGRP - 1) as G:
                stage_f(G, False)
            stage_f(NGRP - 1, True)
            for p in range(2):
                sp.wait_ge(f_xg[p], 16 * (NST // 2 + NGRP))
                sp.wait_ge(f_w[p], 16 * (1 + NGRP))
            stage_ended(sp, end_f)

            for j in range(NT):
                sp.wait_ge(g_o, 2 * (j + 1))
                sp.dma_start(out[j], osb[j % 4][:, :]).then_inc(g_out[j % 4], 16)
            for n in range(4):
                sp.wait_ge(g_out[n], 16 * NT // 4)

        @block.gpsimd
        def _(pl):
            g = nc.gpsimd
            g.memset(zero[:, :], 0.0).then_inc(s_zero, 1)
            g.memset(ident[:, :], 0.0).then_inc(s_const, 1)
            g.memset(tri[:, :], 1.0).then_inc(s_const, 1)
            g.memset(ones[:, :], 1.0).then_inc(s_const, 1)
            g.memset(one8[:, :], 1.0).then_inc(s_const, 1)
            g.memset(tick[:, :], 0.0).then_inc(s_const, 1)
            g.iota(vali[:, :], [[1, NTAB]], base=0, channel_multiplier=0).then_inc(s_const, 1)
            pl.wait_ge(s_const, 6)
            g.affine_select(out=ident[:, :], in_=ident[:, :], compare_op=ALU.not_equal, fill=1.0, base=0,
                            pattern=[[-1, P]], channel_multiplier=1).then_inc(s_const, 1)
            g.affine_select(out=tri[:, :], in_=tri[:, :], compare_op=ALU.is_gt, fill=0.0, base=0,
                            pattern=[[1, P]], channel_multiplier=-1).then_inc(s_const, 1)
            g.tensor_copy(iota_t[:, :], vali[:, :]).then_inc(s_const, 1)
            pl.wait_ge(s_const, 9)
            g.tensor_copy(iota_e[:, :], iota_t[:, 0:E]).then_inc(s_const, 1)
            g.tensor_scalar(iota_m[:, :], iota_t[:, 0:NT], float(P), None, ALU.mult).then_inc(s_const, 1)

            def carry_wait(c):
                g.tensor_tensor(tick[0:1, c:c + 1], tick[0:1, 0:1], tick[0:1, 0:1], ALU.add)

            def inverse_check(q, n):
                pl.wait_ge(s_r0, q + 1)
                g.tensor_tensor(cA["df"][:, n, :], cA["dd"][:, n, :], cA["r0"][:, n, :], ALU.mult).then_inc(s_t, 1)

            def stage_a(b, first):
                for ct in range(KD):
                    p, q = ct % 2, b * KD + ct
                    pl.wait_ge(s_dd, q + 1)
                    static_wait(pl, s_num, q - 1)
                    g.tensor_tensor(cA["dv"][:, p, :], cA["dd"][:, ct, :], cA["kT"][:, p, :], ALU.mult)\
                     .then_inc(s_dv, 1)
                    if not (first and ct < 2):
                        inverse_check(q - 2, (ct + 2) % 4)
                    pl.wait_ge(s_nb, q + 1)
                    g.tensor_tensor(cA["nf"][:, ct, :], cA["nf"][:, ct, :], cA["nb"][:, p, :], ALU.add)\
                     .then_inc(s_s1, 1)
                    pl.wait_ge(s_db, q + 1)
                    g.tensor_tensor(cA["df"][:, ct, :], cA["df"][:, ct, :], cA["db"][:, p, :], ALU.add)\
                     .then_inc(s_s2, 1)
                    pl.wait_ge(s_s2, q + 1)
                    g.tensor_tensor(cA["dd"][:, ct, :], cA["df"][:, ct, :], cA["dd"][:, ct, :], ALU.add)\
                     .then_inc(s_den, 1)

            stage_a(0, True)
            with pl.Fori(1, B) as b:
                stage_a(b, False)
            inverse_check(NQ - 2, 2)
            inverse_check(NQ - 1, 3)

            def scatter(n):
                l, j0, j1 = ROUTE[n]
                pl.wait_ge(s_slot, n + 1)
                pl.wait_ge(s_zout, 16 * NZ)
                if l == 0:
                    stage_ended(pl, end_c[l])
                for k in range(2):
                    for j in range(j0, j1):
                        g.indirect_dma_start(disp[0:ROWS, :], bass.IndirectOffsetOnAxis(slot[l][:, k, j:j + 1], 0),
                                             h_rows[:, j, :], None, bounds_check=ROWS - 1, oob_is_err=False)\
                         .then_inc(s_sc[l], 16)
                if j1 == NT:
                    pl.wait_ge(s_sc[l], 16 * 2 * NT)

            scatter(0)

            def lo_dn(t, p):
                c = pl.value_load(chgi[0:1, bass.ds(t, 1)], min_val=0, max_val=1)
                pl.wait_ge(d_hdn, t + 1)
                static_wait(pl, d_ldn, t)
                carry_wait(7)
                with pl.If(c):
                    n = pl.value_load(wplace[0:1, bass.ds(t, 1)], min_val=0, max_val=2)
                    g.tensor_tensor(place_of(wdn, n + 1), rdn[p][:, :, :], place_of(wdn, n).bitcast(F32), ALU.subtract)
                g.tensor_copy(tick[0:1, 8:9], tick[0:1, 0:1]).then_inc(d_ldn, 1)

            lo_dn(0, 0)

            def stage_d(i, cond):
                if cond:
                    pl.wait_ge(c_dd, i + 1)
                    g.tensor_tensor(cD["e21"][:, :], cD["dd"][:, :], cD["kT"][:, :], ALU.mult).then_inc(c_dv, 1)
                    pl.wait_ge(c_nb, i + 1)
                    g.tensor_tensor(cD["nf"][:, :], cD["nf"][:, :], cD["nb"][:, :], ALU.add).then_inc(c_s1, 1)
                lo_dn(2 * i + 1, 1)
                if cond:
                    pl.wait_ge(c_db, i + 1)
                    g.tensor_tensor(cD["df"][:, :], cD["df"][:, :], cD["db"][:, :], ALU.add).then_inc(c_s2, 1)
                    pl.wait_ge(c_s2, i + 1)
                    g.tensor_tensor(cD["dd"][:, :], cD["df"][:, :], cD["dd"][:, :], ALU.add).then_inc(c_den, 1)
                lo_dn(2 * i + 2, 0)

            with pl.Fori(0, NQ) as i:
                stage_d(i, True)
            with pl.Fori(NQ, NG // 2) as i:
                stage_d(i, False)
            stage_ended(pl, end_d)

            def gather(l):
                for j in range(NT):
                    n = j % 4
                    for k, dst in ((0, y1g), (1, y2g)):
                        if l == 0 and j >= 4:
                            pl.wait_ge(e_p if k == 0 else e_x1, j - 3)
                        if l == 1 and j >= 4:
                            pl.wait_ge(g_o, 2 * (j - 4) + 1 + k)
                        g.indirect_dma_start(dst[n][:, :], None, ybuf[l][:, :],
                                             bass.IndirectOffsetOnAxis(slot[l][:, k, j:j + 1], 0),
                                             bounds_check=ROWS + P - 1, oob_is_err=False)\
                         .then_inc(e_g[k][n], 16)

            gather(0)
            scatter(1)
            scatter(2)
            stage_ended(pl, end_c[1])

            def lo_w(part, wh_sem, wl_sem, c, p):
                pl.wait_ge(wh_sem, c + 1)
                g.tensor_tensor(part(wcl, p), part(wrw, p), part(wch, p).bitcast(F32), ALU.subtract)\
                 .then_inc(wl_sem, 1)

            lo_w(w1c, f_wh1, f_wl1, 0, 0)
            lo_w(w2c, f_wh2, f_wl2, 0, 0)
            lo_w(w1c, f_wh1, f_wl1, 1, 1)
            with pl.Fori(0, NGRP) as G:
                lo_w(w2c, f_wh2, f_wl2, 2 * G + 1, 1)
                lo_w(w1c, f_wh1, f_wl1, 2 * G + 2, 0)
                lo_w(w2c, f_wh2, f_wl2, 2 * G + 2, 0)
                lo_w(w1c, f_wh1, f_wl1, 2 * G + 3, 1)
            stage_ended(pl, end_f)
            gather(1)

        @block.scalar
        def _(act):
            s = nc.scalar
            act.wait_ge(s_vset, 1)
            s.activation(tf[:, :], tsum[:, :], ACT.Sigmoid).then_inc(s_aset, 1)
            act.wait_ge(s_par, 32)
            for l in range(2):
                s.activation(ew[:, l, :], w_col[l], ACT.Exp).then_inc(s_aset, 1)
            act.wait_ge(s_aset, 3)
            s.activation(dcy[:, :, :], ew[:, :, :], ACT.Exp, scale=-1.0).then_inc(s_aset, 1)

            def route_tile(l, j, n):
                p = n % 2
                act.wait_ge(s_ht, NT * l + j + 1)
                s.activation(hT[:, p, :, :], quad(HTB[p]), ACT.Copy).then_inc(s_hte, 1)
                if l == 0:
                    static_wait(act, s_sq, j)
                    s.activation(sqj[:, :], h_rows[:, j, :], ACT.Square, accum_out=ssq[:, bass.ds(j, 1)])\
                     .then_inc(s_sq, 1)

            def exps(b, ct):
                p, q = ct % 2, b * KD + ct
                act.wait_ge(s_kin[p], 16 * (2 * b + ct // 2 + 1))
                static_wait(act, s_ekv, q - 1)
                s.activation(cA["e1"][:, p, :], cA["kT"][:, p, :], ACT.Exp).then_inc(s_e1, 1)
                static_wait(act, s_dd, q - 1)
                s.activation(cA["e20"][:, p, :], cA["kT"][:, p, :], ACT.Exp,
                             bias=u_col[0][:, ct:ct + 1]).then_inc(s_e20, 1)
                static_wait(act, s_euo[p], 16 * (2 * b + ct // 2))
                s.activation(cA["e21"][:, p, :], cA["kT"][:, p, :], ACT.Exp,
                             bias=u_col[1][:, ct:ct + 1]).then_inc(s_e21, 1)

            def first_inverse(q, n):
                act.wait_ge(s_dm, q + 1)
                s.activation(cA["r0"][:, n, :], cA["dd"][:, n, :], ACT.Ln).then_inc(s_ln, 1)
                act.wait_ge(s_ln, q + 1)
                s.activation(cA["r0"][:, n, :], cA["r0"][:, n, :], ACT.Exp, scale=-1.0).then_inc(s_r0, 1)

            def stage_a(b):
                for ct in range(KD):
                    q = b * KD + ct
                    exps(b, ct)
                    if not isinstance(b, int) or q >= 2:
                        first_inverse(q - 2, (ct + 2) % 4)
                    if not isinstance(b, int) or q >= 7:
                        route_tile(0, q - 7, (ct + 1) % 2)
                    if isinstance(b, int) and q == 3:
                        act.wait_ge(s_x, 16 * B)
                        for c in range(4):
                            s.activation(x_rows[:, 4 * c:4 * c + 4, :], x_rows[:, 4 * c:4 * c + 4, :], ACT.Sigmoid)\
                             .then_inc(s_sig, 1)

            stage_a(0)
            stage_a(1)
            with act.Fori(2, B) as b:
                stage_a(b)
            first_inverse(NQ - 2, 2)
            first_inverse(NQ - 1, 3)
            for j in range(NQ - 7, NT):
                route_tile(0, j, j)

            def softmax(n):
                l, j0, j1 = ROUTE[n]
                act.wait_ge(s_lx, n + 1)
                s.activation(ex[:, j0:j1, :], lgs[:, j0:j1, :], ACT.Exp).then_inc(s_ex, 1)
                if j1 == NT:
                    stage_ended(act, end_c[l])

            act.wait_ge(s_ms, 1)
            s.activation(rms[:, :], rstd[:, :], ACT.Sqrt).then_inc(s_rms, 1)
            softmax(0)

            def hi_gu(t, p, n_in):
                c = act.value_load(chgi[0:1, bass.ds(t, 1)], min_val=0, max_val=1)
                act.wait_ge(d_rgu[p], 16 * n_in)
                static_wait(act, d_gu, t - 1)
                static_wait(act, d_hgu, t)
                s.activation(tick[0:1, 1:2], tick[0:1, 0:1], ACT.Copy)
                with act.If(c):
                    n = act.value_load(wplace[0:1, bass.ds(t, 1)], min_val=0, max_val=2)
                    s.activation(place_of(wgu, n), rgu[p][:, :, :], ACT.Copy)
                s.activation(tick[0:1, 2:3], tick[0:1, 0:1], ACT.Copy).then_inc(d_hgu, 1)

            def hi_dn(t, p, n_in):
                c = act.value_load(chgi[0:1, bass.ds(t, 1)], min_val=0, max_val=1)
                act.wait_ge(d_rdn[p], 16 * n_in)
                static_wait(act, d_dn, t - 1)
                static_wait(act, d_hdn, t)
                s.activation(tick[0:1, 3:4], tick[0:1, 0:1], ACT.Copy)
                with act.If(c):
                    n = act.value_load(wplace[0:1, bass.ds(t, 1)], min_val=0, max_val=2)
                    s.activation(place_of(wdn, n), rdn[p][:, :, :], ACT.Copy)
                s.activation(tick[0:1, 4:5], tick[0:1, 0:1], ACT.Copy).then_inc(d_hdn, 1)

            def hi_x(t, p):
                act.wait_ge(d_tx, t + 1)
                s.activation(xth[p][:, :, :], quad(TX), ACT.Copy).then_inc(d_xh, 1)

            hi_gu(0, 0, 1)
            hi_dn(0, 0, 1)
            hi_x(0, 0)
            act.wait_ge(s_sc[0], 16 * 2 * NT)
            hi_gu(1, 1, 1)

            def store_y(t, p):
                act.wait_ge(d_dn, t + 1)
                s.activation(yb[p][:, :], YD[:, :], ACT.Copy).then_inc(d_ye, 1)
                act.wait_ge(d_ye, t + 1)
                act.dma_start(ybuf[0][bass.ds(t * P, P), :], yb[p][:, :]).then_inc(d_yo[p], 16)

            def stage_d(i, first, turn):
                for p in range(2):
                    t = 2 * i + p
                    hi_x(t + 1, 1 - p)
                    act.wait_ge(d_gu, t + 1)
                    s.activation(ga[:, :], GP[:, :], ACT.Gelu).then_inc(d_gelu, 1)
                    hi_gu(t + 2, p, i + 2)
                    if not (first and p == 0):
                        store_y(t - 1, 1 - p)
                    static_wait(act, d_yo[p], 16 * i)
                    act.wait_ge(d_ta, t + 1)
                    s.activation(ath[p][:, :, :], quad(TA), ACT.Copy).then_inc(d_ah, 1)
                    if p == 0 and turn:
                        act.wait_ge(c_tr, i - 1)
                        s.activation(rtb[:, :, :], quad(TRD), ACT.Copy).then_inc(c_rt, 1)
                        act.wait_ge(c_rt, i - 1)
                        act.dma_start(ratio_d[i - 2], rtb[:, :, :]).then_inc(c_out, 16)
                    hi_dn(t + 1, 1 - p, i + 1 + p)
                    if p == 1 and turn:
                        act.wait_ge(c_out, 16 * (i - 1))

            stage_d(0, True, False)
            stage_d(1, False, False)
            with act.Fori(2, NQ + 2) as i:
                stage_d(i, False, True)
            with act.Fori(NQ + 2, NG // 2) as i:
                stage_d(i, False, False)
            store_y(NG - 1, 1)
            for p in range(2):
                act.wait_ge(d_yo[p], 16 * NG // 2)
            stage_ended(act, end_d)

            for j in range(NT):
                act.wait_ge(e_x1, j + 1)
                if j >= 2:
                    act.wait_ge(e_h, j - 1)
                s.activation(sgx[j % 2][:, :], x_rows[:, j, :], ACT.Sigmoid).then_inc(e_sg, 1)
                if j >= 1:
                    route_tile(1, j - 1, j - 1)
                if j == ROUTE_A:
                    softmax(1)
            route_tile(1, NT - 1, NT - 1)
            softmax(2)

            def hi_xg(st, par_next, cols, txb):
                act.wait_ge(f_tx, st + 1)
                s.activation(XTh[:, par_next, :, cols], txb[:, 0:4 * TXR].rearrange("p (k f) -> p k f", k=KD),
                             ACT.Copy).then_inc(f_xh, 1)

            def hi_w(part, wh_sem, c, p, n_in):
                act.wait_ge(f_w[p], 16 * n_in)
                s.activation(part(wch, p), part(wrw, p), ACT.Copy).then_inc(wh_sem, 1)

            def hi_h(f, p):
                act.wait_ge(f_h, f + 1)
                for h, (c, n) in enumerate(PART):
                    if h == 1:
                        static_wait(act, f_hl, 2 * f)
                    s.activation(hth[p][:, c:c + n], HB[h][:, 0:n], ACT.Relu).then_inc(f_hh, 1)

            hi_w(w1c, f_wh1, 0, 0, 1)
            for st in range(NST):
                hi_xg(st, 0, slice(st * TXR, (st + 1) * TXR), TXS[st % 2])
            hi_w(w2c, f_wh2, 0, 0, 1)
            hi_w(w1c, f_wh1, 1, 1, 1)
            hi_h(0, 0)

            def stage_f(e, g, ep, last):
                G = 4 * e + g
                for q in range(4):
                    if q % 2 == 0:
                        hi_xg(NST + 2 * G + q // 2, 1 - ep, bass.ds((2 * g + q // 2) * TXR, TXR), TXF)
                    hi_h(4 * G + q + 1, (q + 1) % 2)
                    if q == 0:
                        hi_w(w2c, f_wh2, 2 * G + 1, 1, G + 1)
                    if q == 1:
                        hi_w(w1c, f_wh1, 2 * G + 2, 0, G + 2)
                    if q == 2:
                        hi_w(w2c, f_wh2, 2 * G + 2, 0, G + 2)
                    if q == 3:
                        hi_w(w1c, f_wh1, 2 * G + 3, 1, G + 2)
                if last:
                    act.wait_ge(f_y, 4 * G + 4)
                    for j in range(5):
                        if j == 0 and ep == 1:
                            act.wait_ge(f_yo, 80 * e)
                        s.activation(yo[j][:, :], bank[j][:, :], ACT.Copy).then_inc(f_ye, 1)
                    for j in range(5):
                        act.wait_ge(f_ye, 5 * e + j + 1)
                        act.dma_start(ybuf[1][bass.ds(e * CAP + j * P, P), :], yo[j][:, :]).then_inc(f_yo, 16)

            with act.Fori(0, E // 2) as e2:
                for ep in range(2):
                    e = 2 * e2 + ep
                    with act.Fori(0, 3) as g:
                        stage_f(e, g, ep, False)
                    stage_f(e, 3, ep, True)
                act.wait_ge(f_yo, 160 * (e2 + 1))
            stage_ended(act, end_f)

        @block.tensor
        def _(pe):
            m = nc.tensor

            def turn_rows(bank_, rows, np_=P, width=P):
                for k in range(KD):
                    last = m.transpose(bank_[:, k * width:(k + 1) * width], rows(k), ident[0:np_, 0:np_])
                return last

            def turn_h(l, j):
                static_wait(pe, s_hte, NT * l + j - 1)
                turn_rows(HTB[j % 2], lambda k: h_rows[:, j, k * P:(k + 1) * P]).then_inc(s_ht, 1)

            def logits(l, j):
                pe.wait_ge(s_hte, NT * l + j + 1)
                w = gate0s if l == 0 else gate[1]
                LG = LGS[0 if l == 0 else 1 if j < NT // 2 else 2]
                for k in range(KD):
                    last = m.matmul(LG[:, j * E:(j + 1) * E], hT[:, j % 2, k, :], w[:, k, :],
                                    start=(k == 0), stop=(k == KD - 1))
                last.then_inc(s_lg, 1)

            pe.wait_ge(s_const, 9)
            pe.wait_ge(s_vset, 15)

            for q in range(NQ + 8):
                if 7 <= q < NT + 7:
                    pe.wait_ge(s_h, (q - 7) // TB * KD + KD)
                    turn_h(0, q - 7)
                if 2 <= q < NQ + 2:
                    pe.wait_ge(s_rat, q - 1)
                    static_wait(pe, s_h, q - 3)
                    turn_rows(TR[q % 2], lambda j: cA["rat"][:, q % 2, j * P:(j + 1) * P]).then_inc(s_tr, 1)
                if q >= 8:
                    logits(0, q - 8)

            def ranks(n):
                l, j0, j1 = ROUTE[n]
                pe.wait_ge(s_mk, n + 1)
                m.matmul(RK[:, j0 * E:j1 * E], tri[:, :], msk[:, j0:j1, :].rearrange("p j e -> p (j e)"),
                         start=True, stop=False, skip_group_check=True)
                for j in range(j1 - 1):
                    c = max(j + 1, j0)
                    last = m.matmul(RK[:, c * E:j1 * E].rearrange("p (j e) -> p j e", e=E), ones[:, :],
                                    msk[:, j:j + 1, :].to_broadcast([P, j1 - c, E]),
                                    start=False, stop=(j == j1 - 2), skip_group_check=True)
                if j1 == NT:
                    for j in range(NT):
                        last = m.matmul(TOT[:, 0:E], ones[:, :], msk[:, j, :], start=(j == 0), stop=(j == NT - 1))
                last.then_inc(s_rk, 1)

            ranks(0)
            stage_ended(pe, end_c[0])

            def turn_x(t, p, n_in):
                pe.wait_ge(d_xr[p], 16 * n_in)
                static_wait(pe, d_xl, t)
                turn_rows(TX, lambda k: xr[p][:, k * P:(k + 1) * P]).then_inc(d_tx, 1)

            def products(p, a_hi, a_lo, w_hi, w_lo, accs, width):
                for k in range(KD):
                    for n, (a, w) in enumerate(((a_hi, w_hi), (a_hi, w_lo), (a_lo, w_hi))):
                        for h, acc in enumerate(accs):
                            yield (acc[:, :], a[p][:, k, :], w[:, k, h * width:(h + 1) * width],
                                   k == 0 and n == 0, k == KD - 1 and n == 2)

            def if_rows(t, terms, n_last, done):
                terms = list(terms)
                with pe.If(t):
                    for o, a, w, start, stop in terms[:-n_last]:
                        m.matmul(o, a, w, start=start, stop=stop, skip_group_check=True)
                for o, a, w, start, stop in terms[-n_last:]:
                    last = m.matmul(o, a, w, start=start, stop=stop, skip_group_check=True)
                last.then_inc(done, 1)

            def row_tile(t):
                return (pe.value_load(vali[0:1, bass.ds(t, 1)], min_val=0, max_val=1),
                        pe.value_load(wplace[0:1, bass.ds(t, 1)], min_val=0, max_val=2))

            def hidden(t, p, some, n):
                pe.wait_ge(d_xl, t + 1)
                pe.wait_ge(d_lgu, t + 1)
                if_rows(some, products(p, xth, xtl, place_of(wgu, n), place_of(wgu, n + 1), (GP, UP), F0), 2, d_gu)

            def turn_act(t):
                pe.wait_ge(d_act, t + 1)
                turn_rows(TA, lambda k: ga[:, k * P:(k + 1) * P]).then_inc(d_ta, 1)

            def down(t, p, some, n):
                pe.wait_ge(d_al, t + 1)
                pe.wait_ge(d_ldn, t + 1)
                static_wait(pe, d_ye, t)
                if_rows(some, products(p, ath, atl, place_of(wdn, n), place_of(wdn, n + 1), (YD,), D), 1, d_dn)

            turn_x(0, 0, 1)

            def stage_d(i, first, turn):
                t = 2 * i
                turn_x(t + 1, 1, i + 1)
                even = row_tile(t)
                hidden(t, 0, *even)
                if not first:
                    down(t - 1, 1, *row_tile(t - 1))
                odd = row_tile(t + 1)
                turn_act(t)
                if turn:
                    pe.wait_ge(c_rat, i - 1)
                    turn_rows(TRD, lambda j: cD["rat"][:, j * P:(j + 1) * P]).then_inc(c_tr, 1)
                turn_x(t + 2, 0, i + 2)
                hidden(t + 1, 1, *odd)
                down(t, 0, *even)
                turn_act(t + 1)

            stage_d(0, True, False)
            stage_d(1, False, False)
            with pe.Fori(2, NQ + 2) as i:
                stage_d(i, False, True)
            with pe.Fori(NQ + 2, NG // 2) as i:
                stage_d(i, False, False)
            down(NG - 1, 1, *row_tile(NG - 1))
            stage_ended(pe, end_d)

            for j in range(NT + 1):
                if j < NT:
                    pe.wait_ge(e_h, j + 1)
                    turn_h(1, j)
                if j >= 1:
                    logits(1, j - 1)
                if j == ROUTE_B - 2:
                    ranks(1)
            ranks(2)
            stage_ended(pe, end_c[1])

            def turn_xg(st, p, n_in, txb, before):
                pe.wait_ge(f_xg[p], 16 * n_in)
                static_wait(pe, f_xl, before)
                turn_rows(txb, lambda k: xg[p][:, k * P:(k + 1) * P], TXR, TXR).then_inc(f_tx, 1)

            def hidden1(f, sub, wp, xp, four, five, not_four):

                def part(h, c, n):
                    for k in range(KD):
                        for i, (w, a) in enumerate(((wch, XTh), (wch, XTl), (wcl, XTh))):
                            last = m.matmul(HB[h][:, 0:n], w1c(w, wp)[:, k, sub * P:(sub + 1) * P],
                                            a[:, xp, k, c:c + n], start=(k == 0 and i == 0),
                                            stop=(k == KD - 1 and i == 2), skip_group_check=True)
                    return last

                with pe.If(five):
                    static_wait(pe, f_hl, 2 * f)
                    part(1, W3, WB)
                static_wait(pe, f_hl, 2 * f - 1)
                with pe.If(four):
                    part(0, 0, W4).then_inc(f_h, 1)
                with pe.If(not_four):
                    part(0, 0, W3).then_inc(f_h, 1)

            def y_part(f, sub, wp, hp, zeroed, four, five, not_four):
                pe.wait_ge(f_hl, 2 * f + 2)
                if zeroed is not None:
                    pe.wait_ge(f_yz, zeroed)

                def rows(j, c):
                    for a, w in ((hth, wch), (hth, wcl), (htl, wch)):
                        last = m.matmul(bank[j][:, :], a[hp][:, c:c + P], w2c(w, wp)[:, sub, :],
                                        start=False, stop=False, skip_group_check=True)
                    return last

                with pe.If(five):
                    rows(4, W4 + P)
                    rows(3, W4)
                with pe.If(four):
                    rows(3, W3)
                for j in range(3):
                    last = rows(j, j * P)
                last.then_inc(f_y, 1)

            def row_counts(e):
                return [pe.value_load(more[0:1, n, bass.ds(e, 1)], min_val=0, max_val=1) for n in range(3)]

            for st in range(NST):
                turn_xg(st, st % 2, st // 2 + 1, TXS[st % 2], st - 1)
            pe.wait_ge(f_xl, NST)
            pe.wait_ge(f_wl1, 1)
            hidden1(0, 0, 0, 0, *row_counts(0))

            def stage_f(e, g, ep, last, now, after):
                G = 4 * e + g
                for q in range(4):
                    f = 4 * G + q
                    if q % 2 == 0:
                        turn_xg(NST + 2 * G + q // 2, q // 2, NST // 2 + G + 1, TXF, NST + 2 * G + q // 2)
                    if q == 1:
                        pe.wait_ge(f_wl1, 2 * G + 2)
                    if q == 3:
                        pe.wait_ge(f_wl1, 2 * G + 3)
                        if last:
                            pe.wait_ge(f_xl, NST * (e + 2))
                    ahead = last and q == 3
                    hidden1(f + 1, (q + 1) % 2, ((q + 1) // 2) % 2, 1 - ep if ahead else ep,
                            *(after if ahead else now))
                    if q == 0:
                        pe.wait_ge(f_wl2, 2 * G + 1)
                    if q == 2:
                        pe.wait_ge(f_wl2, 2 * G + 2)
                    y_part(f, q % 2, q // 2, q % 2, 5 * e + 5 if q == 0 else None, *now)

            with pe.Fori(0, E // 2) as e2:
                for ep in range(2):
                    e = 2 * e2 + ep
                    now, after = row_counts(e), row_counts(e + 1)
                    with pe.Fori(0, 3) as g:
                        stage_f(e, g, ep, False, now, after)
                    stage_f(e, 3, ep, True, now, after)
            stage_ended(pe, end_f)

        @block.vector
        def _(dve):
            v = nc.vector

            dve.wait_ge(s_par, 32)
            v.tensor_reduce(tsum[:, :], rowp[:, 0:B * P].rearrange("p (b t) -> p b t", b=B), AX.X, ALU.add)\
             .then_inc(s_vset, 1)
            dve.wait_ge(s_aset, 1)
            v.tensor_scalar(half[:, :], tf[:, :], 0.5, 0.5, ALU.mult, ALU.add).then_inc(s_vset, 1)
            v.tensor_scalar(gsc[:, :], tf[:, :], -0.2, -0.8, ALU.mult, ALU.add).then_inc(s_vset, 1)
            dve.wait_ge(s_aset, 4)
            dve.wait_ge(s_vset, 3)
            for l in range(2):
                for b in range(B):
                    v.tensor_scalar(dec[:, l, b, :], dcy[:, l, :], half[:, b:b + 1], None, ALU.mult)\
                     .then_inc(s_vset, 1)
            for k in range(KD):
                v.tensor_scalar(gate0s[:, k, :], gate[0][:, k, :], rs_col[:, k:k + 1], float(D) ** -0.5,
                                ALU.mult, ALU.mult).then_inc(s_vset, 1)
            dve.wait_ge(s_vset, 15)

            def scan(dst, src, d, reverse):
                st = slice(None, None, -1) if reverse else slice(None)
                return v.tensor_tensor_scan(dst[:, st], d.to_broadcast([P, T]), src[:, st], 0.0,
                                            ALU.mult, ALU.add)

            def scans(b, ct):
                p, q = ct % 2, b * KD + ct
                d = dec[:, 0, :, :].rearrange("p b c -> p (b c)")[:, bass.ds(q, 1)]
                dve.wait_ge(s_e1, q + 1)
                static_wait(dve, s_eko[p], 16 * (2 * b + ct // 2))
                v.tensor_scalar(cA["ek"][:, p, :], cA["e1"][:, p, :], E30, None, ALU.min).then_inc(s_ek, 1)
                v.scalar_tensor_tensor(cA["ekv"][:, p, :], cA["e1"][:, p, :], E30, cA["kT"][:, p, :],
                                       ALU.min, ALU.mult).then_inc(s_ekv, 1)
                dve.wait_ge(s_ek, q + 1)
                dve.wait_ge(s_e20, q + 1)
                v.scalar_tensor_tensor(cA["dd"][:, ct, :], cA["e20"][:, p, :], E30, cA["ek"][:, p, :],
                                       ALU.min, ALU.subtract).then_inc(s_dd, 1)
                dve.wait_ge(s_ekv, q + 1)
                scan(cA["nf"][:, ct, :], cA["ekv"][:, p, :], d, False).then_inc(s_nf, 1)
                scan(cA["nb"][:, p, :], cA["ekv"][:, p, :], d, True).then_inc(s_nb, 1)
                scan(cA["df"][:, ct, :], cA["ek"][:, p, :], d, False).then_inc(s_df, 1)
                scan(cA["db"][:, p, :], cA["ek"][:, p, :], d, True).then_inc(s_db, 1)

            def num_den(q, ct):
                dve.wait_ge(s_s1, q + 1)
                v.tensor_tensor(cA["nf"][:, ct, :], cA["nf"][:, ct, :], cA["dv"][:, ct % 2, :], ALU.add)\
                 .then_inc(s_num, 1)
                dve.wait_ge(s_den, q + 1)
                v.tensor_scalar(cA["dd"][:, ct, :], cA["dd"][:, ct, :], 1e-8, None, ALU.max).then_inc(s_dm, 1)

            def ratio(q, ct):
                dve.wait_ge(s_r0, q + 1)
                dve.wait_ge(s_num, q + 1)
                v.tensor_tensor(cA["nf"][:, ct, :], cA["nf"][:, ct, :], cA["r0"][:, ct, :], ALU.mult).then_inc(s_a, 1)
                dve.wait_ge(s_a, q + 1)
                dve.wait_ge(s_t, q + 1)
                v.scalar_tensor_tensor(cA["rat"][:, ct % 2, :], cA["df"][:, ct, :], 2.0, cA["nf"][:, ct, :],
                                       ALU.subtract, ALU.mult).then_inc(s_rat, 1)

            def h_part(b, ct):
                q = b * KD + ct
                dve.wait_ge(s_tr, q + 1)
                rows = bass.ds(b * TB, TB)
                v.scalar_tensor_tensor(h_rows[:, rows, ct * P:(ct + 1) * P], x_rows[:, rows, ct * P:(ct + 1) * P],
                                       gsc[:, bass.ds(b, 1)], quad(TR[ct % 2]), ALU.mult, ALU.mult)\
                 .then_inc(s_h, 1)

            def stage_a(b, first):
                for ct in range(KD):
                    q = b * KD + ct
                    scans(b, ct)
                    if not (first and ct < 1):
                        num_den(q - 1, (ct + 3) % 4)
                    if not (first and ct < 2):
                        ratio(q - 2, (ct + 2) % 4)
                    if ct >= 3:
                        if first:
                            dve.wait_ge(s_sig, 4)
                        h_part(b, ct - 3)
                    elif not first:
                        h_part(b - 1, ct + 1)

            stage_a(0, True)
            with dve.Fori(1, B) as b:
                stage_a(b, False)
            num_den(NQ - 1, 3)
            ratio(NQ - 2, 2)
            h_part(B - 1, 1)
            ratio(NQ - 1, 3)
            h_part(B - 1, 2)
            h_part(B - 1, 3)

            steps = [0]

            def link(ins):
                steps[0] += 1
                ins.then_inc(s_vr, 1)
                dve.wait_ge(s_vr, steps[0])

            def over_e(a):
                return a.unsqueeze(2).to_broadcast([P, a.shape[1], E])

            def choose(n):
                l, j0, j1 = ROUTE[n]
                js, nj = slice(j0, j1), j1 - j0
                dve.wait_ge(s_lg, NT * l + j1)
                lg = LGS[n][:, j0 * E:j1 * E].rearrange("p (j e) -> p j e", e=E)
                if l == 0:
                    dve.wait_ge(s_sq, NT)
                    v.tensor_scalar(rstd[:, :], ssq[:, :], 1.0 / D, 1e-6, ALU.mult, ALU.add).then_inc(s_ms, 1)
                    dve.wait_ge(s_rms, 1)
                    link(v.reciprocal(rstd[:, :], rms[:, :]))
                    link(v.tensor_tensor(lgs[:, :, :], lg, over_e(rstd[:, :]), ALU.mult))
                else:
                    link(v.tensor_copy(lgs[:, js, :], lg))
                link(v.tensor_reduce(mx[:, js], lgs[:, js, :], AX.X, ALU.max))
                v.tensor_tensor(lgs[:, js, :], lgs[:, js, :], over_e(mx[:, js]), ALU.subtract).then_inc(s_lx, 1)
                dve.wait_ge(s_ex, n + 1)
                link(v.tensor_reduce(sm[:, js], ex[:, js, :], AX.X, ALU.add))
                link(v.reciprocal(rsm[:, js], sm[:, js]))
                link(v.tensor_tensor(prob[:, js, :], ex[:, js, :], over_e(rsm[:, js]), ALU.mult))
                for j in range(j0, j1):
                    last = v.max(top[:, j, :], prob[:, j, :])
                link(last)
                for j in range(j0, j1):
                    last = v.max_index(tix[:, j, :], top[:, j, :], prob[:, j, :])
                link(last)
                link(v.tensor_copy(tixf[:, js, :], tix[:, js, 0:2]))
                for k in range(2):
                    last = v.tensor_tensor(oh[:, k, js, :], iota_e[:, :].unsqueeze(1).to_broadcast([P, nj, E]),
                                           over_e(tixf[:, js, k]), ALU.is_equal)
                link(last)
                v.tensor_tensor(msk[:, js, :], oh[:, 0, js, :], oh[:, 1, js, :], ALU.add).then_inc(s_mk, 1)

            def place(n):
                l, j0, j1 = ROUTE[n]
                js = slice(j0, j1)
                dve.wait_ge(s_rk, n + 1)
                rank = RK[:, j0 * E:j1 * E].rearrange("p (j e) -> p j e", e=E)
                if l == 0:
                    link(v.tensor_copy(tot[:, :], TOT[:, 0:E]))
                    link(v.tensor_tensor(cmp_m[:, :, :], tot[:, :].unsqueeze(2).to_broadcast([P, E, NT]),
                                         iota_m[:, :].unsqueeze(1).to_broadcast([P, E, NT]), ALU.is_gt))
                    link(v.tensor_reduce(ntile[:, :], cmp_m[:, :, :], AX.X, ALU.add))
                    link(v.tensor_tensor_scan(ends[:, :], one8[:, :], ntile[:, :], 0.0, ALU.mult, ALU.add))
                    link(v.tensor_tensor(base[:, :], ends[:, :], ntile[:, :], ALU.subtract))
                    link(v.tensor_scalar(base[:, :], base[:, :], float(P), None, ALU.mult))
                    link(v.tensor_tensor(pos[:, :, :], rank, base[:, :].unsqueeze(1).to_broadcast([P, NT, E]), ALU.add))
                    link(v.tensor_tensor(cmp_t[:, :, :], ends[:, :].unsqueeze(1).to_broadcast([P, NTAB, E]),
                                         iota_t[:, :].unsqueeze(2).to_broadcast([P, NTAB, E]), ALU.is_le))
                    link(v.tensor_reduce(eidf[:, :], cmp_t[:, :, :], AX.X, ALU.add))
                    sign = cmp_t[:, :, 0:3]
                    link(v.tensor_scalar(eidf[:, :], eidf[:, :], float(E - 1), None, ALU.min))
                    v.tensor_copy(eidi[:, :], eidf[:, :])
                    link(v.memset(chgi[:, :], 1))
                    v.tensor_tensor(chgi[:, 1:NG], eidf[:, 1:NG], eidf[:, 0:NG - 1], ALU.not_equal)
                    link(v.memset(sign[:, :, :], 0.0))
                    link(v.tensor_tensor(sign[:, 1:NG, 0], eidf[:, 1:NG], eidf[:, 0:NG - 1], ALU.not_equal))
                    link(v.tensor_scalar(sign[:, :, 0], sign[:, :, 0], -2.0, 1.0, ALU.mult, ALU.add))
                    link(v.tensor_tensor_scan(sign[:, :, 2], sign[:, :, 0], sign[:, :, 1], 1.0, ALU.mult, ALU.add))
                    v.tensor_scalar(wplace, sign[:, :, 2], 1.0, None, ALU.add)
                    v.tensor_tensor(vali[:, :], iota_t[:, :], ends[:, E - 1:E].to_broadcast([P, NTAB]), ALU.is_lt)
                    link(v.memset(chgi[:, NG:NTAB], 0))
                else:
                    link(v.tensor_copy(pos[:, js, :], rank))
                if l == 1 and j1 == NT:
                    link(v.memset(moref[:, :, :], 0.0))
                    for n in range(2):
                        last = v.tensor_scalar(moref[:, n, 0:E], TOT[:, 0:E], float(LIM[n]), None, ALU.is_gt)
                    link(last)
                    link(v.tensor_tensor(moref[:, 0, :], moref[:, 0, :], moref[:, 1, :], ALU.subtract))
                    link(v.tensor_scalar(moref[:, 2, :], moref[:, 0, :], -1.0, 1.0, ALU.mult, ALU.add))
                    link(v.tensor_copy(more[:, :, :], moref[:, :, :]))
                for k in range(2):
                    last = v.tensor_tensor(tmp8[:, k, js, :], oh[:, k, js, :], pos[:, js, :], ALU.mult)
                link(last)
                link(v.tensor_reduce(slotf[:, :, js], tmp8[:, :, js, :], AX.X, ALU.add))
                if l == 0:
                    link(v.tensor_tensor(wsum[:, :], top[:, :, 0], top[:, :, 1], ALU.add))
                    link(v.tensor_scalar(wsum[:, :], wsum[:, :], 1e-12, None, ALU.max))
                    link(v.reciprocal(wsum[:, :], wsum[:, :]))
                    pes = rowp[:, B * P:B * P + E].unsqueeze(1).to_broadcast([P, NT, E])
                    for k in range(2):
                        last = v.tensor_tensor(tmp8[:, k, :, :], oh[:, k, :, :], pes, ALU.mult)
                    link(last)
                    link(v.tensor_reduce(pesk[:, :, :], tmp8[:, :, :, :], AX.X, ALU.add))
                    for k in range(2):
                        last = v.tensor_tensor(wtok[:, k, :], top[:, :, k], wsum[:, :], ALU.mult)
                    link(last)
                    link(v.tensor_tensor(wtok[:, :, :], wtok[:, :, :], pesk[:, :, :], ALU.mult))
                else:
                    link(v.tensor_scalar(kept[:, :, js], slotf[:, :, js], float(CAP), None, ALU.is_lt))
                    for k in range(2):
                        last = v.scalar_tensor_tensor(slotf[:, k, js], tixf[:, js, k], float(CAP), slotf[:, k, js],
                                                      ALU.mult, ALU.add)
                    link(last)
                    link(v.scalar_tensor_tensor(slotf[:, :, js], slotf[:, :, js], float(ROWS), kept[:, :, js],
                                                ALU.subtract, ALU.mult))
                    link(v.tensor_scalar(slotf[:, :, js], slotf[:, :, js], float(ROWS), None, ALU.add))
                    dve.wait_ge(e_x1, j1)
                    for k in range(2):
                        last = v.tensor_tensor(wtok[:, k, js], top[:, js, k], kept[:, k, js], ALU.mult)
                    link(last)
                v.tensor_copy(slot[l][:, :, js], slotf[:, :, js]).then_inc(s_slot, 1)
                if j1 == NT:
                    stage_ended(dve, end_c[l])

            choose(0)
            place(0)

            def lo_gu(t, p, half):
                c = dve.value_load(chgi[0:1, bass.ds(t, 1)], min_val=0, max_val=1)
                ks = slice(half * KD // 2, (half + 1) * KD // 2)
                if half == 0:
                    dve.wait_ge(d_hgu, t + 1)
                static_wait(dve, d_lgu, t)
                v.tensor_copy(tick[0:1, 5 + half:6 + half], tick[0:1, 0:1])
                with dve.If(c):
                    n = dve.value_load(wplace[0:1, bass.ds(t, 1)], min_val=0, max_val=2)
                    v.tensor_tensor(place_of(wgu, n + 1)[:, ks, :], rgu[p][:, ks, :],
                                    place_of(wgu, n)[:, ks, :].bitcast(F32), ALU.subtract)
                if half == 1:
                    v.tensor_copy(tick[0:1, 9:10], tick[0:1, 0:1]).then_inc(d_lgu, 1)

            def lo_x(t, p):
                dve.wait_ge(d_xh, t + 1)
                v.tensor_tensor(xtl[p][:, :, :], quad(TX), xth[p][:, :, :].bitcast(F32), ALU.subtract)\
                 .then_inc(d_xl, 1)

            def terms(q):
                dve.wait_ge(c_in, 48 * (q + 1))
                v.tensor_tensor(cD["df"][:, :], cD["ek"][:, :], cD["kT"][:, :], ALU.mult).then_inc(c_ekv, 1)
                static_wait(dve, c_dm, q)
                v.scalar_tensor_tensor(cD["dd"][:, :], cD["e21"][:, :], E30, cD["ek"][:, :],
                                       ALU.min, ALU.subtract).then_inc(c_dd, 1)

            def scans_num(q):
                d = dec[:, 1, :, :].rearrange("p b c -> p (b c)")[:, bass.ds(q, 1)]
                static_wait(dve, c_num, q)
                dve.wait_ge(c_ekv, q + 1)
                scan(cD["nf"], cD["df"], d, False).then_inc(c_nf, 1)
                scan(cD["nb"], cD["df"], d, True).then_inc(c_nb, 1)

            def scans_den(q):
                d = dec[:, 1, :, :].rearrange("p b c -> p (b c)")[:, bass.ds(q, 1)]
                dve.wait_ge(c_nb, q + 1)
                scan(cD["df"], cD["ek"], d, False).then_inc(c_df, 1)
                scan(cD["db"], cD["ek"], d, True).then_inc(c_db, 1)

            def num(q):
                dve.wait_ge(c_s1, q + 1)
                static_wait(dve, c_rat, q)
                v.tensor_tensor(cD["num"][:, :], cD["nf"][:, :], cD["e21"][:, :], ALU.add).then_inc(c_num, 1)

            def bound(q):
                dve.wait_ge(c_den, q + 1)
                v.tensor_scalar(cD["inv"][:, :], cD["dd"][:, :], 1e-8, None, ALU.max).then_inc(c_dm, 1)

            def inverse(q):
                dve.wait_ge(c_dm, q + 1)
                v.reciprocal(cD["inv"][:, :], cD["inv"][:, :]).then_inc(c_inv, 1)

            def ratio1(q):
                dve.wait_ge(c_inv, q + 1)
                static_wait(dve, c_tr, q)
                v.scalar_tensor_tensor(cD["rat"][:, :], cD["num"][:, :], -1.0, cD["inv"][:, :],
                                       ALU.mult, ALU.mult).then_inc(c_rat, 1)

            lo_gu(0, 0, 0)
            lo_gu(0, 0, 1)
            lo_x(0, 0)
            lo_gu(1, 1, 0)

            def stage_d(i, cond, fin):
                for p in range(2):
                    t = 2 * i + p
                    lo_x(t + 1, 1 - p)
                    dve.wait_ge(d_gelu, t + 1)
                    v.tensor_tensor(ga[:, :], ga[:, :], UP[:, :], ALU.mult).then_inc(d_act, 1)
                    lo_gu(t + 1, 1 - p, 1)
                    if p == 0 and fin:
                        bound(i - 1)
                        inverse(i - 1)
                    if p == 1 and cond:
                        scans_num(i)
                        scans_den(i)
                    if p == 1 and fin:
                        ratio1(i - 1)
                    dve.wait_ge(d_ah, t + 1)
                    v.tensor_tensor(atl[p][:, :, :], quad(TA), ath[p][:, :, :].bitcast(F32), ALU.subtract)\
                     .then_inc(d_al, 1)
                    if p == 1 and cond:
                        num(i)
                    lo_gu(t + 2, p, 0)
                    if p == 0 and cond:
                        terms(i)

            stage_d(0, True, False)
            with dve.Fori(1, NQ) as i:
                stage_d(i, True, True)
            stage_d(NQ, False, True)
            with dve.Fori(NQ + 1, NG // 2) as i:
                stage_d(i, False, False)
            stage_ended(dve, end_d)

            def h1(j):
                dve.wait_ge(e_sg, j + 1)
                dve.wait_ge(e_r[j % 4], 16 * (j // 4 + 1))
                v.scalar_tensor_tensor(h_rows[:, j, :], sgx[j % 2][:, :], gsc[:, j // TB:j // TB + 1],
                                       rin[j % 4][:, :], ALU.mult, ALU.mult).then_inc(e_h, 1)

            for j in range(NT):
                n = j % 4
                dve.wait_ge(e_g[0][n], 16 * (j // 4 + 1))
                dve.wait_ge(e_x[n], 16 * (j // 4 + 1))
                v.scalar_tensor_tensor(xpt[j % 2][:, :], y1g[n][:, :], wtok[:, 0, j:j + 1], xin[n][:, :],
                                       ALU.mult, ALU.add).then_inc(e_p, 1)
                dve.wait_ge(e_p, j + 1)
                dve.wait_ge(e_g[1][n], 16 * (j // 4 + 1))
                v.scalar_tensor_tensor(x_rows[:, j, :], y2g[n][:, :], wtok[:, 1, j:j + 1], xpt[j % 2][:, :],
                                       ALU.mult, ALU.add).then_inc(e_x1, 1)
                if j >= 1:
                    h1(j - 1)
                if j == ROUTE_A:
                    choose(1)
                if j == ROUTE_B:
                    place(1)
            h1(NT - 1)
            choose(2)
            place(2)

            def lo_xg(st, par_next, cols, txb):
                dve.wait_ge(f_xh, st + 1)
                v.tensor_tensor(XTl[:, par_next, :, cols], txb[:, 0:4 * TXR].rearrange("p (k f) -> p k f", k=KD),
                                XTh[:, par_next, :, cols].bitcast(F32), ALU.subtract).then_inc(f_xl, 1)

            def lo_h(f, p):
                for h, (c, n) in enumerate(PART):
                    dve.wait_ge(f_hh, 2 * f + h + 1)
                    v.scalar_tensor_tensor(htl[p][:, c:c + n], HB[h][:, 0:n], 0.0, hth[p][:, c:c + n].bitcast(F32),
                                           ALU.max, ALU.subtract).then_inc(f_hl, 1)

            for j in range(5):
                v.memset(bank[j][:, :], 0.0).then_inc(f_yz, 1)
            for st in range(NST):
                lo_xg(st, 0, slice(st * TXR, (st + 1) * TXR), TXS[st % 2])
            lo_h(0, 0)

            def stage_f(e, g, ep, last):
                G = 4 * e + g
                for q in range(4):
                    if q % 2 == 0:
                        lo_xg(NST + 2 * G + q // 2, 1 - ep, bass.ds((2 * g + q // 2) * TXR, TXR), TXF)
                    lo_h(4 * G + q + 1, (q + 1) % 2)
                if last:
                    for j in range(5):
                        dve.wait_ge(f_ye, 5 * e + j + 1)
                        v.memset(bank[j][:, :], 0.0).then_inc(f_yz, 1)

            with dve.Fori(0, E // 2) as e2:
                for ep in range(2):
                    e = 2 * e2 + ep
                    with dve.Fori(0, 3) as g:
                        stage_f(e, g, ep, False)
                    stage_f(e, 3, ep, True)
            stage_ended(dve, end_f)

            for j in range(NT):
                n = j % 4
                dve.wait_ge(e_g[0][n], 16 * (NT // 4 + j // 4 + 1))
                if j >= 4:
                    dve.wait_ge(g_out[n], 16 * (j // 4))
                v.scalar_tensor_tensor(osb[n][:, :], y1g[n][:, :], wtok[:, 0, j:j + 1], x_rows[:, j, :],
                                       ALU.mult, ALU.add).then_inc(g_o, 1)
                dve.wait_ge(g_o, 2 * j + 1)
                dve.wait_ge(e_g[1][n], 16 * (NT // 4 + j // 4 + 1))
                v.scalar_tensor_tensor(osb[n][:, :], y2g[n][:, :], wtok[:, 1, j:j + 1], osb[n][:, :],
                                       ALU.mult, ALU.add).then_inc(g_o, 1)


def kernel(x, fside_BxSxS_0, cond_512, L0_cond_w, L0_cond_u, L0_ffn_router_scale, L0_ffn_gate_w,
           L0_ffn_gate_up, L0_ffn_down, L0_ffn_per_expert_scale, L1_cond_w, L1_cond_u, L1_ffn_Wg,
           L1_ffn_w1, L1_ffn_w2):
    import concourse.bacc as bacc
    from concourse.bass_utils import run_bass_kernel_spmd

    def cols(a):
        return np.asarray(a).reshape(KD, P).T

    def gates(a):
        return np.asarray(a).reshape(KD, P, E).transpose(1, 0, 2).reshape(P, KD * E)

    def blocks(a, k):
        a = np.asarray(a)
        return a.reshape(a.shape[0], k, P, a.shape[2]).transpose(0, 2, 1, 3).reshape(a.shape[0], P, -1)

    w1 = np.asarray(L1_ffn_w1).reshape(E, KD, P, NC1, HC).transpose(0, 3, 2, 1, 4).reshape(E * NC1, P, KD * HC)
    w2 = blocks(np.asarray(L1_ffn_w2).reshape(E * NC1, HC, D), HC // P)
    arrays = {
        "x": np.asarray(x).reshape(NT, P, D),
        "fs_t": np.asarray(fside_BxSxS_0).transpose(0, 2, 1).reshape(NQ, P, T),
        "params": np.concatenate([cols(L0_cond_w), cols(L0_cond_u), cols(L1_cond_w), cols(L1_cond_u),
                                  cols(L0_ffn_router_scale), gates(L0_ffn_gate_w), gates(L1_ffn_Wg)], axis=1),
        "rowpar": np.concatenate([np.asarray(cond_512).reshape(-1), np.asarray(L0_ffn_per_expert_scale)]),
        "gu": blocks(L0_ffn_gate_up, KD),
        "dn": blocks(L0_ffn_down, KD),
        "wc": np.concatenate([w1, w2], axis=2),
    }
    arrays = {n: np.ascontiguousarray(a) for n, a in arrays.items()}
    nc = bacc.Bacc("TRN2", target_bir_lowering=False, num_devices=1)
    args = [nc.dram_tensor(n, a.shape, mybir.dt.from_np(a.dtype), kind="ExternalInput").ap()
            for n, a in arrays.items()]
    out = nc.dram_tensor("out", (NT, P, D), F32, kind="ExternalOutput").ap()
    adaln_moe_kernel(nc, *args, out)
    r = run_bass_kernel_spmd(nc, [arrays], core_ids=[0])
    return r.results[0]["out"].reshape(B, T, D)
```
